# Optimizing a Trainium2 kernel written in Bass

```python
import numpy as np
import jax
import jax.numpy as jnp

def _softmax(x, axis=-1):
    return jax.nn.softmax(x, axis=axis)

def _gelu(x):
    return jax.nn.gelu(x, approximate=True)

def _silu(x):
    return jax.nn.silu(x)

def _sigmoid(x):
    return jax.nn.sigmoid(x)

def _layernorm(x, axis=-1, eps=1e-05):
    m = jnp.mean(x, axis=axis, keepdims=True)
    v = jnp.var(x, axis=axis, keepdims=True)
    return (x - m) / jnp.sqrt(v + eps)

def _scatter_add(tgt, idx, src, axis=0):
    return tgt.at[idx].add(src)

def _segment_sum(src, seg, n):
    return jax.ops.segment_sum(src, seg, n)
kernel_name = 'mk_seq_postln_d4_jaxref_r8_7a4626'

def setup_inputs(seed: int=0):
    np.random.seed(seed)
    _w = jnp.asarray

    def _L0_attn_setup():
        import jax, jax.numpy as jnp
        import numpy as np
        import math
        B, T, D_IN, D_OUT = (2, 256, 512, 512)
        N_HEADS, N_KV = (32, 8)
        HEAD_DIM = D_OUT // N_HEADS
        GROUP_SIZE = N_HEADS // N_KV
        ROPE_BASE = 500000.0
        CTX = 256

        def _rope_tables(head_dim, base, seq_len):
            inv_freq = 1.0 / base ** (jnp.arange(0, head_dim, 2, dtype=jnp.float32) / head_dim)
            t = jnp.arange(seq_len, dtype=jnp.float32)
            freqs = jnp.einsum('i,j->ij', t, inv_freq)
            return (jnp.cos(freqs), jnp.sin(freqs))

        def _apply_rope(x, cos, sin):
            x1, x2 = jnp.split(x, 2, axis=-1)
            c = cos[None, None]
            s = sin[None, None]
            return jnp.concatenate([x1 * c - x2 * s, x1 * s + x2 * c], axis=-1)
        key = jax.random.key(seed)
        ks = jax.random.split(key, 5)
        scale = 0.02
        return {'x': jax.random.normal(ks[0], (B, T, D_IN), dtype=jnp.float32), 'Wq': jax.random.normal(ks[1], (D_IN, D_OUT), dtype=jnp.float32) * scale, 'Wk': jax.random.normal(ks[2], (D_IN, N_KV * HEAD_DIM), dtype=jnp.float32) * scale, 'Wv': jax.random.normal(ks[3], (D_IN, N_KV * HEAD_DIM), dtype=jnp.float32) * scale, 'Wo': jax.random.normal(ks[4], (D_OUT, D_OUT), dtype=jnp.float32) * scale}
    _L0_attn_in = _L0_attn_setup()

    def _L0_ffn_setup():
        import jax, jax.numpy as jnp
        import numpy as np
        D_MODEL = 512
        D_FF = 1376

        def _dequant_matmul(x, w_int, s):
            w = w_int.astype(jnp.float32) * s
            return x @ w.T
        key = jax.random.key(seed)
        ks = jax.random.split(key, 7)
        x = jax.random.normal(ks[0], (4, 256, D_MODEL), dtype=jnp.float32)
        gate_w = jax.random.randint(ks[1], (D_FF, D_MODEL), -128, 128, dtype=jnp.int32)
        up_w = jax.random.randint(ks[2], (D_FF, D_MODEL), -128, 128, dtype=jnp.int32)
        down_w = jax.random.randint(ks[3], (D_MODEL, D_FF), -128, 128, dtype=jnp.int32)
        gate_s = jax.random.uniform(ks[4], (D_FF, 1), dtype=jnp.float32) * 0.01
        up_s = jax.random.uniform(ks[5], (D_FF, 1), dtype=jnp.float32) * 0.01
        down_s = jax.random.uniform(ks[6], (D_MODEL, 1), dtype=jnp.float32) * 0.01
        return {'x': x, 'gate_w': gate_w, 'gate_s': gate_s, 'up_w': up_w, 'up_s': up_s, 'down_w': down_w, 'down_s': down_s}
    _L0_ffn_in = _L0_ffn_setup()

    def _L1_attn_setup():
        import jax, jax.numpy as jnp
        import numpy as np
        B, S, EMB = (2, 256, 512)
        NHEADS, KVHEADS, HEAD_D = (32, 8, 128)
        SPLITS = (NHEADS * HEAD_D, KVHEADS * HEAD_D, KVHEADS * HEAD_D)
        key = jax.random.key(seed)
        k1, k2, k3 = jax.random.split(key, 3)
        q = jax.random.normal(k1, (B, S, EMB), dtype=jnp.float32)
        w_qkv = jax.random.normal(k2, (sum(SPLITS), EMB), dtype=jnp.float32) * 0.02
        w_dense = jax.random.normal(k3, (EMB, NHEADS * HEAD_D), dtype=jnp.float32) * 0.02
        return {'q': q, 'w_qkv': w_qkv, 'w_dense': w_dense}
    _L1_attn_in = _L1_attn_setup()

    def _L1_ffn_setup():
        import jax, jax.numpy as jnp
        import numpy as np
        N_STREAMS = 4
        DIM = 128
        SINKHORN_ITERS = 50
        SINKHORN_TAU = 0.1
        RMS_EPS = 1.1920929e-07

        def sinkhorn_log(logits, num_iters=SINKHORN_ITERS, tau=SINKHORN_TAU):
            Z = logits / tau
            u0 = jnp.zeros(Z.shape[:-1], Z.dtype)
            v0 = jnp.zeros_like(u0)

            def step(carry, _):
                u, v = carry
                u = -jax.nn.logsumexp(Z + v[..., None, :], axis=-1)
                v = -jax.nn.logsumexp(Z + u[..., :, None], axis=-2)
                return ((u, v), None)
            (u, v), _ = jax.lax.scan(step, (u0, v0), None, length=num_iters)
            return jnp.exp(Z + u[..., :, None] + v[..., None, :])
        key = jax.random.key(seed)
        ks = jax.random.split(key, 6)
        B, T = (4, 256)
        n, C = (N_STREAMS, DIM)
        wd = n * C
        x = jax.random.normal(ks[0], (B, T, wd), dtype=jnp.float32)
        W_res = 0.01 * jax.random.normal(ks[1], (n * n, wd), dtype=jnp.float32)
        W_pre = 0.01 * jax.random.normal(ks[2], (n, wd), dtype=jnp.float32)
        W_post = 0.01 * jax.random.normal(ks[3], (n, wd), dtype=jnp.float32)
        H_res_base = jnp.full((n, n), -0.5, dtype=jnp.float32)
        H_res_base = H_res_base.at[jnp.arange(n), jnp.arange(n)].set(0.0)
        H_pre_base = jnp.zeros((n,), dtype=jnp.float32).at[0].set(1.0)
        H_post_base = jnp.zeros((n,), dtype=jnp.float32)
        gate = jnp.array([5.0], dtype=jnp.float32)
        W_branch = 1.0 / np.sqrt(C) * jax.random.normal(ks[4], (C, C), dtype=jnp.float32)
        return {'x': x, 'W_res': W_res, 'W_pre': W_pre, 'W_post': W_post, 'H_res_base': H_res_base, 'H_pre_base': H_pre_base, 'H_post_base': H_post_base, 'gate': gate, 'W_branch': W_branch}
    _L1_ffn_in = _L1_ffn_setup()

    def _L2_attn_setup():
        import jax, jax.numpy as jnp
        import numpy as np
        import math
        B, S, DM = (1, 256, 512)
        H, HKV, HD = (32, 8, 128)
        EPS = 1e-06
        NEG_INF = -1e+30

        def _alibi_slopes(n_heads: int) -> np.ndarray:
            start = 2 ** (-2 ** (-(math.log2(n_heads) - 3)))
            return np.array([start * start ** i for i in range(n_heads)], dtype=np.float32)

        def _rmsnorm(t, w):
            tf = t.astype(jnp.float32)
            inv = jax.lax.rsqrt(jnp.mean(tf * tf, axis=-1, keepdims=True) + EPS)
            return (tf * inv * w).astype(t.dtype)
        key = jax.random.key(seed)
        ks = jax.random.split(key, 5)
        std = 0.02
        return {'x': jax.random.normal(ks[0], (B, S, DM), dtype=jnp.float32), 'Wq': jax.random.normal(ks[1], (H * HD, DM), dtype=jnp.float32) * std, 'Wk': jax.random.normal(ks[2], (HKV * HD, DM), dtype=jnp.float32) * std, 'Wv': jax.random.normal(ks[3], (HKV * HD, DM), dtype=jnp.float32) * std, 'Wo': jax.random.normal(ks[4], (H * HD, DM), dtype=jnp.float32).T * (std / math.sqrt(2 * 32)), 'q_norm_w': jnp.ones((HD,), dtype=jnp.float32), 'k_norm_w': jnp.ones((HD,), dtype=jnp.float32)}
    _L2_attn_in = _L2_attn_setup()

    def _L2_ffn_setup():
        import jax, jax.numpy as jnp
        import numpy as np
        HID, BOT, RDIM, NSLOT, K, VB = (512, 64, 48, 128, 8, 32)
        TAU_LOW, TAU_HIGH, EARLY_EXIT = (0.5, 2.0, 0.05)

        def _uncertainty(h, Wu1, bu1, Wu2, bu2):
            var = jnp.var(h, axis=-1)
            log_var = jnp.log1p(var)
            norm_var = log_var / (jnp.mean(log_var) + 1e-06)
            learned = (jax.nn.gelu(h @ Wu1.T + bu1) @ Wu2.T + bu2)[..., 0]
            return jnp.clip(norm_var * 0.5 + jax.nn.sigmoid(learned) * 2.5, 0.0, 5.0)
        key = jax.random.key(seed)
        ks = jax.random.split(key, 12)
        B, S = (2, 256)
        return {'hidden_states': jax.random.normal(ks[0], (B, S, HID), dtype=jnp.float32), 'Wq': jax.random.normal(ks[1], (BOT, HID), dtype=jnp.float32) / np.sqrt(HID), 'Wr': jax.random.normal(ks[2], (RDIM, BOT), dtype=jnp.float32) / np.sqrt(BOT), 'aux_keys': jax.random.normal(ks[3], (NSLOT, BOT), dtype=jnp.float32) * 0.01, 'aux_values': jax.random.normal(ks[4], (NSLOT, HID), dtype=jnp.float32) * 0.02, 'Wvd': jax.random.normal(ks[5], (VB, HID), dtype=jnp.float32) * 0.1 / np.sqrt(HID), 'Wvu': jax.random.normal(ks[6], (HID, VB), dtype=jnp.float32) * 0.1 / np.sqrt(VB), 'Wu1': jax.random.normal(ks[7], (HID // 4, HID), dtype=jnp.float32) / np.sqrt(HID), 'bu1': jnp.zeros((HID // 4,), dtype=jnp.float32), 'Wu2': jax.random.normal(ks[8], (1, HID // 4), dtype=jnp.float32) * 0.01, 'bu2': jnp.zeros((1,), dtype=jnp.float32), 'gate_w1': jnp.float32(0.5), 'gate_bias': jnp.float32(-1.0), 'log_rel': jnp.zeros((NSLOT,), dtype=jnp.float32)}
    _L2_ffn_in = _L2_ffn_setup()

    def _L3_attn_setup():
        import jax, jax.numpy as jnp
        import numpy as np
        B, C, L = (64, 64, 512)
        key = jax.random.key(seed)
        x = jax.random.normal(key, (B, C, L), dtype=jnp.float32)
        return {'x': x}
    _L3_attn_in = _L3_attn_setup()

    def _L3_ffn_setup():
        import jax, jax.numpy as jnp
        import numpy as np
        B, S, D, O, E, R = (2, 512, 512, 512, 8, 16)
        TOP_K = 2
        SCALING = 32.0 / 16.0
        key = jax.random.key(seed)
        k = jax.random.split(key, 6)
        x = jax.random.normal(k[0], (B, S, D), dtype=jnp.float32)
        W_base = jax.random.normal(k[1], (O, D), dtype=jnp.float32) * 0.02
        b_base = jax.random.normal(k[2], (O,), dtype=jnp.float32) * 0.02
        W_router = jax.random.normal(k[3], (E, D), dtype=jnp.float32) * 0.01
        lora_A = jax.random.normal(k[4], (E, R, D), dtype=jnp.float32) * (1.0 / np.sqrt(D))
        lora_B = jax.random.normal(k[5], (E, O, R), dtype=jnp.float32) * 0.02
        return {'x': x, 'W_base': W_base, 'b_base': b_base, 'W_router': W_router, 'lora_A': lora_A, 'lora_B': lora_B}
    _L3_ffn_in = _L3_ffn_setup()
    _d = {'L0_attn_x': _L0_attn_in['x'], 'L0_attn_Wq': _L0_attn_in['Wq'], 'L0_attn_Wk': _L0_attn_in['Wk'], 'L0_attn_Wv': _L0_attn_in['Wv'], 'L0_attn_Wo': _L0_attn_in['Wo'], 'L0_ffn_gate_w': _L0_ffn_in['gate_w'], 'L0_ffn_gate_s': _L0_ffn_in['gate_s'], 'L0_ffn_up_w': _L0_ffn_in['up_w'], 'L0_ffn_up_s': _L0_ffn_in['up_s'], 'L0_ffn_down_w': _L0_ffn_in['down_w'], 'L0_ffn_down_s': _L0_ffn_in['down_s'], 'L1_attn_w_qkv': _L1_attn_in['w_qkv'], 'L1_attn_w_dense': _L1_attn_in['w_dense'], 'L1_ffn_W_res': _L1_ffn_in['W_res'], 'L1_ffn_W_pre': _L1_ffn_in['W_pre'], 'L1_ffn_W_post': _L1_ffn_in['W_post'], 'L1_ffn_H_res_base': _L1_ffn_in['H_res_base'], 'L1_ffn_H_pre_base': _L1_ffn_in['H_pre_base'], 'L1_ffn_H_post_base': _L1_ffn_in['H_post_base'], 'L1_ffn_gate': _L1_ffn_in['gate'], 'L1_ffn_W_branch': _L1_ffn_in['W_branch'], 'L2_attn_Wq': _L2_attn_in['Wq'], 'L2_attn_Wk': _L2_attn_in['Wk'], 'L2_attn_Wv': _L2_attn_in['Wv'], 'L2_attn_Wo': _L2_attn_in['Wo'], 'L2_attn_q_norm_w': _L2_attn_in['q_norm_w'], 'L2_attn_k_norm_w': _L2_attn_in['k_norm_w'], 'L2_ffn_Wq': _L2_ffn_in['Wq'], 'L2_ffn_Wr': _L2_ffn_in['Wr'], 'L2_ffn_aux_keys': _L2_ffn_in['aux_keys'], 'L2_ffn_aux_values': _L2_ffn_in['aux_values'], 'L2_ffn_Wvd': _L2_ffn_in['Wvd'], 'L2_ffn_Wvu': _L2_ffn_in['Wvu'], 'L2_ffn_Wu1': _L2_ffn_in['Wu1'], 'L2_ffn_bu1': _L2_ffn_in['bu1'], 'L2_ffn_Wu2': _L2_ffn_in['Wu2'], 'L2_ffn_bu2': _L2_ffn_in['bu2'], 'L2_ffn_gate_w1': _L2_ffn_in['gate_w1'], 'L2_ffn_gate_bias': _L2_ffn_in['gate_bias'], 'L2_ffn_log_rel': _L2_ffn_in['log_rel'], 'L3_ffn_W_base': _L3_ffn_in['W_base'], 'L3_ffn_b_base': _L3_ffn_in['b_base'], 'L3_ffn_W_router': _L3_ffn_in['W_router'], 'L3_ffn_lora_A': _L3_ffn_in['lora_A'], 'L3_ffn_lora_B': _L3_ffn_in['lora_B']}
    _x0 = _d['L0_attn_x']
    _d['L0_attn_x'] = jax.random.normal(jax.random.fold_in(jax.random.key(seed), 1), (2, 512, 512), dtype=_x0.dtype)
    del _x0
    return _d

def reference(L0_attn_x, L0_attn_Wq, L0_attn_Wk, L0_attn_Wv, L0_attn_Wo, L0_ffn_gate_w, L0_ffn_gate_s, L0_ffn_up_w, L0_ffn_up_s, L0_ffn_down_w, L0_ffn_down_s, L1_attn_w_qkv, L1_attn_w_dense, L1_ffn_W_res, L1_ffn_W_pre, L1_ffn_W_post, L1_ffn_H_res_base, L1_ffn_H_pre_base, L1_ffn_H_post_base, L1_ffn_gate, L1_ffn_W_branch, L2_attn_Wq, L2_attn_Wk, L2_attn_Wv, L2_attn_Wo, L2_attn_q_norm_w, L2_attn_k_norm_w, L2_ffn_Wq, L2_ffn_Wr, L2_ffn_aux_keys, L2_ffn_aux_values, L2_ffn_Wvd, L2_ffn_Wvu, L2_ffn_Wu1, L2_ffn_bu1, L2_ffn_Wu2, L2_ffn_bu2, L2_ffn_gate_w1, L2_ffn_gate_bias, L2_ffn_log_rel, L3_ffn_W_base, L3_ffn_b_base, L3_ffn_W_router, L3_ffn_lora_A, L3_ffn_lora_B):

    def _L0_attn_ref(x, Wq, Wk, Wv, Wo):
        import jax, jax.numpy as jnp
        import numpy as np
        import math
        B, T, D_IN, D_OUT = (2, 256, 512, 512)
        N_HEADS, N_KV = (32, 8)
        HEAD_DIM = D_OUT // N_HEADS
        GROUP_SIZE = N_HEADS // N_KV
        ROPE_BASE = 500000.0
        CTX = 256

        def _rope_tables(head_dim, base, seq_len):
            inv_freq = 1.0 / base ** (jnp.arange(0, head_dim, 2, dtype=jnp.float32) / head_dim)
            t = jnp.arange(seq_len, dtype=jnp.float32)
            freqs = jnp.einsum('i,j->ij', t, inv_freq)
            return (jnp.cos(freqs), jnp.sin(freqs))

        def _apply_rope(x, cos, sin):
            x1, x2 = jnp.split(x, 2, axis=-1)
            c = cos[None, None]
            s = sin[None, None]
            return jnp.concatenate([x1 * c - x2 * s, x1 * s + x2 * c], axis=-1)
        b, t, _ = x.shape
        cos, sin = _rope_tables(HEAD_DIM, ROPE_BASE, t)
        q = (x @ Wq).reshape(b, t, N_HEADS, HEAD_DIM).transpose(0, 2, 1, 3)
        k = (x @ Wk).reshape(b, t, N_KV, HEAD_DIM).transpose(0, 2, 1, 3)
        v = (x @ Wv).reshape(b, t, N_KV, HEAD_DIM).transpose(0, 2, 1, 3)
        q = _apply_rope(q, cos, sin)
        k = _apply_rope(k, cos, sin)
        k_h = jnp.repeat(k, GROUP_SIZE, axis=1)
        v_h = jnp.repeat(v, GROUP_SIZE, axis=1)
        scores = jnp.einsum('bhqd,bhkd->bhqk', q, k_h) / math.sqrt(HEAD_DIM)
        causal = jnp.triu(jnp.ones((t, t), dtype=bool), k=1)
        scores = jnp.where(causal[None, None], jnp.finfo(scores.dtype).min, scores)
        attn = jax.nn.softmax(scores, axis=-1)
        ctx = jnp.einsum('bhqk,bhkd->bhqd', attn, v_h)
        ctx = ctx.transpose(0, 2, 1, 3).reshape(b, t, D_OUT)
        return ctx @ Wo

    def _L0_ffn_ref(x, gate_w, gate_s, up_w, up_s, down_w, down_s):
        import jax, jax.numpy as jnp
        import numpy as np
        D_MODEL = 512
        D_FF = 1376

        def _dequant_matmul(x, w_int, s):
            w = w_int.astype(jnp.float32) * s
            return x @ w.T
        batch, seq_len, hidden = x.shape
        x_flat = x.reshape(-1, hidden).astype(jnp.float32)
        gate = _dequant_matmul(x_flat, gate_w, gate_s)
        up = _dequant_matmul(x_flat, up_w, up_s)
        h = jax.nn.silu(gate) * up
        out = _dequant_matmul(h, down_w, down_s)
        return out.astype(x.dtype).reshape(batch, seq_len, hidden)

    def _L1_attn_ref(q, w_qkv, w_dense):
        import jax, jax.numpy as jnp
        import numpy as np
        B, S, EMB = (2, 256, 512)
        NHEADS, KVHEADS, HEAD_D = (32, 8, 128)
        SPLITS = (NHEADS * HEAD_D, KVHEADS * HEAD_D, KVHEADS * HEAD_D)
        Bq, Sq, _ = q.shape
        qkv = q @ w_qkv.T
        qs, ks, vs = jnp.split(qkv, np.cumsum(SPLITS)[:-1], axis=-1)
        G = NHEADS // KVHEADS
        qh = qs.reshape(Bq, Sq, KVHEADS, G, HEAD_D)
        kh = ks.reshape(Bq, Sq, KVHEADS, HEAD_D)
        vh = vs.reshape(Bq, Sq, KVHEADS, HEAD_D)
        scale = 1.0 / jnp.sqrt(jnp.float32(HEAD_D))
        scores = jnp.einsum('bskgd,btkd->bkgst', qh, kh) * scale
        causal = jnp.tril(jnp.ones((Sq, Sq), dtype=bool))
        scores = jnp.where(causal, scores, jnp.finfo(scores.dtype).min)
        probs = jax.nn.softmax(scores, axis=-1)
        attn = jnp.einsum('bkgst,btkd->bskgd', probs, vh)
        attn = attn.reshape(Bq, Sq, NHEADS * HEAD_D)
        return attn @ w_dense.T

    def _L1_ffn_ref(x, W_res, W_pre, W_post, H_res_base, H_pre_base, H_post_base, gate, W_branch):
        import jax, jax.numpy as jnp
        import numpy as np
        N_STREAMS = 4
        DIM = 128
        SINKHORN_ITERS = 50
        SINKHORN_TAU = 0.1
        RMS_EPS = 1.1920929e-07

        def sinkhorn_log(logits, num_iters=SINKHORN_ITERS, tau=SINKHORN_TAU):
            Z = logits / tau
            u0 = jnp.zeros(Z.shape[:-1], Z.dtype)
            v0 = jnp.zeros_like(u0)

            def step(carry, _):
                u, v = carry
                u = -jax.nn.logsumexp(Z + v[..., None, :], axis=-1)
                v = -jax.nn.logsumexp(Z + u[..., :, None], axis=-2)
                return ((u, v), None)
            (u, v), _ = jax.lax.scan(step, (u0, v0), None, length=num_iters)
            return jnp.exp(Z + u[..., :, None] + v[..., None, :])
        B, T, nC = x.shape
        n = N_STREAMS
        C = nC // n
        x_norm = x * jax.lax.rsqrt(jnp.mean(x * x, axis=-1, keepdims=True) + RMS_EPS)
        H_res_logits = (x_norm @ W_res.T).reshape(B, T, n, n) + H_res_base
        H_pre_logits = x_norm @ W_pre.T + H_pre_base
        H_post_logits = x_norm @ W_post.T + H_post_base
        H_res = sinkhorn_log(H_res_logits)
        H_pre = jax.nn.softmax(H_pre_logits, axis=-1)
        H_post = jax.nn.softmax(H_post_logits, axis=-1)
        g = jax.nn.sigmoid(gate)[0]
        I = jnp.eye(n, dtype=H_res.dtype)
        H_res = (1.0 - g) * I + g * H_res
        x_streams = x.reshape(B, T, n, C)
        x_pre = jnp.einsum('btnc,btn->btc', x_streams, H_pre)
        y = x_pre @ W_branch
        x_mixed = jnp.einsum('btij,btjc->btic', H_res, x_streams)
        y_distributed = jnp.einsum('btc,btn->btnc', y, H_post)
        return (x_mixed + y_distributed).reshape(B, T, nC)

    def _L2_attn_ref(x, Wq, Wk, Wv, Wo, q_norm_w, k_norm_w):
        import jax, jax.numpy as jnp
        import numpy as np
        import math
        B, S, DM = (1, 256, 512)
        H, HKV, HD = (32, 8, 128)
        EPS = 1e-06
        NEG_INF = -1e+30

        def _alibi_slopes(n_heads: int) -> np.ndarray:
            start = 2 ** (-2 ** (-(math.log2(n_heads) - 3)))
            return np.array([start * start ** i for i in range(n_heads)], dtype=np.float32)

        def _rmsnorm(t, w):
            tf = t.astype(jnp.float32)
            inv = jax.lax.rsqrt(jnp.mean(tf * tf, axis=-1, keepdims=True) + EPS)
            return (tf * inv * w).astype(t.dtype)
        b, s, _ = x.shape
        G = H // HKV
        q = (x @ Wq.T).reshape(b, s, H, HD).transpose(0, 2, 1, 3)
        k = (x @ Wk.T).reshape(b, s, HKV, HD).transpose(0, 2, 1, 3)
        v = (x @ Wv.T).reshape(b, s, HKV, HD).transpose(0, 2, 1, 3)
        q = _rmsnorm(q, q_norm_w)
        k = _rmsnorm(k, k_norm_w)
        qg = q.reshape(b, HKV, G, s, HD)
        scores = jnp.einsum('bkgqd,bksd->bkgqs', qg, k) / math.sqrt(HD)
        slopes = jnp.asarray(_alibi_slopes(H)).reshape(HKV, G)
        pos = jnp.arange(s, dtype=jnp.float32)
        rel = pos[None, :] - pos[:, None]
        bias = jnp.where(rel > 0, NEG_INF, slopes[:, :, None, None] * rel)
        attn = jax.nn.softmax(scores + bias[None], axis=-1)
        out = jnp.einsum('bkgqs,bksd->bkgqd', attn, v)
        out = out.reshape(b, H, s, HD).transpose(0, 2, 1, 3).reshape(b, s, H * HD)
        return out @ Wo.T

    def _L2_ffn_ref(hidden_states, Wq, Wr, aux_keys, aux_values, Wvd, Wvu, Wu1, bu1, Wu2, bu2, gate_w1, gate_bias, log_rel):
        import jax, jax.numpy as jnp
        import numpy as np
        HID, BOT, RDIM, NSLOT, K, VB = (512, 64, 48, 128, 8, 32)
        TAU_LOW, TAU_HIGH, EARLY_EXIT = (0.5, 2.0, 0.05)

        def _uncertainty(h, Wu1, bu1, Wu2, bu2):
            var = jnp.var(h, axis=-1)
            log_var = jnp.log1p(var)
            norm_var = log_var / (jnp.mean(log_var) + 1e-06)
            learned = (jax.nn.gelu(h @ Wu1.T + bu1) @ Wu2.T + bu2)[..., 0]
            return jnp.clip(norm_var * 0.5 + jax.nn.sigmoid(learned) * 2.5, 0.0, 5.0)
        query = hidden_states @ Wq.T
        rq = query @ Wr.T
        rk = aux_keys @ Wr.T
        router_scores = jnp.einsum('bsr,nr->bsn', rq, rk) / np.sqrt(RDIM) + log_rel
        top_scores, top_idx = jax.lax.top_k(router_scores, K)
        sel_keys = aux_keys[top_idx]
        attn = jnp.einsum('bsd,bskd->bsk', query, sel_keys) / np.sqrt(BOT) + log_rel[top_idx]
        w = jax.nn.softmax(attn, axis=-1)
        sel_vals = aux_values[top_idx]
        aux_out = jnp.einsum('bsk,bskh->bsh', w, sel_vals)
        aux_out = aux_out @ Wvd.T @ Wvu.T
        u = _uncertainty(hidden_states, Wu1, bu1, Wu2, bu2)
        u_norm = jnp.clip((u - TAU_LOW) / (TAU_HIGH - TAU_LOW), 0.0, 1.0)
        gate = jax.nn.sigmoid(gate_w1 * u_norm + gate_bias)
        gate = jnp.where(gate < EARLY_EXIT, 0.0, gate)
        return hidden_states + gate[..., None] * aux_out

    def _L3_attn_ref(x):
        import jax, jax.numpy as jnp
        import numpy as np
        B, C, L = (64, 64, 512)
        b, c, l = x.shape
        q = jnp.transpose(x, (2, 0, 1))
        scale = jnp.asarray(c, x.dtype) ** 0.5
        scores = jnp.einsum('lnc,lmc->lnm', q, q) / scale
        prob = jax.nn.softmax(scores, axis=-1)
        msg = jnp.einsum('lnm,lmc->lnc', prob, q)
        return x + jnp.transpose(msg, (1, 2, 0))

    def _L3_ffn_ref(x, W_base, b_base, W_router, lora_A, lora_B):
        import jax, jax.numpy as jnp
        import numpy as np
        B, S, D, O, E, R = (2, 512, 512, 512, 8, 16)
        TOP_K = 2
        SCALING = 32.0 / 16.0
        d = x.shape[-1]
        n_experts = W_router.shape[0]
        xf = x.reshape(-1, d)
        logits = xf @ W_router.T
        probs = jax.nn.softmax(logits, axis=-1)
        topk_p, topk_i = jax.lax.top_k(probs, TOP_K)
        topk_p = topk_p / jnp.sum(topk_p, axis=-1, keepdims=True)
        w = jnp.sum(jax.nn.one_hot(topk_i, n_experts, dtype=xf.dtype) * topk_p[..., None], axis=1)
        h = jnp.einsum('td,erd->ter', xf, lora_A)
        lora_out = jnp.einsum('ter,eor,te->to', h, lora_B, w) * SCALING
        base = x @ W_base.T + b_base
        return base + lora_out.reshape(x.shape[:-1] + (W_base.shape[0],))
    x = L0_attn_x
    x = _layernorm(x + _L0_attn_ref(x, L0_attn_Wq, L0_attn_Wk, L0_attn_Wv, L0_attn_Wo), axis=-1)
    x = _layernorm(x + _L0_ffn_ref(x, L0_ffn_gate_w, L0_ffn_gate_s, L0_ffn_up_w, L0_ffn_up_s, L0_ffn_down_w, L0_ffn_down_s), axis=-1)
    x = _layernorm(x + _L1_attn_ref(x, L1_attn_w_qkv, L1_attn_w_dense), axis=-1)
    x = _layernorm(x + _L1_ffn_ref(x, L1_ffn_W_res, L1_ffn_W_pre, L1_ffn_W_post, L1_ffn_H_res_base, L1_ffn_H_pre_base, L1_ffn_H_post_base, L1_ffn_gate, L1_ffn_W_branch), axis=-1)
    x = _layernorm(x + _L2_attn_ref(x, L2_attn_Wq, L2_attn_Wk, L2_attn_Wv, L2_attn_Wo, L2_attn_q_norm_w, L2_attn_k_norm_w), axis=-1)
    x = _layernorm(x + _L2_ffn_ref(x, L2_ffn_Wq, L2_ffn_Wr, L2_ffn_aux_keys, L2_ffn_aux_values, L2_ffn_Wvd, L2_ffn_Wvu, L2_ffn_Wu1, L2_ffn_bu1, L2_ffn_Wu2, L2_ffn_bu2, L2_ffn_gate_w1, L2_ffn_gate_bias, L2_ffn_log_rel), axis=-1)
    x = _layernorm(x + _L3_attn_ref(x), axis=-1)
    x = _layernorm(x + _L3_ffn_ref(x, L3_ffn_W_base, L3_ffn_b_base, L3_ffn_W_router, L3_ffn_lora_A, L3_ffn_lora_B), axis=-1)
    return x

_drawn_inputs = setup_inputs


def setup_inputs(seed=0):
    import zlib

    import numpy as np

    out = dict(_drawn_inputs(seed))
    spreads = {'L1_ffn_H_post_base': (0.0, 0.527),
     'L2_attn_q_norm_w': (1.0, 0.6),
     'L2_attn_k_norm_w': (1.0, 0.6),
     'L2_ffn_bu1': (0.0, 2.0),
     'L2_ffn_log_rel': (0.0, 2.0)}
    factors = {'L0_attn_Wq': 6.156,
     'L0_attn_Wk': 6.428,
     'L1_ffn_W_pre': 3.325,
     'L1_ffn_W_post': 3.292,
     'L2_ffn_Wq': 41.833,
     'L2_ffn_Wr': 46.177,
     'L2_ffn_aux_keys': 46.378,
     'L2_ffn_aux_values': 44.509,
     'L2_ffn_Wvd': 38.603,
     'L2_ffn_Wvu': 38.756,
     'L2_ffn_Wu1': 64.0,
     'L2_ffn_Wu2': 64.0,
     'L3_ffn_b_base': 3.14}
    for name, (base, spread) in spreads.items():
        noise = np.random.default_rng([zlib.crc32(name.encode()), seed]).standard_normal(out[name].shape)
        drawn = base * np.exp(spread * noise) if base else spread * noise
        out[name] = jnp.asarray(drawn.astype(out[name].dtype))
    for name, factor in factors.items():
        out[name] = (out[name] * factor).astype(out[name].dtype)
    return out
```

```python
from contextlib import ExitStack

import concourse.bass as bass
from concourse import mybir

P = 128
TOK = 1024
NB = 2
SEQ = TOK // NB
NT = TOK // P
TB = SEQ // P
D = 512
NC_ = D // P
HEADS, KV = 32, 8
GROUP = HEADS // KV
LN_EPS = 1e-5
MASKED = 1e30

F32 = mybir.dt.float32
F32R = mybir.dt.float32r
I32 = mybir.dt.int32
BF16 = mybir.dt.bfloat16
ALU = mybir.AluOpType
ACT = mybir.ActivationFunctionType
AX_X = mybir.AxisListType.X

SLOT = {3: (0, 0), 2: (1, 0), 0: (1, 384), 1: (2, 0)}
COL = {qi: 512 * b + o for qi, (b, o) in SLOT.items()}
ORDER = (3, 2, 0, 1)
PACKED = 1280


STAGES = ('attn0', 'ffn0', 'attn1', 'ffn1', 'attn2', 'ffn2', 'attn3', 'ffn3', )


class Memory:

    def __init__(self, nc, ctx, prefix):
        self.nc, self.ctx, self.prefix = nc, ctx, prefix
        self.sems = []
        ctx.callback(self.clear)

    def sb(self, name, shape, dt=F32):
        return self.ctx.enter_context(self.nc.sbuf_tensor(f"{self.prefix}_{name}", shape, dt))

    def ps(self, name, shape=(P, 512)):
        return self.ctx.enter_context(self.nc.psum_tensor(f"{self.prefix}_{name}", list(shape), F32))

    def sem(self, name):
        self.sems.append(self.nc.alloc_semaphore(name=f"{self.prefix}_{name}"))
        return self.sems[-1]

    def clear(self):
        if self.sems:
            self.nc.clear_and_free_semaphores(self.sems)
            self.nc.all_engine_barrier()


class Chain:

    def __init__(self, eng, sem):
        self.eng, self.sem, self.n = eng, sem, 0

    def __call__(self, instruction):
        self.n += 1
        instruction.then_inc(self.sem, 1)
        self.eng.wait_ge(self.sem, self.n)


def split_products(hi, lo):
    return ((0, 0), (0, 1), (1, 0))


def mm3(nc, out, a, b, start, stop):
    last = None
    for n, (i, j) in enumerate(((0, 0), (0, 1), (1, 0))):
        last = nc.tensor.matmul(out, a[i], b[j], start=start and n == 0, stop=stop and n == 2)
    return last


def setup_stage(nc, K, dram, pre):
    with ExitStack() as ctx:
        m = Memory(nc, ctx, pre)
        mask = m.sb("mask", [P, P])
        x_in, made, done = m.sem("x_in"), m.sem("made"), m.sem("done")
        block = ctx.enter_context(nc.Block())

        @block.sync
        def _(sp):
            sp.dma_start(K.xs[:], dram["x"].rearrange("(t p) d -> p t d", p=P)).then_inc(x_in, 16)
            sp.wait_ge(x_in, 16)

        @block.gpsimd
        def _(pool):
            step = Chain(pool, made)
            step(nc.gpsimd.memset(K.ident[:], 0.0))
            step(nc.gpsimd.affine_select(out=K.ident[:], in_=K.ident[:], compare_op=ALU.not_equal, fill=1.0,
                                         base=0, pattern=[[-1, P]], channel_multiplier=1))
            step(nc.gpsimd.memset(mask[:], 0.0))
            step(nc.gpsimd.affine_select(out=mask[:], in_=mask[:], compare_op=ALU.is_ge, fill=MASKED,
                                         base=0, pattern=[[-1, P]], channel_multiplier=1))
            step(nc.gpsimd.memset(K.half[:], -0.5))
            step(nc.gpsimd.memset(K.zero[:], 0.0))
            nc.gpsimd.tensor_copy(K.ident_r[:], K.ident[:]).then_inc(done, 1)
            nc.gpsimd.tensor_copy(K.mask_r[:], mask[:]).then_inc(done, 1)
            pool.wait_ge(done, 2)


def norm_stage(nc, K, pre, normalize=True, full=None, out=None):
    with ExitStack() as ctx:
        m = Memory(nc, ctx, pre)
        stats, mv = m.sb("stats", [P, NT, 6]), m.sb("mv", [P, NT, 2])
        rstd, vare = m.sb("rstd", [P, NT]), m.sb("vare", [P, NT])
        banks = [m.ps(f"bank{n}") for n in range(4)]
        stats_done, mv_done, eps_done, rstd_done = (m.sem(n) for n in ("stats", "mv", "eps", "rstd"))
        normed, transposed, hi_done, evacuated = (m.sem(n) for n in ("normed", "transposed", "hi", "evacuated"))
        stored = K.stored
        block = ctx.enter_context(nc.Block())

        if out is not None:
            @block.sync
            def _(sp):
                for t in range(NT):
                    sp.wait_ge(normed, t + 1)
                    sp.dma_start(out[t * P:(t + 1) * P, :], K.xs[:, t, :]).then_inc(stored, 16)
                sp.wait_ge(stored, 16 * NT)

        if normalize:
            @block.gpsimd
            def _(pool):
                for b in range(NB):
                    s = slice(b * TB, (b + 1) * TB)
                    pool.wait_ge(mv_done, (b + 1) * TB)
                    nc.gpsimd.tensor_scalar(vare[:, s], mv[:, s, 1], LN_EPS, None, ALU.add).then_inc(eps_done, 1)
                    pool.wait_ge(eps_done, b + 1)
                    nc.gpsimd.tensor_tensor(rstd[:, s], vare[:, s], K.half[:, s], ALU.pow).then_inc(rstd_done, 1)

        @block.vector
        def _(dve):
            if normalize:
                for t in range(NT):
                    nc.vector.bn_stats(stats[:, t, :], K.xs[:, t, :]).then_inc(stats_done, 1)
                for t in range(NT):
                    dve.wait_ge(stats_done, t + 1)
                    nc.vector.bn_aggr(mv[:, t, :], stats[:, t, :]).then_inc(mv_done, 1)
                for t in range(NT):
                    if t % TB == 0:
                        dve.wait_ge(rstd_done, t // TB + 1)
                    dve.wait_ge(mv_done, t + 1)
                    nc.vector.tensor_scalar(K.xs[:, t, :], K.xs[:, t, :], mv[:, t, 0:1], rstd[:, t:t + 1],
                                            ALU.subtract, ALU.mult).then_inc(normed, 1)
            if out is None and full is None:
                for n in range(NB * NC_):
                    b, c = divmod(n, NC_)
                    dve.wait_ge(hi_done, n + 1)
                    s = slice(b * SEQ, (b + 1) * SEQ)
                    nc.vector.tensor_tensor(K.xl[:, c, s], banks[n % 4][:], K.xh[:, c, s].bitcast(F32),
                                            ALU.subtract).then_inc(evacuated, 1)

        if out is not None:
            return

        @block.tensor
        def _(pe):
            for n in range(NB * NC_):
                b, c = divmod(n, NC_)
                if normalize and c == 0:
                    pe.wait_ge(normed, (b + 1) * TB)
                if n >= 4:
                    pe.wait_ge(evacuated, n - 3)
                for i in range(TB):
                    last = nc.tensor.transpose(banks[n % 4][:, i * P:(i + 1) * P],
                                               K.xs[:, b * TB + i, c * P:(c + 1) * P], K.ident[:])
                last.then_inc(transposed, 1)

        @block.scalar
        def _(act):
            for n in range(NB * NC_):
                b, c = divmod(n, NC_)
                s = slice(b * SEQ, (b + 1) * SEQ)
                act.wait_ge(transposed, n + 1)
                if full is None:
                    nc.scalar.activation(K.xh[:, c, s], banks[n % 4][:], ACT.Copy).then_inc(hi_done, 1)
                else:
                    nc.scalar.activation(full[:, c, s], banks[n % 4][:], ACT.Copy).then_inc(evacuated, 1)


HD0 = 16
G0 = (GROUP + 2) * HD0


def rotary_attention_stage(nc, K, dram, pre):
    NEG = -float(HD0) ** -0.5
    with ExitStack() as ctx:
        m = Memory(nc, ctx, pre)
        sb, sem = m.sb, m.sem
        S = [m.ps(f"scores{n}") for n in range(3)]
        T = [m.ps(f"turned{n}") for n in range(3)]
        O = m.ps("mixed")
        W = m.ps("work")
        area = [sb(f"area{n}", [P, KV * SEQ], F32R) for n in "hl"]
        w = [a[:, 0:NC_ * KV * G0] for a in area]
        cT = [[a[:].rearrange("p c t -> p (c t)") for a in (K.xh, K.xl)], [a[:] for a in area]]
        wo = [sb(f"wo{n}", [P, KV, D], F32R) for n in "hl"]
        cos, sin = sb("cos", [P, TB, HD0]), sb("sin", [P, TB, HD0])
        qkv = sb("qkv", [P, NT, KV * G0])
        rot, rot2 = sb("rot", [P, TB, GROUP + 1, HD0]), sb("rot2", [P, TB, GROUP + 1, HD0])
        qs = sb("qs", [P, TB, GROUP, 2, HD0])
        ks = [sb(f"ks{n}", [P, TB, 2 * GROUP, HD0]) for n in "hl"]
        qT = sb("qT", [P, NB, SEQ], F32R)
        kT = [sb(f"kT{n}", [P, NB, SEQ], F32R) for n in "hl"]
        v = [sb(f"v{n}", [P, NB, TB, 224], F32R) for n in "hl"]
        probs = sb("probs", [P, 2 * PACKED])
        n_w, n_wo = NC_ * KV * G0, KV * D // 2
        flat = qkv[:].rearrange("p t n -> p (t n)")
        w_raw = flat[:, 0:n_w]
        wo_raw = [a.rearrange("p (i n) -> p i n", n=D) for a in (flat[:, n_w:n_w + n_wo], probs[:, 0:n_wo])]
        negmax, rowsum = (sb(n, [P, 2, 4]) for n in ("negmax", "rowsum"))
        recip = sb("recip", [P, 2, 4])
        pT = [sb(f"pT{n}", [P, PACKED], F32R) for n in "hl"]
        x = [K.xh, K.xl]
        w_in, table_in, wo_in = sem("w_in"), sem("table_in"), [sem(f"wo_in{n}") for n in range(2)]
        w_hi, w_split, wo_split = sem("w_hi"), sem("w_split"), sem("wo_split")
        work_full, work_free = sem("work_full"), sem("work_free")
        proj_full, proj_taken = sem("proj_full"), sem("proj_taken")
        rotated_step, rotated, parts_step, parts_done = (
            sem(n) for n in ("rotated_step", "rotated", "parts_step", "parts"))
        scored, min_done, exp_done, recip_done, scaled = (
            sem(n) for n in ("scored", "min", "exp", "recip", "scaled"))
        turned, pT_hi_done, pT_done = sem("turned"), sem("pT_hi"), sem("pT")
        mixed, mixed_hi, mixed_taken, out_full, out_free = (
            sem(n) for n in ("mixed", "mixed_hi", "mixed_taken", "out", "out_free"))
        block = ctx.enter_context(nc.Block())

        def unit(i, b, j):
            return 8 * i + 4 * b + j

        def ends(i, b):
            at = isinstance(i, int)
            return at and i == 0 and b == 0, at and i == KV - 1 and b == 1

        def use(i, b, n):
            return 3 * (2 * i + b) + n

        def before(i, b, j):
            return (i, b, j - 1) if j else (i, 0, 3) if b else (i - 1, 1, 3)

        def after(i, b, j):
            return (i, b, j + 1) if j < 3 else (i, 1, 0) if b == 0 else (i + 1, 0, 0)

        def loop(eng, body):
            body(0)
            with eng.Fori(1, KV - 1) as i:
                body(i)
            body(KV - 1)

        @block.sync
        def _(sp):
            sp.dma_start(w_raw, dram["w0"]).then_inc(w_in, 16)
            sp.dma_start(cos[:], dram["cos"]).then_inc(table_in, 16)
            sp.dma_start(sin[:], dram["sin"]).then_inc(table_in, 16)
            for n in range(2):
                sp.dma_start(wo_raw[n], dram["wo0"][:, n * KV // 2:(n + 1) * KV // 2, :]).then_inc(wo_in[n], 16)

        @block.gpsimd
        def _(pool):
            step = Chain(pool, w_hi)
            pool.wait_ge(w_in, 16)
            step(nc.gpsimd.tensor_copy(w[0], w_raw))
            nc.gpsimd.tensor_tensor(w[1], w_raw, w[0].bitcast(F32), ALU.subtract).then_inc(w_split, 1)
            for a in v:
                step(nc.gpsimd.memset(a[:].bitcast(F32), 0.0))
            for n in range(2):
                hi, lo = (a[:, n * KV // 2:(n + 1) * KV // 2, :] for a in wo)
                pool.wait_ge(wo_in[n], 16)
                step(nc.gpsimd.tensor_copy(hi, wo_raw[n]))
                nc.gpsimd.tensor_tensor(lo, wo_raw[n], hi.bitcast(F32), ALU.subtract).then_inc(wo_split, 1)

            def parts(i, b):
                p = 2 * i + b
                pool.wait_ge(rotated, p + 1)
                if not (isinstance(p, int) and p == 0):
                    pool.wait_ge(work_full, 3 * p)
                zero = K.zero[:, 0:1].unsqueeze(2)
                q_in = rot[:, :, 0:GROUP, :]
                k_in = rot[:, :, GROUP:GROUP + 1, :].to_broadcast([P, TB, 2 * GROUP, HD0])
                v_in = qkv[:, b * TB:(b + 1) * TB, bass.ds(i * G0 + (GROUP + 1) * HD0, HD0)]
                q_hi = qs[:, :, :, 0, :]
                nc.gpsimd.tensor_tensor(q_hi.bitcast(F32R), q_in,
                                        zero.unsqueeze(3).to_broadcast([P, TB, GROUP, HD0]), ALU.add
                                        ).then_inc(parts_step, 1)
                nc.gpsimd.tensor_tensor(ks[0][:].bitcast(F32R), k_in,
                                        zero.unsqueeze(3).to_broadcast([P, TB, 2 * GROUP, HD0]), ALU.add
                                        ).then_inc(parts_step, 1)
                if not (isinstance(p, int) and p < 2):
                    pool.wait_ge(mixed, 4 * (p - 1))
                for a in v:
                    nc.gpsimd.tensor_tensor(a[:, b, :, 96:96 + HD0], v_in, zero.to_broadcast([P, TB, HD0]),
                                            ALU.add).then_inc(parts_step, 1)
                pool.wait_ge(parts_step, 4 * p + 4)
                nc.gpsimd.tensor_tensor(qs[:, :, :, 1, :].bitcast(F32R), q_in, q_hi, ALU.subtract
                                        ).then_inc(parts_done, 1)
                nc.gpsimd.tensor_tensor(ks[1][:].bitcast(F32R), k_in, ks[0][:], ALU.subtract
                                        ).then_inc(parts_done, 1)
                nc.gpsimd.tensor_tensor(v[0][:, b, :, 96 + HD0:128], v_in, v[0][:, b, :, 96:96 + HD0].bitcast(F32),
                                        ALU.subtract).then_inc(parts_done, 1)

            def scale(i, b, j):
                u = unit(i, b, j)
                pool.wait_ge(recip_done, u + 1)
                for qi in ORDER:
                    pr = probs[:, j % 2 * PACKED + COL[qi]:j % 2 * PACKED + COL[qi] + (qi + 1) * P]
                    nc.gpsimd.tensor_tensor(pr, pr, recip[:, j % 2, qi:qi + 1].to_broadcast([P, (qi + 1) * P]),
                                            ALU.mult).then_inc(scaled, 1)

            parts(0, 0)

            def body(i):
                for b in range(NB):
                    for j in range(GROUP):
                        scale(i, b, j)
                        if j == 0 and not ends(i, b)[1]:
                            parts(*((i, 1) if b == 0 else (i + 1, 0)))
            loop(pool, body)

        @block.tensor
        def _(pe):
            wv = [a.rearrange("p (c n) -> p c n", c=NC_) for a in w]

            pe.wait_ge(w_split, 1)
            half = KV * G0 // 2
            for n in range(2 * NT):
                t, h = divmod(n, 2)
                if n >= 2:
                    pe.wait_ge(proj_taken, n - 1)
                for c in range(NC_):
                    last = mm3(nc, (W, O)[h][:, 0:half], [a[:, c, t * P:(t + 1) * P] for a in x],
                               [a[:, c, h * half:(h + 1) * half] for a in wv], c == 0, c == NC_ - 1)
                last.then_inc(proj_full, 1)

            def turn(i, b, n):
                if not (ends(i, b)[0] and n == 0):
                    pe.wait_ge(work_free, use(i, b, n))
                if n == 0:
                    pe.wait_ge(parts_done, 3 * (2 * i + b) + 3)
                for t in range(TB):
                    src = (qs[:, t].rearrange("p h a d -> p (h a d)") if n == 0 else
                           ks[n - 1][:, t].rearrange("p h d -> p (h d)"))
                    last = nc.tensor.transpose(W[:, t * P:(t + 1) * P], src, K.ident[:])
                last.then_inc(work_full, 1)

            def scores(i, b, j):
                u = unit(i, b, j)
                if j == 0:
                    pe.wait_ge(work_free, use(i, b, 3))
                strip = slice(32 * j, 32 * j + 32)
                for n, group in enumerate(((3,), (2, 0), (1,))):
                    if not (ends(i, b)[0] and j == 0):
                        pe.wait_ge(exp_done, 4 * (u - 1) + (1, 3, 4)[n])
                    for qi in group:
                        keys = (qi + 1) * P
                        off = COL[qi] - 512 * n
                        out = S[n][:, off:off + keys]
                        for a in (0, 1):
                            nc.tensor.matmul(out, qT[strip, b, qi * P:(qi + 1) * P], kT[a][strip, b, 0:keys],
                                             start=a == 0, stop=False)
                        last = nc.tensor.matmul(out[:, qi * P:keys], K.ident_r[:], K.mask_r[:],
                                                start=False, stop=True)
                    last.then_inc(scored, 1)

            def turn_probs(i, b, j):
                u = unit(i, b, j)
                pe.wait_ge(scaled, 4 * (u + 1))
                for n, group in enumerate(((3,), (2, 0), (1,))):
                    for back in group:
                        kj = 3 - back
                        off = COL[back] - 512 * n
                        for qi in range(kj, TB):
                            last = nc.tensor.transpose(
                                T[n][:, off + (qi - kj) * P:off + (qi - kj + 1) * P],
                                probs[:, j % 2 * PACKED + COL[qi] + kj * P:][:, 0:P], K.ident[:])
                    last.then_inc(turned, 1)

            def mix(i, b, j):
                if j == 0 and not ends(i, b)[0]:
                    pe.wait_ge(mixed_taken, 2 * i + b)
                pe.wait_ge(pT_done, 3 * unit(i, b, j) + 3)
                for kj in range(TB):
                    for a in (0, 1):
                        last = nc.tensor.matmul(O[:, kj * P:], v[a][:, b, kj, 96 - 32 * j:224 - 32 * j],
                                                pT[a][:, COL[3 - kj]:COL[3 - kj] + (TB - kj) * P],
                                                start=j == 0 and kj == 0 and a == 0,
                                                stop=j == 3 and kj == 3 and a == 1)
                last.then_inc(mixed, 1)

            pe.wait_ge(proj_taken, 2 * NT)
            for n in range(3):
                turn(0, 0, n)
            scores(0, 0, 0)

            def body(i):
                for b in range(NB):
                    last = ends(i, b)[1]
                    for j in range(GROUP):
                        new = (i, 1) if b == 0 else (i + 1, 0)
                        if not (last and j == 3):
                            scores(*after(i, b, j))
                        if not last and j in (1, 2):
                            turn(*new, 2 * (j - 1))
                        if not (ends(i, b)[0] and j == 0):
                            mix(*before(i, b, j))
                        turn_probs(i, b, j)
                        if not last and j == 1:
                            turn(*new, 1)
            loop(pe, body)
            mix(KV - 1, 1, 3)

            pe.wait_ge(wo_split, 2)
            for t in range(NT):
                b, q = divmod(t, TB)
                if t == 0:
                    pe.wait_ge(exp_done, 4 * 64)
                if t == TB:
                    pe.wait_ge(mixed_taken, 2 * KV)
                if t == NT - 1:
                    pe.wait_ge(out_free, 1)
                for i in range(KV):
                    at = i * SEQ + q * P
                    last = mm3(nc, (S + T + [W, S[0]])[t][:], [a[:, at:at + P] for a in cT[b]],
                               [a[:, i, :] for a in wo], i == 0, i == KV - 1)
                last.then_inc(out_full, 1)

        @block.scalar
        def _(act):
            for n in range(2 * NT):
                t, h = divmod(n, 2)
                half = KV * G0 // 2
                act.wait_ge(proj_full, n + 1)
                if t == NT // 2:
                    act.wait_ge(wo_split, 1)
                nc.scalar.activation(qkv[:, t, h * half:(h + 1) * half], (W, O)[h][:, 0:half], ACT.Copy
                                     ).then_inc(proj_taken, 1)

            def keep(i, b, n):
                act.wait_ge(work_full, use(i, b, n) + 1)
                dst = qT if n == 0 else kT[n - 1]
                nc.scalar.activation(dst[:, b, :], W[:], ACT.Copy, scale=NEG if n == 0 else 1.0
                                     ).then_inc(work_free, 1)

            def exps(i, b, j):
                u = unit(i, b, j)
                for qi, minima in zip(ORDER, (1, 3, 3, 4)):
                    act.wait_ge(min_done, 4 * u + minima)
                    nc.scalar.activation(probs[:, j % 2 * PACKED + COL[qi]:j % 2 * PACKED + COL[qi] + (qi + 1) * P],
                                         S[SLOT[qi][0]][:, SLOT[qi][1]:SLOT[qi][1] + (qi + 1) * P],
                                         ACT.Exp, bias=negmax[:, j % 2, qi:qi + 1], scale=-1.0,
                                         accum_out=rowsum[:, j % 2, qi:qi + 1]).then_inc(exp_done, 1)

            for n in range(3):
                keep(0, 0, n)
            act.wait_ge(wo_split, 2)
            exps(0, 0, 0)

            def body(i):
                for b in range(NB):
                    last = ends(i, b)[1]
                    ni, nb = (i, 1) if b == 0 else (i + 1, 0)
                    for j in range(GROUP):
                        u = unit(i, b, j)
                        if not (last and j == 3):
                            exps(*after(i, b, j))
                        if not last and j in (1, 2):
                            keep(ni, nb, 2 * (j - 1))
                        for n in range(3):
                            act.wait_ge(turned, 3 * u + n + 1)
                            s = slice(512 * n, min(512 * (n + 1), PACKED))
                            nc.scalar.activation(pT[0][:, s], T[n][:, 0:s.stop - s.start], ACT.Copy
                                                 ).then_inc(pT_hi_done, 1)
                        if not last and j == 1:
                            keep(ni, nb, 1)
            loop(act, body)

        @block.vector
        def _(dve):
            def rotate(i, b):
                p = 2 * i + b
                if not (isinstance(p, int) and p == 0):
                    dve.wait_ge(parts_done, 3 * p)
                if isinstance(p, int) and p < 2:
                    dve.wait_ge(proj_taken, (b + 1) * NT)
                qk = (qkv[:, b * TB:(b + 1) * TB, bass.ds(i * G0, (GROUP + 1) * HD0)]
                      .rearrange("p t (h d) -> p t h d", d=HD0))
                half = HD0 // 2

                def table(t, lo, hi):
                    return t[:, :, lo:hi].unsqueeze(2).to_broadcast([P, TB, GROUP + 1, hi - lo])
                nc.vector.tensor_tensor(rot[:], qk, table(cos, 0, HD0), ALU.mult).then_inc(rotated_step, 1)
                nc.vector.tensor_tensor(rot2[:, :, :, 0:half], qk[:, :, :, half:], table(sin, 0, half),
                                        ALU.mult).then_inc(rotated_step, 1)
                nc.vector.tensor_tensor(rot2[:, :, :, half:], qk[:, :, :, 0:half], table(sin, half, HD0),
                                        ALU.mult).then_inc(rotated_step, 1)
                dve.wait_ge(rotated_step, 3 * p + 3)
                nc.vector.tensor_tensor(rot[:], rot[:], rot2[:], ALU.add).then_inc(rotated, 1)

            def minima(i, b, j):
                u = unit(i, b, j)
                for qi, need in zip(ORDER, (1, 2, 2, 3)):
                    dve.wait_ge(scored, 3 * u + need)
                    nc.vector.tensor_reduce(negmax[:, j % 2, qi:qi + 1],
                                            S[SLOT[qi][0]][:, SLOT[qi][1]:SLOT[qi][1] + (qi + 1) * P],
                                            AX_X, ALU.min).then_inc(min_done, 1)

            def reciprocals(i, b, j):
                dve.wait_ge(exp_done, 4 * unit(i, b, j) + 4)
                nc.vector.reciprocal(recip[:, j % 2, :], rowsum[:, j % 2, :]).then_inc(recip_done, 1)

            dve.wait_ge(table_in, 32)
            rotate(0, 0)
            minima(0, 0, 0)
            reciprocals(0, 0, 0)

            def take_mixed(i, b):
                p = 2 * i + b
                hi, lo = (a[:, bass.ds(i * SEQ, SEQ)] for a in cT[b])
                dve.wait_ge(mixed, 4 * p + 4)
                nc.vector.tensor_tensor(hi, O[:], K.zero[:, 0:1].to_broadcast([P, SEQ]), ALU.add
                                        ).then_inc(mixed_hi, 1)
                dve.wait_ge(mixed_hi, p + 1)
                nc.vector.tensor_tensor(lo, O[:], hi.bitcast(F32), ALU.subtract).then_inc(mixed_taken, 1)

            def body(i):
                for b in range(NB):
                    last = ends(i, b)[1]
                    for j in range(GROUP):
                        u = unit(i, b, j)
                        if not last and j == 0:
                            rotate(*((i, 1) if b == 0 else (i + 1, 0)))
                        if not (last and j == 3):
                            minima(*after(i, b, j))
                            reciprocals(*after(i, b, j))
                        for n in range(3):
                            dve.wait_ge(pT_hi_done, 3 * u + n + 1)
                            s = slice(512 * n, min(512 * (n + 1), PACKED))
                            nc.vector.tensor_tensor(pT[1][:, s], T[n][:, 0:s.stop - s.start],
                                                    pT[0][:, s].bitcast(F32), ALU.subtract
                                                    ).then_inc(pT_done, 1)
                        if j == 0 and not ends(i, b)[0]:
                            take_mixed(*before(i, b, 0)[:2])
            loop(dve, body)
            take_mixed(KV - 1, 1)
            for t in range(NT):
                dve.wait_ge(out_full, t + 1)
                xt = K.xs[:, t, :]
                done = nc.vector.tensor_tensor(xt, xt, (S + T + [W, S[0]])[t][:], ALU.add)
                if t == 0:
                    done.then_inc(out_free, 1)


FF = 1376
NF = -(-FF // P)


def gated_ffn_stage(nc, K, dram, pre):
    with ExitStack() as ctx:
        m = Memory(nc, ctx, pre)
        sb, sem = m.sb, m.sem
        bank = [[[m.ps(f"bank{s}{w}{b}") for b in range(NB)] for w in range(2)] for s in range(2)]
        raw = sb("raw", [P, 2, 2 * NC_ * P], I32)
        wgu = sb("wgu", [P, 2, 2, NC_, P], F32R)
        down = sb("down", [P, NF, D], F32R)
        down_raw = sb("down_raw", [P, 2, D], I32)
        scales = sb("scales", [P, NF, 2])
        gate_scale = sb("gate_scale", [P, 2])
        down_scale, scaled = sb("down_scale", [P, D]), sb("scaled", [P, 2, D])
        silu = sb("silu", [P, 2, TOK])
        h = sb("h", [P, TOK])
        hT = [sb(f"hT{n}", [P, NF, TOK], F32R) for n in "hl"]
        raw_in, scale_in, down_in = [sem("raw_in0"), sem("raw_in1")], sem("scale_in"), [sem("down_in0"), sem("down_in1")]
        w_ready, down_ready = sem("w_ready"), sem("down_ready")
        full, gate_taken, gate_scaled, h_step, h_done = (
            sem(n) for n in ("full", "gate_taken", "gate_scaled", "h_step", "h_done"))
        out_full, out_step, out_done = sem("out_full"), sem("out_step"), sem("out_done")
        down_scale_in = sem("down_scale_in")
        block = ctx.enter_context(nc.Block())
        x = [K.xh, K.xl]

        def loop(eng, body):
            body(0, 0)
            body(1, 1)
            with eng.Fori(2, NF - 1, 2) as f:
                body(f, 0)
                body(f + 1, 1)
            body(NF - 1, (NF - 1) % 2)

        @block.sync
        def _(sp):
            sp.dma_start(scales[:], dram["gu_scale"]).then_inc(scale_in, 16)

            def body(f, s):
                if not (isinstance(f, int) and f < 2):
                    sp.wait_ge(w_ready, f - 1)
                row = bass.ds(f, 1)
                sp.dma_start(raw[:, s, :], dram["gu"][row, :, :].rearrange("a p n -> p (a n)")
                             ).then_inc(raw_in[s], 16)
                if isinstance(f, int) and f == 1:
                    sp.dma_start(down_scale[:], dram["down_scale"]).then_inc(down_scale_in, 16)
                if not (isinstance(f, int) and f < 2):
                    sp.wait_ge(down_ready, f - 1)
                sp.dma_start(down_raw[:, s, :], dram["down"][row, :, :].rearrange("a p n -> p (a n)")
                             ).then_inc(down_in[s], 16)
            loop(sp, body)

        @block.gpsimd
        def _(pool):
            for f in range(NF):
                pool.wait_ge(down_in[f % 2], 16 * (f // 2 + 1))
                nc.gpsimd.tensor_copy(down[:, f, :], down_raw[:, f % 2, :]).then_inc(down_ready, 1)

        @block.tensor
        def _(pe):
            def body(f, s):
                pe.wait_ge(w_ready, f + 1)
                for w in range(2):
                    if not (isinstance(f, int) and f < 2):
                        if w == 0:
                            pe.wait_ge(gate_taken, f - 1)
                        else:
                            pe.wait_ge(h_step, 2 * (f - 2) + 2)
                    for c in range(NC_):
                        for a in range(2):
                            for b in range(NB):
                                last = nc.tensor.matmul(bank[s][w][b][:], wgu[:, s, w, c, :],
                                                        x[a][:, c, b * SEQ:(b + 1) * SEQ],
                                                        start=c == 0 and a == 0, stop=c == NC_ - 1 and a == 1)
                    last.then_inc(full, 1)
            loop(pe, body)
            pe.wait_ge(down_ready, NF)
            flat = [bank[s][w][b] for s in range(2) for w in range(2) for b in range(NB)]
            pe.wait_ge(h_done, NF)
            for t in range(NT):
                for f in range(NF):
                    for a in range(2):
                        last = nc.tensor.matmul(flat[t][:], hT[a][:, f, t * P:(t + 1) * P], down[:, f, :],
                                                start=f == 0 and a == 0, stop=f == NF - 1 and a == 1)
                last.then_inc(out_full, 1)

        @block.scalar
        def _(act):
            def body(f, s):
                if not (isinstance(f, int) and f < 2):
                    act.wait_ge(h_step, 2 * (f - 2) + 2)
                act.wait_ge(gate_scaled, f + 1)
                act.wait_ge(full, 2 * f + 1)
                nc.scalar.activation(silu[:, s, 0:SEQ], bank[s][0][0][:], ACT.Silu, scale=gate_scale[:, s:s + 1])
                nc.scalar.activation(silu[:, s, SEQ:], bank[s][0][1][:], ACT.Silu, scale=gate_scale[:, s:s + 1]
                                     ).then_inc(gate_taken, 1)
            loop(act, body)

        @block.vector
        def _(dve):
            dve.wait_ge(scale_in, 16)

            def prepare(f, s):
                if not (isinstance(f, int) and f < 2):
                    dve.wait_ge(gate_taken, f - 1)
                nc.vector.tensor_scalar(gate_scale[:, s:s + 1], scales[:, bass.ds(f, 1), 0:1]
                                        .rearrange("p a b -> p (a b)"), 1.0, None, ALU.mult
                                        ).then_inc(gate_scaled, 1)
                dve.wait_ge(raw_in[s], 16 * count(f, s))
                if not (isinstance(f, int) and f < 2):
                    dve.wait_ge(full, 2 * (f - 2) + 2)
                nc.vector.tensor_copy(wgu[:, s].rearrange("p w c n -> p (w c n)"), raw[:, s, :]
                                      ).then_inc(w_ready, 1)

            marks = {}

            def count(f, s):
                return f // 2 + 1 if isinstance(f, int) else marks["k"] + 1

            def hidden(f):
                s = marks["s"]
                dve.wait_ge(gate_taken, f + 1)
                dve.wait_ge(full, 2 * f + 2)
                if not (isinstance(f, int) and f == 0):
                    dve.wait_ge(h_done, f)
                for b in range(NB):
                    cols = slice(b * SEQ, (b + 1) * SEQ)
                    nc.vector.scalar_tensor_tensor(
                        out=h[:, cols], in0=bank[s][1][b][:],
                        scalar=scales[:, bass.ds(f, 1), 1:2].rearrange("p a b -> p (a b)"),
                        in1=silu[:, s, cols], op0=ALU.mult, op1=ALU.mult).then_inc(h_step, 1)
                dve.wait_ge(h_step, 2 * f + 2)
                hi = hT[0][:, bass.ds(f, 1), :].rearrange("p a n -> p (a n)")
                nc.vector.tensor_scalar(hi, h[:], 1.0, None, ALU.mult).then_inc(hi_done, 1)
                dve.wait_ge(hi_done, f + 1)
                nc.vector.tensor_tensor(hT[1][:, bass.ds(f, 1), :].rearrange("p a n -> p (a n)"), h[:],
                                        hi.bitcast(F32), ALU.subtract).then_inc(h_done, 1)
            hi_done = sem("hi_done")
            prepare(0, 0)
            prepare(1, 1)
            marks["s"] = 0
            hidden(0)
            prepare(2, 0)
            marks["s"] = 1
            hidden(1)
            prepare(3, 1)
            with dve.Fori(1, (NF - 1) // 2 - 1) as k:
                for s in range(2):
                    marks["s"] = s
                    marks["k"] = k + 1
                    hidden(2 * k + s)
                    prepare(2 * k + s + 2, s)
            for f in range(NF - 3, NF):
                marks["s"] = f % 2
                hidden(f)
                if f == NF - 3:
                    prepare(NF - 1, (NF - 1) % 2)
            flat = [bank[s][w][b] for s in range(2) for w in range(2) for b in range(NB)]
            dve.wait_ge(down_scale_in, 16)
            for t in range(NT):
                dve.wait_ge(out_full, t + 1)
                nc.vector.tensor_tensor(scaled[:, t % 2, :], flat[t][:], down_scale[:], ALU.mult
                                        ).then_inc(out_step, 1)
                dve.wait_ge(out_step, t + 1)
                nc.vector.tensor_tensor(K.xs[:, t, :], K.xs[:, t, :], scaled[:, t % 2, :], ALU.add
                                        ).then_inc(out_done, 1)


RAW_SLOTS = 2
PIECES = 10
RMS_EPS = 1e-6


def attention_stage(nc, K, dram, kind, pre):
    NEG = -float(P) ** -0.5
    with ExitStack() as ctx:
        m = Memory(nc, ctx, pre)
        sb, sem = m.sb, m.sem
        S = [m.ps(f"scores{n}") for n in range(3)]
        T = [m.ps(f"turned{n}") for n in range(2)]
        O = m.ps("mixed")
        WB = [m.ps(f"work{n}") for n in range(2)]
        T.append(S[2][:, 256:])
        probs = sb("probs", [P, 2, PACKED])
        negmax, rowsum, recip = (sb(n, [P, 2, 4]) for n in ("negmax", "rowsum", "recip"))
        pT = [sb(f"pT{n}", [P, PACKED], F32R) for n in "hl"]
        raw_in = [sem(f"raw_in{n}") for n in range(RAW_SLOTS)]
        raw_split = sem("raw_split")
        pool_step = sem("pool_step")
        work_full, work_hi, work_free = sem("work_full"), sem("work_hi"), sem("work_free")
        scored, min_done, exp_done, recip_done, scaled = (
            sem(n) for n in ("scored", "min", "exp", "recip", "scaled"))
        turned, pT_hi_done, pT_done = sem("turned"), sem("pT_hi"), sem("pT")
        mixed, mixed_hi, mixed_done = sem("mixed"), sem("mixed_hi"), sem("mixed_done")

        raw = sb("raw", [P, RAW_SLOTS, 512])
        wq = [sb(f"wq{n}", [P, GROUP, NC_, P], F32R) for n in "hl"]
        wkv = [sb(f"wkv{n}", [P, NC_, 2, P], F32R) for n in "hl"]
        wk, wv = ([a[:, :, n, :] for a in wkv] for n in range(2))
        wd = [sb(f"wd{n}", [P, GROUP, D], F32R) for n in "hl"]
        q = [sb(f"q{n}", [P, 2, GROUP, SEQ], F32R) for n in "hl"]
        k = [sb(f"k{n}", [P, NB, SEQ], F32R) for n in "hl"]
        v = [sb(f"v{n}", [P, NB, TB, P], F32R) for n in "hl"]
        ctxT = [sb(f"c{n}", [P, NB, GROUP, SEQ], F32R) for n in "hl"]
        x = [K.xh, K.xl]
        if kind == 2:
            square = sb("square", [P, 512])
            square_k = sb("square_k", [P, TB, P])
            sumsq, rms, qkw = sb("sumsq", [P, 4]), sb("rms", [P, 4]), sb("qkw", [P, 2])
            tab, pick = sb("tab", [3 * GROUP, SEQ], BF16), sb("pick", [3 * GROUP, GROUP, P], BF16)
            square_done, sumsq_done, mean_done, rms_done = (
                sem(n) for n in ("square", "sumsq", "mean", "rms"))
            qkw_in, pick_in, tab_in = sem("qkw_in"), sem("pick_in"), sem("tab_in")
            qkw_done = sem("qkw_done")
            raw_q = sb("raw_q", [P, GROUP, 512])
            raw_q_in, wq_hi, wq_split = sem("raw_q_in"), sem("wq_hi"), sem("wq_split")
        block = ctx.enter_context(nc.Block())

        def ends(i, b):
            at = isinstance(i, int)
            return at and i == 0 and b == 0, at and i == KV - 1 and b == 1

        OUT_TILES = ((), (0,), (1,), (2, 3))

        def uses(i, b, j):
            first, last = ends(i, b)
            out = [] if first else [f"D{t}" for t in OUT_TILES[j]]
            if last:
                return out
            if j == 0:
                return ["Q", "K"] if kind == 1 else ["Q", "QT", "KV0", "KV1"]
            if kind == 2:
                return ["Q"] + ["KT"] * (j == 1) + out + ["QT"]
            return ["Q"] + out + ["V"] * (j == 2)

        PROLOGUE = ["Q"] * 4 + ["K", "V"] if kind == 1 else ["Q", "QT"] * 4 + ["KV0", "KV1", "KT"]
        PRO = len(PROLOGUE)

        def start(i, b):
            return PRO if ends(i, b)[0] else (PRO + 4) * (2 * i + b) + PRO - 4

        def use(i, b, j, name):
            if isinstance(i, int) and i == -1:
                return [n for n, o in enumerate(PROLOGUE) if o == name][j if name in ("Q", "QT") else 0]
            return start(i, b) + sum(len(uses(i, b, jj)) for jj in range(j)) + uses(i, b, j).index(name)

        def work(i, b, j, name):
            return WB[use(i if isinstance(i, int) else 1, b, j, name) % 2]

        def before(i, b, j):
            return (i, b, j - 1) if j else (i, 0, 3) if b else (i - 1, 1, 3)

        def unit(i, b, j):
            return 8 * i + 4 * b + j

        STREAM = [0, 4, 1, 2, 5, 3] if kind == 1 else [4, 5]
        FIRST, PER = len(STREAM), len(STREAM) + GROUP

        def piece(g, n):
            if n < 6:
                return (sorted(STREAM).index(n) if isinstance(g, int) and g == 0
                        else FIRST + PER * (g - 1) + STREAM.index(n))
            return FIRST + PER * g + (n - 6 if isinstance(g, int) and g == KV - 1 else FIRST + n - 6)

        def stream(i):
            last = isinstance(i, int) and i == KV - 1
            out = [] if last else [(i + 1, n, FIRST + at) for at, n in enumerate(STREAM)]
            return out + [(i, n, FIRST + n - 6 + (0 if last else FIRST)) for n in range(6, PIECES)]

        def arrivals(i, place):
            return (PER // RAW_SLOTS) * i + place // RAW_SLOTS + 1

        def loop(eng, body):
            body(0)
            with eng.Fori(1, KV - 1) as i:
                body(i)
            body(KV - 1)

        @block.sync
        def _(sp):
            w = dram["w"]
            if kind == 2:
                sp.dma_start(qkw[:], dram["qkw"]).then_inc(qkw_in, 16)

            def load(i, g, n, place):
                if not (isinstance(i, int) and i == 0 and place < RAW_SLOTS):
                    sp.wait_ge(raw_split, PER * i + place - RAW_SLOTS + 1)
                sp.dma_start(raw[:, place % RAW_SLOTS, :],
                             w[bass.ds(PIECES * g + n, 1), :, :].rearrange("a p n -> p (a n)")
                             ).then_inc(raw_in[place % RAW_SLOTS], 16)

            def load_q(g):
                if not (isinstance(g, int) and g == 0):
                    sp.wait_ge(wq_split, g)
                sp.dma_start(raw_q[:], w[bass.ds(PIECES * g, GROUP), :, :].rearrange("a p n -> p a n")
                             ).then_inc(raw_q_in, 16)

            if kind == 2:
                load_q(0)
            for place, n in enumerate(sorted(STREAM)):
                load(0, 0, n, place)

            def body(i):
                if kind == 2 and not (isinstance(i, int) and i == KV - 1):
                    load_q(i + 1)
                for g, n, place in stream(i):
                    load(i, g, n, place)
            loop(sp, body)

        @block.gpsimd
        def _(pool):
            parts = [(wq, j) for j in range(4)] + [(wk, None), (wv, None)] + [(wd, j) for j in range(4)]

            def split(i, n, place):
                pool.wait_ge(raw_in[place % RAW_SLOTS], 16 * arrivals(i, place))
                pair, j = parts[n]
                hi, lo = (t[:, j] if j is not None else t for t in pair)
                if n >= 6:
                    hi, lo = (t.rearrange("p (c d) -> p c d", c=NC_) for t in (hi, lo))
                src = raw[:, place % RAW_SLOTS, :].rearrange("p (c d) -> p c d", c=NC_)
                zero = K.zero[:, 0:1].unsqueeze(2).to_broadcast([P, NC_, P])
                nc.gpsimd.tensor_tensor(hi, src, zero, ALU.add
                                        ).then_inc(pool_step, 1)
                pool.wait_ge(pool_step, PER * i + place + 1)
                nc.gpsimd.tensor_tensor(lo, src, hi.bitcast(F32), ALU.subtract).then_inc(raw_split, 1)

            def ran(i, b, j, name):
                pool.wait_ge(work_full, use(i, b, j, name) + 1)

            def scale(i, b, j):
                pool.wait_ge(recip_done, unit(i, b, j) + 1)
                for qi in ORDER:
                    pr = probs[:, j % 2, COL[qi]:COL[qi] + (qi + 1) * P]
                    nc.gpsimd.tensor_tensor(pr, pr, recip[:, j % 2, qi:qi + 1].to_broadcast([P, (qi + 1) * P]),
                                            ALU.mult).then_inc(scaled, 1)

            def root(n, s=slice(0, 4)):
                pool.wait_ge(mean_done, n + 1)
                nc.gpsimd.tensor_tensor(rms[:, s], sumsq[:, s], K.half[:, s], ALU.pow).then_inc(rms_done, 1)

            def load_tab(g):
                pool.dma_start(tab[:], dram["tab"][bass.ds(g, 1), :, :].rearrange("a r n -> r (a n)")
                               ).then_inc(tab_in, 16)

            def body(i):
                for b in range(NB):
                    last = ends(i, b)[1]
                    for j in range(GROUP):
                        scale(i, b, j)
                        if kind == 2 and not last:
                            root(6 + 12 * i + 6 * b + (j and j + 2))
                        if kind == 2 and not last and j == 0:
                            for n in range(2):
                                root(6 + 12 * i + 6 * b + 1 + n, slice(2 * n, 2 * n + 2))
                        if kind == 2 and b == 1 and j == 2 and not last:
                            pool.wait_ge(scored, 3 * unit(i, 1, 4))
                            load_tab(i + 1)
                        if kind == 2:
                            turn_of = {(0, 1): (4,), (0, 2): (5,), (0, 3): (6, 7), (1, 0): (8, 9)}.get((b, j), ())
                            for g, n, place in stream(i):
                                if n in turn_of:
                                    if n == 4:
                                        ran(i, 0, 0, "KV1")
                                    if n == 6 and not (isinstance(i, int) and i == 0):
                                        ran(i, 0, 3, "D3")
                                    split(i, n, place)
                        if kind == 1 and b == 0:
                            for g, n, place in stream(i):
                                at = {4: (0, 0, "K"), 5: (2, 2, "V")}.get(n)
                                if n < 4:
                                    at = (n, n, "Q")
                                if n < 6 and at[0] == j:
                                    ran(i, b, at[1], at[2])
                                    split(i, n, place)
                    if kind == 1 and b == 0:
                        if not (isinstance(i, int) and i == 0):
                            ran(i, 0, 3, "D3")
                        for g, n, place in stream(i):
                            if n >= 6:
                                split(i, n, place)

            if kind == 2:
                pool.dma_start(pick[:], dram["pick"]).then_inc(pick_in, 16)
                load_tab(0)
            for place, n in enumerate(sorted(STREAM)):
                split(0, n, place)
            if kind == 2:
                for n in range(4):
                    root(n)
                for n in range(2):
                    root(4 + n, slice(2 * n, 2 * n + 2))
            loop(pool, body)

        @block.tensor
        def _(pe):
            def bank(n):
                if not (isinstance(n, int) and n < 2):
                    pe.wait_ge(work_free, n - 1)

            def weights(g, n):
                pe.wait_ge(raw_split, piece(g, n) + 1)

            def project_q(i, b, j, g, nb):
                W = work(i, b, j, "Q")
                bank(use(i, b, j, "Q"))
                if kind == 1:
                    weights(g, j)
                    for c in range(NC_):
                        last = mm3(nc, W[:], [w[:, j, c, :] for w in wq],
                                   [a[:, c, nb * SEQ:(nb + 1) * SEQ] for a in x], c == 0, c == NC_ - 1)
                else:
                    pe.wait_ge(wq_split, g + 1)
                    t = nb * TB + j
                    for c in range(NC_):
                        last = mm3(nc, W[:].rearrange("p (h d) -> p h d", h=GROUP),
                                   [a[:, c, t * P:(t + 1) * P] for a in x],
                                   [w[:, :, c, :] for w in wq], c == 0, c == NC_ - 1)
                last.then_inc(work_full, 1)

            def project_tokens(w, i, b, j, name, g, nb, pc):
                W = work(i, b, j, name)
                bank(use(i, b, j, name))
                weights(g, pc)
                for t in range(TB):
                    for c in range(NC_):
                        s = slice((nb * TB + t) * P, (nb * TB + t + 1) * P)
                        last = mm3(nc, W[:, t * P:(t + 1) * P], [a[:, c, s] for a in x],
                                   [y[:, c, :] for y in w], c == 0, c == NC_ - 1)
                last.then_inc(work_full, 1)

            def project_k(i, b, j, g, nb):
                W = work(i, b, j, "K")
                bank(use(i, b, j, "K"))
                weights(g, 4)
                for c in range(NC_):
                    last = mm3(nc, W[:], [w[:, c, :] for w in wk],
                               [a[:, c, nb * SEQ:(nb + 1) * SEQ] for a in x], c == 0, c == NC_ - 1)
                last.then_inc(work_full, 1)

            def project_kv(i, b, j, g, nb, n):
                W = work(i, b, j, f"KV{n}")
                bank(use(i, b, j, f"KV{n}"))
                weights(g, 5)
                for t in range(2):
                    s = slice((nb * TB + 2 * n + t) * P, (nb * TB + 2 * n + t + 1) * P)
                    for c in range(NC_):
                        last = mm3(nc, W[:, 2 * t * P:2 * (t + 1) * P], [a[:, c, s] for a in x],
                                   [a[:, c].rearrange("p k d -> p (k d)") for a in wkv], c == 0, c == NC_ - 1)
                last.then_inc(work_full, 1)

            def turn(i, b, j, name):
                W = work(i, b, j, name)
                bank(use(i, b, j, name))
                pe.wait_ge(work_free, use(i, b, j, "Q") + 1 if name == "QT" else use(i, b, 0, "KV1") + 1)
                for h in range(4):
                    src = square[:, h * P:(h + 1) * P] if name == "QT" else square_k[:, h, :]
                    last = nc.tensor.transpose(W[:, h * P:(h + 1) * P], src, K.ident[:])
                last.then_inc(work_full, 1)

            def scores(i, b, j):
                u = unit(i, b, j)
                if j == 0:
                    pe.wait_ge(work_free, start(i, b))
                    if kind == 2:
                        pe.wait_ge(tab_in, 16 * (i + 1))
                        if ends(i, b)[0]:
                            pe.wait_ge(pick_in, 16)
                for n, group in enumerate(((3,), (2, 0), (1,))):
                    if not (ends(i, b)[0] and j == 0):
                        pe.wait_ge(exp_done, 4 * (u - 1) + (1, 3, 4)[n])
                    if n == 2 and not (ends(i, b)[0] and j < 2):
                        pe.wait_ge(pT_done, 3 * (u - 1 if j else u))
                    for qi in group:
                        keys = (qi + 1) * P
                        off = COL[qi] - 512 * n
                        out = S[n][:, off:off + keys]
                        mm3(nc, out, [a[:, b, j, qi * P:(qi + 1) * P] for a in q],
                            [a[:, b, 0:keys] for a in k], True, False)
                        if kind == 2:
                            nc.tensor.matmul(out, pick[:, j, :], tab[:, SEQ - keys:SEQ],
                                             start=False, stop=False)
                        last = nc.tensor.matmul(out[:, qi * P:keys], K.ident_r[:], K.mask_r[:],
                                                start=False, stop=True)
                    last.then_inc(scored, 1)

            def turn_probs(i, b, j):
                u = unit(i, b, j)
                pe.wait_ge(scaled, 4 * (u + 1))
                for n, group in enumerate(((3,), (2, 0), (1,))):
                    if not (ends(i, b)[0] and j == 0):
                        pe.wait_ge(pT_done, 3 * (u - 1) + n + 1)
                    if n == 2 and j < 3:
                        pe.wait_ge(exp_done, 4 * (u + 2))
                    for back in group:
                        kj = 3 - back
                        off = COL[back] - 512 * n
                        for qi in range(kj, TB):
                            last = nc.tensor.transpose(
                                T[n][:, off + (qi - kj) * P:off + (qi - kj + 1) * P],
                                probs[:, j % 2, COL[qi] + kj * P:COL[qi] + (kj + 1) * P], K.ident[:])
                    last.then_inc(turned, 1)

            def mix(i, b, j):
                u = unit(i, b, j)
                if not (ends(i, b)[0] and j == 0):
                    pe.wait_ge(mixed_done, u)
                for kj, bank_n in ((0, 0), (1, 1), (3, 1), (2, 2)):
                    pe.wait_ge(pT_done, 3 * u + bank_n + 1)
                    cols = slice(COL[3 - kj], COL[3 - kj] + (TB - kj) * P)
                    last = mm3(nc, O[:, kj * P:], [a[:, b, kj, :] for a in v], [a[:, cols] for a in pT],
                               kj == 0, kj == 2)
                last.then_inc(mixed, 1)

            def project_out(i, b, j, t):
                pi, pb = (i, 0) if b == 1 else (i - 1, 1)
                W = work(i, b, j, f"D{t}")
                bank(use(i, b, j, f"D{t}"))
                if t == 0:
                    weights(pi, PIECES - 1)
                    pe.wait_ge(mixed_done, unit(pi, pb, 4))
                for h in range(GROUP):
                    last = mm3(nc, W[:], [a[:, pb, h, t * P:(t + 1) * P] for a in ctxT],
                               [w[:, h, :] for w in wd], h == 0, h == GROUP - 1)
                last.then_inc(work_full, 1)

            def body(i):
                for b in range(NB):
                    first, last = ends(i, b)
                    g, nb = (i, 1) if b == 0 else (i + 1, 0)
                    scores(i, b, 0)
                    for j in range(GROUP):
                        if not last:
                            project_q(i, b, j, g, nb)
                        if j < 3:
                            scores(i, b, j + 1)
                        if not (first and j == 0):
                            mix(*before(i, b, j))
                        turn_probs(i, b, j)
                        if kind == 2 and j == 1 and not last:
                            turn(i, b, j, "KT")
                        if not first:
                            for t in OUT_TILES[j]:
                                project_out(i, b, j, t)
                        if kind == 2 and not last:
                            turn(i, b, j, "QT")
                            for n in range(2 if j == 0 else 0):
                                project_kv(i, b, j, g, nb, n)
                        if kind == 1 and j == 0 and not last:
                            project_k(i, b, j, g, nb)
                        if kind == 1 and j == 2 and not last:
                            project_tokens(wv, i, b, j, "V", g, nb, 5)

            for j in range(GROUP):
                project_q(-1, 0, j, 0, 0)
                if kind == 2:
                    turn(-1, 0, j, "QT")
            if kind == 2:
                for n in range(2):
                    project_kv(-1, 0, 0, 0, 0, n)
                turn(-1, 0, 0, "KT")
            else:
                project_k(-1, 0, 0, 0, 0)
                project_tokens(wv, -1, 0, 0, "V", 0, 0, 5)
            loop(pe, body)
            mix(KV - 1, 1, 3)
            weights(KV - 1, PIECES - 1)
            pe.wait_ge(mixed_done, unit(KV - 1, 1, 4))
            for j in range(TB):
                dst = (S + T)[j]
                for h in range(GROUP):
                    last = mm3(nc, dst[:], [a[:, 1, h, j * P:(j + 1) * P] for a in ctxT],
                               [w[:, h, :] for w in wd], h == 0, h == GROUP - 1)
                last.then_inc(work_full, 1)

        FINAL = (PRO + 4) * (2 * KV - 1) + PRO - 4 + 4

        @block.scalar
        def _(act):
            def high(i, b, j, name, dst, scale):
                act.wait_ge(work_full, use(i, b, j, name) + 1)
                src = work(i, b, j, name)[:]
                if len(dst.shape) == 3:
                    src = src.rearrange("p (a b) -> p a b", a=4)
                nc.scalar.activation(dst, src, ACT.Copy, scale=scale).then_inc(work_hi, 1)

            def squares(i, b, j, name):
                act.wait_ge(work_full, use(i, b, j, name) + 1)
                nc.scalar.activation(square[:], work(i, b, j, name)[:], ACT.Square).then_inc(square_done, 1)

            def split_q(g):
                act.wait_ge(raw_q_in, 16 * (g + 1))
                nc.scalar.activation(wq[0][:].rearrange("p j c n -> p (j c n)"),
                                     raw_q[:].rearrange("p j n -> p (j n)"), ACT.Copy).then_inc(wq_hi, 1)

            def exps(i, b, j):
                u = unit(i, b, j)
                for qi, minima in zip(ORDER, (1, 3, 3, 4)):
                    act.wait_ge(min_done, 4 * u + minima)
                    nc.scalar.activation(probs[:, j % 2, COL[qi]:COL[qi] + (qi + 1) * P],
                                         S[SLOT[qi][0]][:, SLOT[qi][1]:SLOT[qi][1] + (qi + 1) * P],
                                         ACT.Exp, bias=negmax[:, j % 2, qi:qi + 1], scale=-1.0,
                                         accum_out=rowsum[:, j % 2, qi:qi + 1]).then_inc(exp_done, 1)

            def queries(i, b, j, nb):
                if kind == 1:
                    high(i, b, j, "Q", q[0][:, nb, j, :], NEG)
                else:
                    squares(i, b, j, "Q")

            def keys_values(i, b, j, nb, n):
                src = work(i, b, j, f"KV{n}")[:].rearrange("p (t k d) -> p t k d", t=2, k=2)
                act.wait_ge(work_full, use(i, b, j, f"KV{n}") + 1)
                nc.scalar.activation(square_k[:, 2 * n:2 * n + 2, :], src[:, :, 0, :], ACT.Square
                                     ).then_inc(square_done, 1)
                nc.scalar.activation(v[0][:, nb, 2 * n:2 * n + 2, :], src[:, :, 1, :], ACT.Copy
                                     ).then_inc(work_hi, 1)

            def keys(i, b, j, nb):
                high(i, b, j, "K", k[0][:, nb, :], 1.0)

            def values(i, b, j, nb):
                high(i, b, j, "V", v[0][:, nb, :, :], 1.0)

            def turned_q(i, b, j, nb):
                high(i, b, j, "QT", q[0][:, nb, :, j * P:(j + 1) * P], qkw[:, 0:1])

            def turned_k(i, b, j, nb):
                high(i, b, j, "KT", k[0][:, nb, :], qkw[:, 1:2])

            def take_mixed(i, b, j):
                act.wait_ge(mixed, unit(i, b, j) + 1)
                nc.scalar.activation(ctxT[0][:, b, j, :], O[:], ACT.Copy).then_inc(mixed_hi, 1)

            def body(i):
                for b in range(NB):
                    last = ends(i, b)[1]
                    nb = 1 - b
                    exps(i, b, 0)
                    for j in range(GROUP):
                        u = unit(i, b, j)
                        if not last:
                            queries(i, b, j, nb)
                        if j < 3:
                            exps(i, b, j + 1)
                        if not (ends(i, b)[0] and j == 0):
                            take_mixed(*before(i, b, j))
                        for n in range(3):
                            act.wait_ge(turned, 3 * u + n + 1)
                            s = slice(512 * n, min(512 * (n + 1), PACKED))
                            nc.scalar.activation(pT[0][:, s], T[n][:, 0:s.stop - s.start], ACT.Copy
                                                 ).then_inc(pT_hi_done, 1)
                        if kind == 2 and b == 0 and j == 3 and not (isinstance(i, int) and i == KV - 1):
                            split_q(i + 1)
                        if kind == 2 and not last:
                            if j == 1:
                                turned_k(i, b, j, nb)
                            turned_q(i, b, j, nb)
                            for n in range(2 if j == 0 else 0):
                                keys_values(i, b, j, nb, n)
                        if kind == 1 and j == 0 and not last:
                            keys(i, b, j, nb)
                        if kind == 1 and j == 2 and not last:
                            values(i, b, j, nb)

            if kind == 2:
                split_q(0)
                act.wait_ge(qkw_done, 1)
            for j in range(GROUP):
                queries(-1, 0, j, 0)
                if kind == 2:
                    turned_q(-1, 0, j, 0)
            if kind == 2:
                for n in range(2):
                    keys_values(-1, 0, 0, 0, n)
                turned_k(-1, 0, 0, 0)
            else:
                keys(-1, 0, 0, 0)
                values(-1, 0, 0, 0)
            loop(act, body)
            take_mixed(KV - 1, 1, 3)

        @block.vector
        def _(dve):
            def hi_count(i, b, j, name):
                count = 0
                mine = [nm for nm in PROLOGUE if takes_hi(nm)]
                if isinstance(i, int) and i == -1:
                    at = use(i, b, j, name)
                    return sum(takes_hi(nm) for nm in PROLOGUE[:at + 1])
                per = len(mine)
                at = sum(takes_hi(nm) for jj in range(j) for nm in uses(i, b, jj))
                names = uses(i, b, j)
                at += sum(takes_hi(nm) for nm in names[:names.index(name) + 1])
                return per + per * (2 * i + b) + at

            def takes_hi(name):
                return name in (("Q", "K", "V") if kind == 1 else ("QT", "KT", "KV0", "KV1"))

            def low(i, b, j, name, hi, lo, scale):
                dve.wait_ge(work_hi, hi_count(i, b, j, name))
                src = work(i, b, j, name)[:]
                if len(hi.shape) == 3:
                    src = src.rearrange("p (a b) -> p a b", a=4)
                if scale is None:
                    ins = nc.vector.tensor_tensor(lo, src, hi.bitcast(F32), ALU.subtract)
                else:
                    ins = nc.vector.scalar_tensor_tensor(out=lo, in0=src, scalar=scale, in1=hi.bitcast(F32),
                                                         op0=ALU.mult, op1=ALU.subtract)
                ins.then_inc(work_free, 1)

            def split_q(g):
                four = "p j c n -> p (j c n)"
                dve.wait_ge(wq_hi, g + 1)
                nc.vector.tensor_tensor(wq[1][:].rearrange(four), raw_q[:].rearrange("p j n -> p (j n)"),
                                        wq[0][:].rearrange(four).bitcast(F32), ALU.subtract).then_inc(wq_split, 1)

            def mean(n):
                four = "p (h d) -> p h d"
                dve.wait_ge(square_done, n + 1)
                nc.vector.reduce_sum(sumsq[:], square[:].rearrange(four, h=4), AX_X
                                     ).then_inc(sumsq_done, 1)
                dve.wait_ge(sumsq_done, n + 1)
                nc.vector.tensor_scalar(sumsq[:], sumsq[:], 1.0 / P, RMS_EPS, ALU.mult, ALU.add
                                        ).then_inc(mean_done, 1)

            def norm(i, b, j, name, n):
                four = "p (h d) -> p h d"
                dve.wait_ge(rms_done, n + 1)
                nc.vector.tensor_tensor(square[:].rearrange(four, h=4), work(i, b, j, name)[:].rearrange(four, h=4),
                                        rms[:].unsqueeze(2).to_broadcast([P, 4, P]),
                                        ALU.mult).then_inc(work_free, 1)

            def queries(i, b, j, nb, n):
                if kind == 1:
                    low(i, b, j, "Q", q[0][:, nb, j, :], q[1][:, nb, j, :], NEG)
                else:
                    mean(n)

            def keys(i, b, j, nb):
                low(i, b, j, "K", k[0][:, nb, :], k[1][:, nb, :], None)

            def keys_values(i, b, j, nb, n, root):
                src = work(i, b, j, f"KV{n}")[:].rearrange("p (t k d) -> p t k d", t=2, k=2)
                s = slice(2 * n, 2 * n + 2)
                dve.wait_ge(square_done, root + 1)
                nc.vector.reduce_sum(sumsq[:, s], square_k[:, s, :], AX_X).then_inc(sumsq_done, 1)
                dve.wait_ge(sumsq_done, root + 1)
                nc.vector.tensor_scalar(sumsq[:, s], sumsq[:, s], 1.0 / P, RMS_EPS, ALU.mult, ALU.add
                                        ).then_inc(mean_done, 1)
                dve.wait_ge(work_hi, hi_count(i, b, j, f"KV{n}"))
                nc.vector.tensor_tensor(v[1][:, nb, s, :], src[:, :, 1, :], v[0][:, nb, s, :].bitcast(F32),
                                        ALU.subtract)
                dve.wait_ge(rms_done, root + 1)
                nc.vector.tensor_tensor(square_k[:, s, :], src[:, :, 0, :],
                                        rms[:, s].unsqueeze(2).to_broadcast([P, 2, P]), ALU.mult
                                        ).then_inc(work_free, 1)

            def values(i, b, j, nb):
                low(i, b, j, "V", v[0][:, nb, :, :], v[1][:, nb, :, :], None)

            def turned_q(i, b, j, nb):
                s = slice(j * P, (j + 1) * P)
                low(i, b, j, "QT", q[0][:, nb, :, s], q[1][:, nb, :, s], qkw[:, 0:1])

            def turned_k(i, b, j, nb):
                low(i, b, j, "KT", k[0][:, nb, :], k[1][:, nb, :], qkw[:, 1:2])

            def minima(i, b, j):
                u = unit(i, b, j)
                for qi, need in zip(ORDER, (1, 2, 2, 3)):
                    dve.wait_ge(scored, 3 * u + need)
                    nc.vector.tensor_reduce(negmax[:, j % 2, qi:qi + 1],
                                            S[SLOT[qi][0]][:, SLOT[qi][1]:SLOT[qi][1] + (qi + 1) * P],
                                            AX_X, ALU.min).then_inc(min_done, 1)

            def reciprocals(i, b, j):
                dve.wait_ge(exp_done, 4 * unit(i, b, j) + 4)
                nc.vector.reciprocal(recip[:, j % 2, :], rowsum[:, j % 2, :]).then_inc(recip_done, 1)

            def body(i):
                for b in range(NB):
                    first, last = ends(i, b)
                    nb = 1 - b
                    pb = 1 - b
                    turns = 6 + 12 * i + 6 * b
                    minima(i, b, 0)
                    reciprocals(i, b, 0)
                    for j in range(GROUP):
                        u = unit(i, b, j)
                        if not last:
                            queries(i, b, j, nb, turns + (j and j + 2))
                        if j < 3:
                            minima(i, b, j + 1)
                        if kind == 2 and not last:
                            norm(i, b, j, "Q", turns + (j and j + 2))

                        if not (first and j == 0):
                            take_mixed(*before(i, b, j))
                        if j < 3:
                            reciprocals(i, b, j + 1)
                        for n in range(3):
                            dve.wait_ge(pT_hi_done, 3 * u + n + 1)
                            s = slice(512 * n, min(512 * (n + 1), PACKED))
                            nc.vector.tensor_tensor(pT[1][:, s], T[n][:, 0:s.stop - s.start],
                                                    pT[0][:, s].bitcast(F32), ALU.subtract
                                                    ).then_inc(pT_done, 1)
                        if kind == 2 and j == 1 and not last:
                            turned_k(i, b, j, nb)
                        for t in () if first else OUT_TILES[j]:
                            dve.wait_ge(work_full, use(i, b, j, f"D{t}") + 1)
                            xt = K.xs[:, pb * TB + t, :]
                            nc.vector.tensor_tensor(xt, xt, work(i, b, j, f"D{t}")[:], ALU.add
                                                    ).then_inc(work_free, 1)
                        if kind == 2 and b == 0 and j == 3 and not (isinstance(i, int) and i == KV - 1):
                            split_q(i + 1)
                        if kind == 2 and not last:
                            turned_q(i, b, j, nb)
                            for n in range(2 if j == 0 else 0):
                                keys_values(i, b, j, nb, n, turns + 1 + n)
                        if kind == 1 and j == 0 and not last:
                            keys(i, b, j, nb)
                        if kind == 1 and j == 2 and not last:
                            values(i, b, j, nb)

            def take_mixed(i, b, j):
                dve.wait_ge(mixed_hi, unit(i, b, j) + 1)
                nc.vector.tensor_tensor(ctxT[1][:, b, j, :], O[:], ctxT[0][:, b, j, :].bitcast(F32),
                                        ALU.subtract).then_inc(mixed_done, 1)

            if kind == 2:
                dve.wait_ge(qkw_in, 16)
                nc.vector.tensor_scalar(qkw[:, 0:1], qkw[:, 0:1], NEG, None, ALU.mult).then_inc(qkw_done, 1)
                dve.wait_ge(qkw_done, 1)
                split_q(0)
            for j in range(GROUP):
                queries(-1, 0, j, 0, j)
                if kind == 2:
                    norm(-1, 0, j, "Q", j)
                    turned_q(-1, 0, j, 0)
            if kind == 2:
                for n in range(2):
                    keys_values(-1, 0, 0, 0, n, 4 + n)
                turned_k(-1, 0, 0, 0)
            else:
                keys(-1, 0, 0, 0)
                values(-1, 0, 0, 0)
            loop(dve, body)
            take_mixed(KV - 1, 1, 3)
            for j in range(TB):
                dve.wait_ge(work_full, FINAL + j + 1)
                t = TB + j
                nc.vector.tensor_tensor(K.xs[:, t, :], K.xs[:, t, :], (S + T)[j][:], ALU.add
                                        ).then_inc(work_free, 1)


SINK_ITERS = 50
TAU = 0.1
STREAMS = 4
RMS1_EPS = 1.1920929e-07


def streams_stage(nc, K, dram, pre):
    N, C = STREAMS, P
    NL = N * N + 2 * N
    HALF = NT // 2
    with ExitStack() as ctx:
        m = Memory(nc, ctx, pre)
        sb, sem = m.sb, m.sem
        w_raw, w = sb("w_raw", [P, NC_, NL]), [sb(f"w{n}", [P, NC_, NL], F32R) for n in "hl"]
        wb_raw, wb = sb("wb_raw", [P, C]), [sb(f"wb{n}", [P, C], F32R) for n in "hl"]
        base = sb("base", [P, NL])
        gate = sb("gate", [P, 4])
        square = sb("square", [P, 2, D])
        ms, rms = sb("ms", [P, NT]), sb("rms", [P, NT])
        logit = sb("logit", [P, NT, NL])
        Z = sb("Z", [P, NT, N, N])
        diff, expd = sb("diff", [P, NT, N, N]), sb("expd", [P, NT, N, N])
        top, total, logs = (sb(n, [P, NT, N]) for n in ("top", "total", "logs"))
        u, v = sb("u", [P, NT, N]), sb("v", [P, NT, N])
        H = sb("H", [P, NT, N, N])
        soft = sb("soft", [P, NT, 2, N])
        sm, ss = sb("sm", [P, NT, 2]), sb("ss", [P, NT, 2])
        eye = sb("eye", [P, N, N])
        xin = sb("xin", [P, 2, C])
        xT = [sb(f"xT{n}", [P, NT, P], F32R) for n in "hl"]
        acc = sb("acc", [P, 2, D])
        lg = m.ps("logits")
        tb = [m.ps(f"turned{n}") for n in range(2)]
        yb = [m.ps(f"branch{n}") for n in range(2)]
        in_w, in_wb, in_base, in_gate = sem("in_w"), sem("in_wb"), sem("in_base"), sem("in_gate")
        pool_step, w_split, eye_made = sem("pool_step"), sem("w_split"), sem("eye_made")
        ms_done, rms_done, logits, ready = sem("ms_done"), sem("rms_done"), sem("logits"), sem("ready")
        d0, d1 = sem("dve_set0"), sem("dve_set1")
        exp_done, log_done = [sem("exp0"), sem("exp1")], [sem("log0"), sem("log1")]
        small, small_exp = sem("small"), sem("small_exp")
        xin_done, xturned, x_hi, x_lo = sem("xin"), sem("xturned"), sem("x_hi"), sem("x_lo")
        branch, out_step = sem("branch"), sem("out_step")
        chain = sem("chain")
        block = ctx.enter_context(nc.Block())
        x = [K.xh, K.xl]

        @block.sync
        def _(sp):
            sp.dma_start(w_raw[:], dram["s_w"]).then_inc(in_w, 16)
            sp.dma_start(wb_raw[:], dram["s_wb"]).then_inc(in_wb, 16)
            sp.dma_start(base[:], dram["s_base"]).then_inc(in_base, 16)
            sp.dma_start(gate[:, 0:1], dram["s_gate"]).then_inc(in_gate, 16)

        @block.gpsimd
        def _(pool):
            step = Chain(pool, pool_step)
            step(nc.gpsimd.memset(eye[:], 0.0))
            for n in range(N):
                last = nc.gpsimd.memset(eye[:, n, n:n + 1], 1.0)
            last.then_inc(eye_made, 1)
            pool.wait_ge(in_w, 16)
            step(nc.gpsimd.tensor_copy(w[0][:], w_raw[:]))
            nc.gpsimd.tensor_tensor(w[1][:], w_raw[:], w[0][:].bitcast(F32), ALU.subtract).then_inc(w_split, 1)
            pool.wait_ge(in_wb, 16)
            step(nc.gpsimd.tensor_copy(wb[0][:], wb_raw[:]))
            nc.gpsimd.tensor_tensor(wb[1][:], wb_raw[:], wb[0][:].bitcast(F32), ALU.subtract).then_inc(w_split, 1)
            pool.wait_ge(ms_done, NT + 1)
            nc.gpsimd.tensor_tensor(rms[:], ms[:], K.half[:], ALU.pow).then_inc(rms_done, 1)

        @block.tensor
        def _(pe):
            pe.wait_ge(w_split, 1)
            for t in range(NT):
                for c in range(NC_):
                    last = mm3(nc, lg[:, t * NL:(t + 1) * NL], [a[:, c, t * P:(t + 1) * P] for a in x],
                               [a[:, c, :] for a in w], c == 0, c == NC_ - 1)
            last.then_inc(logits, 1)
            pe.wait_ge(w_split, 2)
            for t in range(NT):
                pe.wait_ge(xin_done, t + 1)
                if t >= 2:
                    pe.wait_ge(x_lo, t - 1)
                nc.tensor.transpose(tb[t % 2][:, 0:P], xin[:, t % 2, :], K.ident[:]).then_inc(xturned, 1)
            for t in range(NT):
                pe.wait_ge(x_lo, t + 1)
                if t >= 2:
                    pe.wait_ge(out_step, (N + 1) * (t - 1))
                mm3(nc, yb[t % 2][:, 0:C], [a[:, t, :] for a in xT], [a[:] for a in wb], True, True
                    ).then_inc(branch, 1)

        @block.scalar
        def _(act):
            act.wait_ge(in_gate, 16)
            nc.scalar.activation(gate[:, 1:2], gate[:, 0:1], ACT.Exp, scale=-1.0).then_inc(small_exp, 1)
            act.wait_ge(small, 1)
            nc.scalar.activation(soft[:], soft[:], ACT.Exp).then_inc(small_exp, 1)

            def step(n, k):
                s = slice(n * HALF, (n + 1) * HALF)
                act.wait_ge(d[n], 5 * k + 3)
                nc.scalar.activation(expd[:, s], diff[:, s], ACT.Exp).then_inc(exp_done[n], 1)
                return s

            def log(n, k):
                s = slice(n * HALF, (n + 1) * HALF)
                act.wait_ge(d[n], 5 * k + 4)
                nc.scalar.activation(logs[:, s], total[:, s], ACT.Ln).then_inc(log_done[n], 1)
            d = [d0, d1]
            for t in range(NT):
                act.wait_ge(xturned, t + 1)
                nc.scalar.activation(xT[0][:, t, :], tb[t % 2][:, 0:P], ACT.Copy).then_inc(x_hi, 1)
            nc.scalar.preload_act_table_set("natural_log_exp_and_others")
            with act.Fori(0, SINK_ITERS) as i:
                for way in range(2):
                    for n in range(2):
                        step(n, 2 * i + way)
                    for n in range(2):
                        log(n, 2 * i + way)
            for n in range(2):
                s = slice(n * HALF, (n + 1) * HALF)
                act.wait_ge(d[n], 10 * SINK_ITERS + 2)
                nc.scalar.activation(H[:, s], diff[:, s], ACT.Exp).then_inc(exp_done[n], 1)

        @block.vector
        def _(dve):
            step = Chain(dve, chain)
            for t in range(NT):
                if t >= 2:
                    dve.wait_ge(ms_done, t - 1)
                nc.vector.tensor_tensor_reduce(out=square[:, t % 2, :], in0=K.xs[:, t, :], in1=K.xs[:, t, :],
                                               scale=1.0, scalar=0.0, op0=ALU.mult, op1=ALU.add,
                                               accum_out=ms[:, t:t + 1]).then_inc(ms_done, 1)
            dve.wait_ge(ms_done, NT)
            nc.vector.tensor_scalar(ms[:], ms[:], 1.0 / D, RMS1_EPS, ALU.mult, ALU.add).then_inc(ms_done, 1)
            dve.wait_ge(logits, 1)
            dve.wait_ge(rms_done, 1)
            dve.wait_ge(in_base, 16)
            lv = lg[:, 0:NT * NL].rearrange("p (t n) -> p t n", t=NT)
            step(nc.vector.tensor_tensor(logit[:], lv, rms[:].unsqueeze(2).to_broadcast([P, NT, NL]), ALU.mult))
            step(nc.vector.tensor_tensor(logit[:], logit[:], base[:].unsqueeze(1).to_broadcast([P, NT, NL]),
                                         ALU.add))
            Zl = logit[:, :, 0:N * N].rearrange("p t (i j) -> p t i j", i=N)
            nc.vector.tensor_scalar(Z[:], Zl, 1.0 / TAU, None, ALU.mult)
            nc.vector.memset(v[:], 0.0)
            two = logit[:, :, N * N:].rearrange("p t (a n) -> p t a n", a=2)
            step(nc.vector.tensor_reduce(sm[:], two, AX_X, ALU.max))
            nc.vector.tensor_tensor(soft[:], two, sm[:].unsqueeze(3).to_broadcast([P, NT, 2, N]), ALU.subtract
                                    ).then_inc(small, 1)
            dve.wait_ge(small_exp, 2)
            step(nc.vector.reduce_sum(ss[:], soft[:], AX_X))
            step(nc.vector.reciprocal(ss[:], ss[:]))
            step(nc.vector.tensor_tensor(soft[:], soft[:], ss[:].unsqueeze(3).to_broadcast([P, NT, 2, N]),
                                         ALU.mult))
            for t in range(NT):
                if t >= 2:
                    dve.wait_ge(xturned, t - 1)
                o = xin[:, t % 2, :]
                step(nc.vector.tensor_scalar(o, K.xs[:, t, 0:C], soft[:, t, 0, 0:1], None, ALU.mult))
                for n in range(1, N):
                    ins = nc.vector.scalar_tensor_tensor(out=o, in0=K.xs[:, t, n * C:(n + 1) * C],
                                                         scalar=soft[:, t, 0, n:n + 1], in1=o,
                                                         op0=ALU.mult, op1=ALU.add)
                    if n < N - 1:
                        step(ins)
                ins.then_inc(xin_done, 1)
                if t >= 1:
                    dve.wait_ge(x_hi, t)
                    nc.vector.tensor_tensor(xT[1][:, t - 1, :], tb[(t - 1) % 2][:, 0:P],
                                            xT[0][:, t - 1, :].bitcast(F32), ALU.subtract).then_inc(x_lo, 1)
            dve.wait_ge(x_hi, NT)
            nc.vector.tensor_tensor(xT[1][:, NT - 1, :], tb[(NT - 1) % 2][:, 0:P],
                                    xT[0][:, NT - 1, :].bitcast(F32), ALU.subtract).then_inc(x_lo, 1)

            d = [d0, d1]

            def views(n, way):
                s = slice(n * HALF, (n + 1) * HALF)
                order = "p t i j -> p t i j" if way == 0 else "p t i j -> p t j i"
                return s, [a[:, s].rearrange(order) for a in (Z, diff, expd)]

            def begin(n, way, k):
                s, (z, df, _) = views(n, way)
                other = (v if way == 0 else u)[:, s].unsqueeze(2).to_broadcast([P, HALF, N, N])
                if not (isinstance(k, int) and k == 0):
                    dve.wait_ge(d[n], 5 * k)
                nc.vector.tensor_tensor(df, z, other, ALU.add).then_inc(d[n], 1)
                dve.wait_ge(d[n], 5 * k + 1)
                nc.vector.tensor_reduce(top[:, s], df, AX_X, ALU.max).then_inc(d[n], 1)
                dve.wait_ge(d[n], 5 * k + 2)
                nc.vector.tensor_tensor(df, df, top[:, s].unsqueeze(3).to_broadcast([P, HALF, N, N]),
                                        ALU.subtract).then_inc(d[n], 1)

            def sums(n, way, k):
                s, (_, _, e) = views(n, way)
                dve.wait_ge(exp_done[n], k + 1)
                nc.vector.tensor_reduce(total[:, s], e, AX_X, ALU.add).then_inc(d[n], 1)

            def end(n, way, k):
                s = slice(n * HALF, (n + 1) * HALF)
                dve.wait_ge(log_done[n], k + 1)
                nc.vector.scalar_tensor_tensor(out=(u if way == 0 else v)[:, s], in0=top[:, s], scalar=-1.0,
                                               in1=logs[:, s], op0=ALU.mult, op1=ALU.subtract
                                               ).then_inc(d[n], 1)

            step(nc.vector.memset(u[:], 0.0))
            with dve.Fori(0, SINK_ITERS) as i:
                for way in range(2):
                    k = 2 * i + way
                    for n in range(2):
                        begin(n, way, k)
                    for n in range(2):
                        sums(n, way, k)
                    for n in range(2):
                        end(n, way, k)
            for n in range(2):
                s = slice(n * HALF, (n + 1) * HALF)
                base_n = 10 * SINK_ITERS
                dve.wait_ge(d[n], base_n)
                nc.vector.tensor_tensor(diff[:, s], Z[:, s], u[:, s].unsqueeze(3).to_broadcast([P, HALF, N, N]),
                                        ALU.add).then_inc(d[n], 1)
                dve.wait_ge(d[n], base_n + 1)
                nc.vector.tensor_tensor(diff[:, s], diff[:, s],
                                        v[:, s].unsqueeze(2).to_broadcast([P, HALF, N, N]), ALU.add
                                        ).then_inc(d[n], 1)
            step(nc.vector.tensor_scalar(gate[:, 1:2], gate[:, 1:2], 1.0, None, ALU.add))
            step(nc.vector.reciprocal(gate[:, 2:3], gate[:, 1:2]))
            step(nc.vector.tensor_scalar(gate[:, 3:4], gate[:, 2:3], -1.0, 2.0, ALU.mult, ALU.add))
            dve.wait_ge(eye_made, 1)
            step(nc.vector.tensor_scalar(eye[:], eye[:], gate[:, 3:4], None, ALU.mult))
            for n in range(2):
                dve.wait_ge(exp_done[n], 2 * SINK_ITERS + 1)
            step(nc.vector.tensor_scalar(H[:], H[:], gate[:, 2:3], None, ALU.mult))
            step(nc.vector.tensor_tensor(H[:], H[:], eye[:].unsqueeze(1).to_broadcast([P, NT, N, N]), ALU.add))
            for t in range(NT):
                a = acc[:, t % 2, :]
                dve.wait_ge(branch, t + 1)
                count = [(N + 1) * t]

                def link(ins):
                    count[0] += 1
                    ins.then_inc(out_step, 1)
                    dve.wait_ge(out_step, count[0])
                for n in range(N + 1):
                    for i in range(N):
                        o = a[:, i * C:(i + 1) * C]
                        if n == 0:
                            ins = nc.vector.tensor_scalar(o, yb[t % 2][:, 0:C], soft[:, t, 1, i:i + 1], None,
                                                          ALU.mult)
                        else:
                            src = K.xs[:, t, (n - 1) * C:n * C]
                            ins = nc.vector.scalar_tensor_tensor(out=o, in0=src, scalar=H[:, t, i, n - 1:n],
                                                                 in1=o, op0=ALU.mult, op1=ALU.add)
                    link(ins)
                step(nc.vector.tensor_copy(K.xs[:, t, :], a))


BOT, RDIM, NSLOT, TOPK, VB = 64, 48, 128, 8, 32
TAU_LOW, TAU_HIGH, EARLY_EXIT = 0.5, 2.0, 0.05
HIDDEN = 3.0e38


def slots_stage(nc, K, dram, pre):
    with ExitStack() as ctx:
        m = Memory(nc, ctx, pre)
        sb, sem = m.sb, m.sem
        names = {"wq": [P, NC_, BOT], "wr": [RDIM, BOT], "wrT": [BOT, RDIM], "keysT": [BOT, NSLOT],
                 "valuesT": [P, NC_, NSLOT], "wvdT": [P, NC_, VB], "wvuT": [VB, D], "wu1": [P, NC_, P],
                 "wu2": [P, 1], "bu1": [P, 1], "scalars": [P, 3], "log_rel": [P, NSLOT]}
        W = {n: sb(n, s) for n, s in names.items()}
        loaded = {n: sem(f"in_{n}") for n in names}
        wq = [sb(f"wq{n}", [P, NC_, P], F32R) for n in "hl"]
        wu = [sb(f"wu{n}", [P, NC_, P], F32R) for n in "hl"]
        rkT, avT = sb("rkT", [RDIM, NSLOT]), sb("avT", [VB, NSLOT])
        router = sb("router", [BOT, 2 * NSLOT])
        slot_out = sb("slot_out", [NSLOT, D])
        query = sb("query", [BOT, TOK])
        act_u = sb("act_u", [P, TOK])
        stats, mv = sb("stats", [P, NT, 6]), sb("mv", [P, NT, 2])
        logv, logsum, mean = sb("logv", [P, NT]), sb("logsum", [P, 1]), sb("mean", [P, 1])
        ones = sb("ones", [P, P])
        learned, gate, live = sb("learned", [P, NT]), sb("gate", [P, NT]), sb("live", [P, NT])
        R, R2, A = (sb(n, [P, 2, NSLOT]) for n in ("R", "R2", "A"))
        best = sb("best", [P, 2, 8])
        chosen, off = sb("chosen", [P, 2, NSLOT]), sb("off", [P, 2, NSLOT])
        least, total, factor = sb("least", [P, NT]), sb("total", [P, NT]), sb("factor", [P, NT])
        E, ET = sb("E", [P, 2, NSLOT]), sb("ET", [P, 2, P])
        pre_bank, u_bank, l_bank = m.ps("prepare_bank"), m.ps("uncertain_bank"), m.ps("learned_bank")
        s_bank = [m.ps(f"scores{n}") for n in range(2)]
        t_bank = m.ps("turned")
        o_bank = [m.ps(f"out{n}") for n in range(2)]
        split, split_step, ones_made = sem("split"), sem("split_step"), sem("ones_made")
        prep, prep_out = sem("prep"), sem("prep_out")
        u_full, u_out = sem("u_full"), sem("u_out")
        l_full, var_done, logv_done, sum_done, mean_full = (
            sem(n) for n in ("l_full", "var", "logv", "sum", "mean_full"))
        z_ready, z_exp = sem("z_ready"), sem("z_exp")
        s_full, s_out, least_done, E_done, E_turned, ET_done, out_full, out_done = (
            sem(n) for n in ("s_full", "s_out", "least", "E", "E_turned", "ET", "out_full", "out"))
        stats_done, doubled, chain = sem("stats_done"), sem("doubled"), sem("chain")
        block = ctx.enter_context(nc.Block())
        x = [K.xh, K.xl]

        @block.sync
        def _(sp):
            for n in names:
                sp.dma_start(W[n][:], dram[f"u_{n}"]).then_inc(loaded[n], 16)

        @block.gpsimd
        def _(pool):
            step = Chain(pool, split_step)
            nc.gpsimd.memset(ones[:], 1.0).then_inc(ones_made, 1)
            nc.gpsimd.memset(wq[0][:].bitcast(F32), 0.0)
            step(nc.gpsimd.memset(wq[1][:].bitcast(F32), 0.0))
            pool.wait_ge(loaded["wq"], 16)
            step(nc.gpsimd.tensor_copy(wq[0][:, :, 0:BOT], W["wq"][:]))
            nc.gpsimd.tensor_tensor(wq[1][:, :, 0:BOT], W["wq"][:], wq[0][:, :, 0:BOT].bitcast(F32), ALU.subtract
                                    ).then_inc(split, 1)
            pool.wait_ge(loaded["wu1"], 16)
            step(nc.gpsimd.tensor_copy(wu[0][:], W["wu1"][:]))
            nc.gpsimd.tensor_tensor(wu[1][:], W["wu1"][:], wu[0][:].bitcast(F32), ALU.subtract
                                    ).then_inc(split, 1)
            for t in range(NT):
                pool.wait_ge(stats_done, t + 1)
                nc.gpsimd.tensor_tensor(K.xs[:, t, :], K.xs[:, t, :], K.xs[:, t, :], ALU.add
                                        ).then_inc(doubled, 1)

        @block.tensor
        def _(pe):
            pe.wait_ge(loaded["wrT"], 16)
            pe.wait_ge(loaded["keysT"], 16)
            nc.tensor.matmul(pre_bank[0:RDIM, 0:NSLOT], W["wrT"][:], W["keysT"][:], start=True, stop=True)
            pe.wait_ge(loaded["valuesT"], 16)
            pe.wait_ge(loaded["wvdT"], 16)
            for c in range(NC_):
                last = nc.tensor.matmul(pre_bank[0:VB, NSLOT:2 * NSLOT], W["wvdT"][:, c, :], W["valuesT"][:, c, :],
                                        start=c == 0, stop=c == NC_ - 1)
            last.then_inc(prep, 1)
            pe.wait_ge(split, 1)
            for n in range(2 * NB):
                b, which = divmod(n, 2)
                if n == 1:
                    pe.wait_ge(split, 2)
                if n > 0:
                    pe.wait_ge(u_out, n)
                for c in range(NC_):
                    last = mm3(nc, u_bank[:], [a[:, c, :] for a in (wq, wu)[which]],
                               [a[:, c, b * SEQ:(b + 1) * SEQ] for a in x], c == 0, c == NC_ - 1)
                last.then_inc(u_full, 1)
            pe.wait_ge(prep_out, 2)
            pe.wait_ge(loaded["wr"], 16)
            nc.tensor.matmul(pre_bank[0:BOT, 0:NSLOT], W["wr"][:], rkT[:], start=True, stop=True).then_inc(prep, 1)
            pe.wait_ge(prep_out, 3)
            pe.wait_ge(loaded["wvuT"], 16)
            nc.tensor.matmul(pre_bank[:], avT[:], W["wvuT"][:], start=True, stop=True).then_inc(prep, 1)
            pe.wait_ge(u_out, 2 * NB)
            pe.wait_ge(loaded["wu2"], 16)
            for t in range(NT):
                nc.tensor.matmul(l_bank[:, t:t + 1], act_u[:, t * P:(t + 1) * P], W["wu2"][:],
                                 start=True, stop=True)
            pe.wait_ge(sum_done, 1)
            pe.wait_ge(ones_made, 1)
            nc.tensor.matmul(l_bank[:, NT:NT + 1], ones[:], logsum[:], start=True, stop=True).then_inc(l_full, 1)
            pe.wait_ge(prep_out, 5)

            def scores(t):
                if t >= 2:
                    pe.wait_ge(s_out, 2 * (t - 1))
                nc.tensor.matmul(s_bank[t % 2][:, 0:2 * NSLOT], query[:, t * P:(t + 1) * P], router[:],
                                 start=True, stop=True).then_inc(s_full, 1)
            scores(0)
            for t in range(NT):
                if t + 1 < NT:
                    scores(t + 1)
                pe.wait_ge(E_done, t + 1)
                if t:
                    pe.wait_ge(ET_done, t)
                nc.tensor.transpose(t_bank[:, 0:P], E[:, t % 2, :], K.ident[:]).then_inc(E_turned, 1)
                pe.wait_ge(ET_done, t + 1)
                if t >= 2:
                    pe.wait_ge(out_done, t - 1)
                nc.tensor.matmul(o_bank[t % 2][:], ET[:, t % 2, :], slot_out[:], start=True, stop=True
                                 ).then_inc(out_full, 1)

        @block.scalar
        def _(act):
            act.wait_ge(prep, 1)
            nc.scalar.activation(rkT[:], pre_bank[0:RDIM, 0:NSLOT], ACT.Copy).then_inc(prep_out, 1)
            nc.scalar.activation(avT[:], pre_bank[0:VB, NSLOT:2 * NSLOT], ACT.Copy).then_inc(prep_out, 1)
            act.wait_ge(loaded["bu1"], 16)
            for n in range(2 * NB):
                b, which = divmod(n, 2)
                s = slice(b * SEQ, (b + 1) * SEQ)
                act.wait_ge(u_full, n + 1)
                if which == 0:
                    nc.scalar.activation(query[:, s], u_bank[0:BOT, :], ACT.Copy).then_inc(u_out, 1)
                else:
                    nc.scalar.activation(act_u[:, s], u_bank[:], ACT.Gelu_apprx_tanh, bias=W["bu1"][:, 0:1]
                                         ).then_inc(u_out, 1)
            act.wait_ge(prep, 2)
            nc.scalar.activation(router[:, 0:NSLOT], pre_bank[0:BOT, 0:NSLOT], ACT.Copy).then_inc(prep_out, 1)
            nc.scalar.activation(router[:, NSLOT:], W["keysT"][:], ACT.Copy).then_inc(prep_out, 1)
            act.wait_ge(prep, 3)
            nc.scalar.activation(slot_out[:], pre_bank[:], ACT.Copy).then_inc(prep_out, 1)
            act.wait_ge(var_done, NT)
            nc.scalar.activation(logv[:], mv[:, :, 1], ACT.Ln, bias=1.0).then_inc(logv_done, 1)
            act.wait_ge(z_ready, 1)
            nc.scalar.activation(learned[:], learned[:], ACT.Exp, scale=-1.0
                                 ).then_inc(z_exp, 1)
            act.wait_ge(z_ready, 2)
            nc.scalar.activation(gate[:], gate[:], ACT.Exp, scale=-1.0
                                 ).then_inc(z_exp, 1)
            for t in range(NT):
                act.wait_ge(least_done, t + 1)
                if t >= 2:
                    act.wait_ge(E_turned, t - 1)
                nc.scalar.activation(E[:, t % 2, :], A[:, t % 2, :], ACT.Exp, scale=-1.0, bias=least[:, t:t + 1],
                                     accum_out=total[:, t:t + 1]).then_inc(E_done, 1)
                act.wait_ge(E_turned, t + 1)
                if t >= 2:
                    act.wait_ge(out_full, t - 1)
                nc.scalar.activation(ET[:, t % 2, :], t_bank[:, 0:P], ACT.Copy).then_inc(ET_done, 1)

        @block.vector
        def _(dve):
            step = Chain(dve, chain)
            for t in range(NT):
                nc.vector.bn_stats(stats[:, t, :], K.xs[:, t, :]).then_inc(stats_done, 1)
            for t in range(NT):
                dve.wait_ge(stats_done, t + 1)
                nc.vector.bn_aggr(mv[:, t, :], stats[:, t, :]).then_inc(var_done, 1)
            dve.wait_ge(logv_done, 1)
            nc.vector.reduce_sum(logsum[:], logv[:], AX_X).then_inc(sum_done, 1)
            dve.wait_ge(loaded["scalars"], 16)
            dve.wait_ge(l_full, 1)
            nc.vector.tensor_scalar(learned[:], l_bank[:, 0:NT], W["scalars"][:, 0:1], -80.0, ALU.add, ALU.max
                                    ).then_inc(z_ready, 1)
            step(nc.vector.tensor_scalar(mean[:], l_bank[:, NT:NT + 1], 1.0 / TOK, 1e-6, ALU.mult, ALU.add))
            step(nc.vector.reciprocal(mean[:], mean[:]))
            step(nc.vector.tensor_scalar(logv[:], logv[:], mean[:, 0:1], 0.5, ALU.mult, ALU.mult))
            dve.wait_ge(z_exp, 1)
            step(nc.vector.tensor_scalar(learned[:], learned[:], 1.0, None, ALU.add))
            step(nc.vector.reciprocal(learned[:], learned[:]))
            step(nc.vector.scalar_tensor_tensor(out=gate[:], in0=learned[:], scalar=2.5, in1=logv[:],
                                                op0=ALU.mult, op1=ALU.add))
            step(nc.vector.tensor_scalar(gate[:], gate[:], 0.0, 5.0, ALU.max, ALU.min))
            step(nc.vector.tensor_scalar(gate[:], gate[:], TAU_LOW, 1.0 / (TAU_HIGH - TAU_LOW),
                                         ALU.subtract, ALU.mult))
            step(nc.vector.tensor_scalar(gate[:], gate[:], 0.0, 1.0, ALU.max, ALU.min))
            step(nc.vector.tensor_scalar(gate[:], gate[:], W["scalars"][:, 1:2], W["scalars"][:, 2:3],
                                         ALU.mult, ALU.add))
            nc.vector.tensor_scalar(gate[:], gate[:], -80.0, None, ALU.max).then_inc(z_ready, 1)
            dve.wait_ge(z_exp, 2)
            step(nc.vector.tensor_scalar(gate[:], gate[:], 1.0, None, ALU.add))
            step(nc.vector.reciprocal(gate[:], gate[:]))
            step(nc.vector.tensor_scalar(live[:], gate[:], EARLY_EXIT, None, ALU.is_ge))
            step(nc.vector.tensor_tensor(gate[:], gate[:], live[:], ALU.mult))
            dve.wait_ge(loaded["log_rel"], 16)

            def pick(t):
                n = t % 2
                dve.wait_ge(s_full, t + 1)
                if t >= 2:
                    dve.wait_ge(E_done, t - 1)
                nc.vector.scalar_tensor_tensor(out=R[:, n, :], in0=s_bank[n][:, 0:NSLOT],
                                               scalar=float(RDIM) ** -0.5, in1=W["log_rel"][:],
                                               op0=ALU.mult, op1=ALU.add).then_inc(s_out, 1)
                nc.vector.scalar_tensor_tensor(out=A[:, n, :], in0=s_bank[n][:, NSLOT:2 * NSLOT],
                                               scalar=-float(BOT) ** -0.5, in1=W["log_rel"][:],
                                               op0=ALU.mult, op1=ALU.subtract).then_inc(s_out, 1)
                dve.wait_ge(s_out, 2 * t + 2)
                step(nc.vector.max(best[:, n, :], R[:, n, :]))
                step(nc.vector.match_replace(out=R2[:, n, :], in_to_replace=best[:, n, :], in_values=R[:, n, :],
                                             imm_value=-HIDDEN))
                step(nc.vector.tensor_tensor(chosen[:, n, :], R[:, n, :], R2[:, n, :], ALU.not_equal))
                nc.vector.tensor_scalar(off[:, n, :], chosen[:, n, :], 1.0, -HIDDEN, ALU.subtract, ALU.mult)
                step(nc.vector.tensor_tensor(A[:, n, :], A[:, n, :], chosen[:, n, :], ALU.mult))
                step(nc.vector.tensor_tensor(A[:, n, :], A[:, n, :], off[:, n, :], ALU.add))
                nc.vector.tensor_reduce(least[:, t:t + 1], A[:, n, :], AX_X, ALU.min).then_inc(least_done, 1)
            pick(0)
            for t in range(NT):
                if t + 1 < NT:
                    pick(t + 1)
                dve.wait_ge(E_done, t + 1)
                step(nc.vector.reciprocal(factor[:, t:t + 1], total[:, t:t + 1]))
                step(nc.vector.tensor_tensor(factor[:, t:t + 1], factor[:, t:t + 1], gate[:, t:t + 1], ALU.mult))
                dve.wait_ge(out_full, t + 1)
                dve.wait_ge(doubled, t + 1)
                nc.vector.scalar_tensor_tensor(out=K.xs[:, t, :], in0=o_bank[t % 2][:], scalar=factor[:, t:t + 1],
                                               in1=K.xs[:, t, :], op0=ALU.mult, op1=ALU.add).then_inc(out_done, 1)


def pair_stage(nc, K, xf, pre):
    SCALE = float(SEQ) ** -0.5
    with ExitStack() as ctx:
        m = Memory(nc, ctx, pre)
        sb, sem = m.sb, m.sem
        prod = sb("prod", [P, 2, SEQ])
        G = sb("G", [P, NC_, NB, NB])
        top, total = sb("top", [P, NC_, NB]), sb("total", [P, NC_, NB])
        mixed, other = sb("mixed", [P, NC_, TOK]), sb("other", [P, 2, SEQ])
        bank = [m.ps(f"bank{n}") for n in range(4)]
        dots, chain, diff, expd, prob = sem("dots"), sem("chain"), sem("diff"), sem("expd"), sem("prob")
        other_done, mixed_done, turned, taken = (sem(n) for n in ("other", "mixed", "turned", "taken"))
        block = ctx.enter_context(nc.Block())

        @block.vector
        def _(dve):
            step = Chain(dve, chain)
            n = 0
            for c in range(NC_):
                for i, j in ((0, 0), (0, 1), (1, 1)):
                    if n >= 2:
                        dve.wait_ge(dots, n - 1)
                    nc.vector.tensor_tensor_reduce(
                        out=prod[:, n % 2, :], in0=xf[:, c, i * SEQ:(i + 1) * SEQ],
                        in1=xf[:, c, j * SEQ:(j + 1) * SEQ], scale=SCALE, scalar=0.0, op0=ALU.mult,
                        op1=ALU.add, accum_out=G[:, c, i, j:j + 1]).then_inc(dots, 1)
                    n += 1
            dve.wait_ge(dots, n)
            step(nc.vector.tensor_copy(G[:, :, 1, 0], G[:, :, 0, 1]))
            step(nc.vector.tensor_reduce(top[:], G[:], AX_X, ALU.max))
            nc.vector.tensor_tensor(G[:], G[:], top[:].unsqueeze(3).to_broadcast([P, NC_, NB, NB]), ALU.subtract
                                    ).then_inc(diff, 1)
            dve.wait_ge(expd, 1)
            step(nc.vector.reduce_sum(total[:], G[:], AX_X))
            step(nc.vector.reciprocal(total[:], total[:]))
            step(nc.vector.tensor_tensor(G[:], G[:], total[:].unsqueeze(3).to_broadcast([P, NC_, NB, NB]),
                                         ALU.mult))
            for b in range(NB):
                ins = nc.vector.tensor_scalar(G[:, :, b, b], G[:, :, b, b], 1.0, None, ALU.add)
            ins.then_inc(prob, 1)
            dve.wait_ge(prob, 1)
            for n in range(NB * NC_):
                b, c = divmod(n, NC_)
                s = slice(b * SEQ, (b + 1) * SEQ)
                dve.wait_ge(other_done, n + 1)
                nc.vector.scalar_tensor_tensor(out=mixed[:, c, s], in0=xf[:, c, s], scalar=G[:, c, b, b:b + 1],
                                               in1=other[:, n % 2, :], op0=ALU.mult, op1=ALU.add
                                               ).then_inc(mixed_done, 1)

        @block.scalar
        def _(act):
            act.wait_ge(diff, 1)
            nc.scalar.activation(G[:], G[:], ACT.Exp).then_inc(expd, 1)
            act.wait_ge(prob, 1)

            def other_part(n):
                b, c = divmod(n, NC_)
                if n >= 2:
                    act.wait_ge(mixed_done, n - 1)
                nc.scalar.activation(other[:, n % 2, :], xf[:, c, (1 - b) * SEQ:(2 - b) * SEQ], ACT.Copy,
                                     scale=G[:, c, b, 1 - b:2 - b]).then_inc(other_done, 1)
            for b in range(NB):
                for c in range(NC_):
                    other_part(b * NC_ + c)
            for t in range(NT):
                act.wait_ge(turned, t + 1)
                nc.scalar.activation(K.xs[:, t, :], bank[t % 4][:], ACT.Copy).then_inc(taken, 1)

        @block.tensor
        def _(pe):
            for t in range(NT):
                pe.wait_ge(mixed_done, NC_ * (t // TB + 1))
                if t >= 4:
                    pe.wait_ge(taken, t - 3)
                for c in range(NC_):
                    last = nc.tensor.transpose(bank[t % 4][:, c * P:(c + 1) * P], mixed[:, c, t * P:(t + 1) * P],
                                               K.ident[:])
                last.then_inc(turned, 1)


EXPERTS, RANK = 8, 16
SCALING = 32.0 / 16.0


def experts_stage(nc, K, dram, pre):
    ER = EXPERTS * RANK
    NA = ER + EXPERTS
    with ExitStack() as ctx:
        m = Memory(nc, ctx, pre)
        sb, sem = m.sb, m.sem
        shapes = {"wa": [P, NC_, NA], "wb": [P, NC_, D], "lb": [ER, D]}
        raw = {n: sb(f"{n}_raw", s) for n, s in shapes.items()}
        W = {n: [sb(f"{n}{h}", s, F32R) for h in "hl"] for n, s in shapes.items()}
        bias = sb("bias", [P, D])
        ranks = sb("ranks", [P, NT, EXPERTS, RANK])
        rT = [sb(f"rT{n}", [P, TOK], F32R) for n in "hl"]
        L, first, cand, best = (sb(n, [P, NT, EXPERTS]) for n in ("L", "first", "cand", "best"))
        weight, order = sb("weight", [P, NT, EXPERTS]), sb("order", [P, EXPERTS])
        top, m1, m2 = sb("top", [P, NT]), sb("m1", [P, NT]), sb("m2", [P, NT])
        a_bank = [m.ps(f"ranks{n}") for n in range(2)]
        t_bank = [m.ps(f"turned{n}") for n in range(2)]
        o_bank = [m.ps(f"out{n}") for n in range(4)]
        loaded = {n: sem(f"in_{n}") for n in (*shapes, "bias", "order")}
        split_step, split = sem("split_step"), sem("split")
        a_full, a_out, chain, ready, expd, weighted = (
            sem(n) for n in ("a_full", "a_out", "chain", "ready", "expd", "weighted"))
        turned, t_hi, t_lo, o_full, o_out, biased = (
            sem(n) for n in ("turned", "t_hi", "t_lo", "o_full", "o_out", "biased"))
        block = ctx.enter_context(nc.Block())
        x = [K.xh, K.xl]

        @block.sync
        def _(sp):
            for n in shapes:
                sp.dma_start(raw[n][:], dram[f"e_{n}"]).then_inc(loaded[n], 16)
            sp.dma_start(bias[:], dram["e_bias"]).then_inc(loaded["bias"], 16)
            sp.dma_start(order[:], dram["e_order"]).then_inc(loaded["order"], 16)

        @block.gpsimd
        def _(pool):
            step = Chain(pool, split_step)
            for n in shapes:
                pool.wait_ge(loaded[n], 16)
                hi, lo = W[n]
                step(nc.gpsimd.tensor_copy(hi[:], raw[n][:]))
                nc.gpsimd.tensor_tensor(lo[:], raw[n][:], hi[:].bitcast(F32), ALU.subtract).then_inc(split, 1)

        @block.tensor
        def _(pe):
            pe.wait_ge(split, 1)
            for t in range(NT):
                if t >= 2:
                    pe.wait_ge(a_out, t - 1)
                for c in range(NC_):
                    last = mm3(nc, a_bank[t % 2][:, 0:NA], [a[:, c, t * P:(t + 1) * P] for a in x],
                               [a[:, c, :] for a in W["wa"]], c == 0, c == NC_ - 1)
                last.then_inc(a_full, 1)

            def base(t):
                if t >= 4:
                    pe.wait_ge(o_out, t - 3)
                for c in range(NC_):
                    mm3(nc, o_bank[t % 4][:], [a[:, c, t * P:(t + 1) * P] for a in x],
                        [a[:, c, :] for a in W["wb"]], c == 0, False)
            pe.wait_ge(split, 2)
            for t in range(4):
                base(t)
            pe.wait_ge(weighted, 1)
            for b in range(NB):
                for i in range(TB):
                    t = b * TB + i
                    last = nc.tensor.transpose(t_bank[b][:, i * P:(i + 1) * P],
                                               ranks[:, t].rearrange("p e r -> p (e r)"), K.ident[:])
                last.then_inc(turned, 1)
            pe.wait_ge(split, 3)
            for t in range(NT):
                if t >= 4:
                    base(t)
                if t % TB == 0:
                    pe.wait_ge(t_lo, t // TB + 1)
                mm3(nc, o_bank[t % 4][:], [a[:, t * P:(t + 1) * P] for a in rT], [a[:] for a in W["lb"]],
                    False, True).then_inc(o_full, 1)

        @block.scalar
        def _(act):
            for t in range(NT):
                act.wait_ge(a_full, t + 1)
                nc.scalar.activation(ranks[:, t].rearrange("p e r -> p (e r)"), a_bank[t % 2][:, 0:ER], ACT.Copy)
                nc.scalar.activation(L[:, t, :], a_bank[t % 2][:, ER:NA], ACT.Copy).then_inc(a_out, 1)
            act.wait_ge(ready, 1)
            nc.scalar.activation(L[:], L[:], ACT.Exp).then_inc(expd, 1)
            for b in range(NB):
                act.wait_ge(turned, b + 1)
                nc.scalar.activation(rT[0][:, b * SEQ:(b + 1) * SEQ], t_bank[b][:], ACT.Copy).then_inc(t_hi, 1)

        @block.vector
        def _(dve):
            step = Chain(dve, chain)
            wide = [P, NT, EXPERTS]

            def over(t):
                return t[:].unsqueeze(2).to_broadcast(wide)
            dve.wait_ge(loaded["order"], 16)
            dve.wait_ge(a_out, NT)
            step(nc.vector.tensor_reduce(top[:], L[:], AX_X, ALU.max))
            nc.vector.tensor_tensor(L[:], L[:], over(top), ALU.subtract).then_inc(ready, 1)
            dve.wait_ge(expd, 1)
            step(nc.vector.reduce_sum(top[:], L[:], AX_X))
            step(nc.vector.reciprocal(top[:], top[:]))
            step(nc.vector.tensor_tensor(L[:], L[:], over(top), ALU.mult))

            def first_best(value, mark):
                step(nc.vector.tensor_reduce(value[:], L[:], AX_X, ALU.max))
                step(nc.vector.tensor_tensor(cand[:], L[:], over(value), ALU.is_equal))
                step(nc.vector.tensor_tensor(cand[:], cand[:], order[:].unsqueeze(1).to_broadcast(wide), ALU.mult))
                step(nc.vector.tensor_reduce(top[:], cand[:], AX_X, ALU.max))
                step(nc.vector.tensor_tensor(mark[:], cand[:], over(top), ALU.is_equal))
            first_best(m1, first)
            step(nc.vector.scalar_tensor_tensor(out=L[:].rearrange("p t e -> p (t e)"),
                                                in0=first[:].rearrange("p t e -> p (t e)"), scalar=-2.0,
                                                in1=L[:].rearrange("p t e -> p (t e)"),
                                                op0=ALU.mult, op1=ALU.add))
            first_best(m2, best)
            step(nc.vector.tensor_tensor(first[:], first[:], over(m1), ALU.mult))
            step(nc.vector.tensor_tensor(best[:], best[:], over(m2), ALU.mult))
            step(nc.vector.tensor_tensor(weight[:], first[:], best[:], ALU.add))
            step(nc.vector.tensor_tensor(m1[:], m1[:], m2[:], ALU.add))
            step(nc.vector.reciprocal(m1[:], m1[:]))
            step(nc.vector.tensor_scalar(m1[:], m1[:], SCALING, None, ALU.mult))
            step(nc.vector.tensor_tensor(weight[:], weight[:], over(m1), ALU.mult))
            flat = ranks[:].rearrange("p t e r -> p (t e) r")
            nc.vector.tensor_tensor(flat, flat, weight[:].rearrange("p t e -> p (t e)").unsqueeze(2)
                                    .to_broadcast([P, NT * EXPERTS, RANK]), ALU.mult).then_inc(weighted, 1)
            dve.wait_ge(loaded["bias"], 16)
            for t in range(NT):
                nc.vector.tensor_tensor(K.xs[:, t, :], K.xs[:, t, :], bias[:], ALU.add).then_inc(biased, 1)
            for b in range(NB):
                dve.wait_ge(t_hi, b + 1)
                s = slice(b * SEQ, (b + 1) * SEQ)
                nc.vector.tensor_tensor(rT[1][:, s], t_bank[b][:], rT[0][:, s].bitcast(F32), ALU.subtract
                                        ).then_inc(t_lo, 1)
            for t in range(NT):
                dve.wait_ge(o_full, t + 1)
                dve.wait_ge(biased, t + 1)
                nc.vector.tensor_tensor(K.xs[:, t, :], K.xs[:, t, :], o_bank[t % 4][:], ALU.add).then_inc(o_out, 1)


class Kept:

    def __init__(self, nc, ctx):
        m = Memory(nc, ctx, "kept")
        self.stored = m.sem("stored")
        self.xs = m.sb("x", [P, NT, D])
        self.xh = m.sb("x_hi", [P, NC_, TOK], F32R)
        self.xl = m.sb("x_lo", [P, NC_, TOK], F32R)
        self.ident = m.sb("ident", [P, P])
        self.ident_r, self.mask_r = m.sb("ident_r", [P, P], F32R), m.sb("mask_r", [P, P], F32R)
        self.half, self.zero = m.sb("minus_half", [P, NT]), m.sb("zero", [P, 1])


def program(nc, dram, out, stages=STAGES):
    with ExitStack() as ctx:
        K = Kept(nc, ctx)
        x0 = dram["x"].rearrange("b t d -> (b t) d")
        setup_stage(nc, K, {"x": x0}, "setup")
        norm_stage(nc, K, "turn0", normalize=False)
        for n, stage in enumerate(stages):
            if stage == "attn3":
                with ExitStack() as own:
                    xf = Memory(nc, own, "pair").sb("x_turned", [P, NC_, TOK])
                    norm_stage(nc, K, f"turn{n + 1}", normalize=False, full=xf)
                    pair_stage(nc, K, xf, "a3")
            else:
                STAGE[stage](nc, K, dram)
            end = n == len(stages) - 1
            norm_stage(nc, K, f"norm{n}", out=out.rearrange("b t d -> (b t) d") if end else None)


STAGE = {
    "ffn2": lambda nc, K, d: slots_stage(nc, K, d, "f2"),
    "ffn3": lambda nc, K, d: experts_stage(nc, K, d, "f3"),
    "ffn1": lambda nc, K, d: streams_stage(nc, K, d, "f1"),
    "attn0": lambda nc, K, d: rotary_attention_stage(nc, K, d, "a0"),
    "ffn0": lambda nc, K, d: gated_ffn_stage(nc, K, d, "f0"),
    "attn1": lambda nc, K, d: attention_stage(nc, K, {"w": d["w1"]}, 1, "a1"),
    "attn2": lambda nc, K, d: attention_stage(nc, K, {"w": d["w2"], "qkw": d["qkw"], "pick": d["pick"],
                                                      "tab": d["tab"]}, 2, "a2"),
}


def layout(inputs):
    import numpy as np
    a = {n: np.asarray(v) for n, v in inputs.items()}
    f = np.float32

    def group_weights(wq, wk, wv, wo):
        q = wq.reshape(NC_, P, KV, GROUP, P).transpose(2, 3, 1, 0, 4).reshape(KV, GROUP, P, 512)
        k = wk.reshape(NC_, P, KV, P).transpose(2, 1, 0, 3).reshape(KV, 1, P, 512)
        v = wv.reshape(NC_, P, KV, P).transpose(2, 1, 0, 3).reshape(KV, 1, P, 512)
        o = wo.reshape(KV, GROUP, P, D)
        return np.concatenate([q, k, v, o], axis=1).reshape(KV * PIECES, P, 512)

    out = {"x": a["L0_attn_x"]}
    wq = a["L0_attn_Wq"].reshape(NC_, P, KV, GROUP * HD0)
    wk, wv = (a[n].reshape(NC_, P, KV, HD0) for n in ("L0_attn_Wk", "L0_attn_Wv"))
    out["w0"] = np.concatenate([wq, wk, wv], axis=3).transpose(1, 0, 2, 3).reshape(P, -1)
    wo = a["L0_attn_Wo"].reshape(KV, GROUP, 1, HD0, D)
    out["wo0"] = np.concatenate([wo, wo], axis=2).reshape(KV, P, D).transpose(1, 0, 2)
    inv_freq = f(1.0) / f(500000.0) ** (np.arange(0, HD0, 2, dtype=f) / f(HD0))
    angle = np.arange(SEQ, dtype=f)[:, None] * inv_freq.astype(f)[None, :]
    cos, sin = np.cos(angle).astype(f), np.sin(angle).astype(f)
    out["cos"] = np.concatenate([cos, cos], axis=1).reshape(TB, P, HD0).transpose(1, 0, 2)
    out["sin"] = np.concatenate([-sin, sin], axis=1).reshape(TB, P, HD0).transpose(1, 0, 2)
    pad = NF * P - FF

    def hidden_rows(w):
        return np.pad(w, ((0, pad), (0, 0)))
    gu = [hidden_rows(a[n]).reshape(NF, P, NC_, P).transpose(0, 3, 2, 1)
          for n in ("L0_ffn_gate_w", "L0_ffn_up_w")]
    out["gu"] = np.stack(gu, axis=2).reshape(NF, P, 2 * NC_ * P)
    out["gu_scale"] = np.stack([hidden_rows(a[n]).reshape(NF, P).T for n in ("L0_ffn_gate_s", "L0_ffn_up_s")],
                               axis=2)
    out["down"] = hidden_rows(a["L0_ffn_down_w"].T).reshape(NF, P, D)
    out["down_scale"] = np.broadcast_to(a["L0_ffn_down_s"].reshape(1, D), (P, D))
    w = a["L1_attn_w_qkv"].T
    n, kv = HEADS * P, KV * P
    out["w1"] = group_weights(w[:, :n], w[:, n:n + kv], w[:, n + kv:], a["L1_attn_w_dense"].T)
    ws = np.concatenate([a["L1_ffn_W_res"], a["L1_ffn_W_pre"], a["L1_ffn_W_post"]], axis=0)
    out["s_w"] = ws.T.reshape(NC_, P, -1).transpose(1, 0, 2)
    out["s_wb"] = a["L1_ffn_W_branch"]
    b = np.concatenate([a["L1_ffn_H_res_base"].reshape(-1), a["L1_ffn_H_pre_base"], a["L1_ffn_H_post_base"]])
    out["s_base"] = np.broadcast_to(b, (P, b.size))
    out["s_gate"] = np.broadcast_to(a["L1_ffn_gate"], (P, 1))
    out["w2"] = group_weights(a["L2_attn_Wq"].T, a["L2_attn_Wk"].T, a["L2_attn_Wv"].T, a["L2_attn_Wo"].T)
    out["qkw"] = np.stack([a["L2_attn_q_norm_w"], a["L2_attn_k_norm_w"]], axis=1)
    def chunks(w):
        return w.reshape(NC_, P, -1).transpose(1, 0, 2)
    s = {n: a[f"L2_ffn_{n}"] for n in ("Wq", "Wr", "aux_keys", "aux_values", "Wvd", "Wvu", "Wu1", "bu1", "Wu2",
                                       "bu2", "gate_w1", "gate_bias", "log_rel")}
    out.update(u_wq=chunks(s["Wq"].T), u_wr=s["Wr"], u_wrT=s["Wr"].T, u_keysT=s["aux_keys"].T,
               u_valuesT=chunks(s["aux_values"].T), u_wvdT=chunks(s["Wvd"].T), u_wvuT=s["Wvu"].T,
               u_wu1=chunks(s["Wu1"].T), u_wu2=s["Wu2"].T, u_bu1=s["bu1"].reshape(P, 1),
               u_scalars=np.broadcast_to(np.stack([s["bu2"].reshape(()), s["gate_w1"], s["gate_bias"]]), (P, 3)),
               u_log_rel=np.broadcast_to(s["log_rel"], (P, NSLOT)))
    out["e_wa"] = chunks(np.concatenate([a["L3_ffn_lora_A"].reshape(-1, D), a["L3_ffn_W_router"]]).T)
    out["e_wb"] = chunks(a["L3_ffn_W_base"].T)
    out["e_lb"] = a["L3_ffn_lora_B"].transpose(0, 2, 1).reshape(-1, D)
    out["e_bias"] = np.broadcast_to(a["L3_ffn_b_base"], (P, D))
    out["e_order"] = np.broadcast_to(np.arange(EXPERTS, 0, -1).astype(f), (P, EXPERTS))
    import math
    start = 2 ** (-2 ** (-(math.log2(HEADS) - 3)))
    slopes = np.array([start * start ** i for i in range(HEADS)], dtype=f)
    t = -(slopes[:, None] * (np.arange(SEQ, dtype=f) - f(SEQ - P // 2)))

    def top(t):
        return (t.view(np.uint32) & np.uint32(0xFFFF0000)).view(f)
    hi = top(t)
    mid = top(t - hi)
    out["tab"] = np.stack([hi, mid, t - hi - mid], axis=1).reshape(KV, 3 * GROUP, SEQ)
    pick = np.zeros((3 * GROUP, GROUP, P), f)
    for j in range(GROUP):
        pick[3 * j:3 * j + 3, j, :] = 1.0
    out["pick"] = pick
    used = NEEDS["x"].union(*(NEEDS[s] for s in STAGES))
    return {n: np.ascontiguousarray(v) for n, v in out.items() if n in used}


NEEDS = {"x": {"x"}, "attn3": set(), "ffn3": {"e_wa", "e_wb", "e_lb", "e_bias", "e_order"},
         "ffn2": {"u_wq", "u_wr", "u_wrT", "u_keysT", "u_valuesT", "u_wvdT", "u_wvuT", "u_wu1", "u_wu2", "u_bu1",
                  "u_scalars", "u_log_rel"},
         "ffn1": {"s_w", "s_wb", "s_base", "s_gate"}, "attn0": {"w0", "wo0", "cos", "sin"}, "ffn0": {"gu", "gu_scale", "down", "down_scale"}, "attn1": {"w1"}, "attn2": {"w2", "qkw", "pick", "tab"}}


def kernel(**inputs):
    import concourse.bacc as _bacc
    from concourse import mybir as _mybir
    from concourse.bass_utils import run_bass_kernel_spmd as _run

    nc = _bacc.Bacc("TRN2", target_bir_lowering=False, num_devices=1)
    arrays, dram = {}, {}
    for name, a in layout(inputs).items():
        arrays[f"in_{name}"] = a
        dram[name] = nc.dram_tensor(f"in_{name}", a.shape, _mybir.dt.from_np(a.dtype), kind="ExternalInput").ap()
    out = nc.dram_tensor("out", (NB, SEQ, D), F32, kind="ExternalOutput").ap()
    program(nc, dram, out)
    r = _run(nc, [arrays], core_ids=[0])
    return r.results[0]["out"]
```

```python
from contextlib import ExitStack

import concourse.bass as bass
from concourse import mybir

P = 128
TOK = 1024
NB = 2
SEQ = TOK // NB
NT = TOK // P
TB = SEQ // P
D = 512
NC_ = D // P
HEADS, KV = 32, 8
GROUP = HEADS // KV
LN_EPS = 1e-5
MASKED = 1e30

F32 = mybir.dt.float32
F32R = mybir.dt.float32r
I32 = mybir.dt.int32
BF16 = mybir.dt.bfloat16
ALU = mybir.AluOpType
ACT = mybir.ActivationFunctionType
AX_X = mybir.AxisListType.X

SLOT = {3: (0, 0), 2: (1, 0), 0: (1, 384), 1: (2, 0)}
COL = {qi: 512 * b + o for qi, (b, o) in SLOT.items()}
ORDER = (3, 2, 0, 1)
PACKED = 1280


STAGES = ('attn0', 'ffn0', 'attn1', 'ffn1', 'attn2', 'ffn2', 'attn3', 'ffn3', )


class Memory:

    def __init__(self, nc, ctx, prefix):
        self.nc, self.ctx, self.prefix = nc, ctx, prefix
        self.sems = []
        ctx.callback(self.clear)

    def sb(self, name, shape, dt=F32):
        return self.ctx.enter_context(self.nc.sbuf_tensor(f"{self.prefix}_{name}", shape, dt))

    def ps(self, name, shape=(P, 512)):
        return self.ctx.enter_context(self.nc.psum_tensor(f"{self.prefix}_{name}", list(shape), F32))

    def sem(self, name):
        self.sems.append(self.nc.alloc_semaphore(name=f"{self.prefix}_{name}"))
        return self.sems[-1]

    def clear(self):
        if self.sems:
            self.nc.clear_and_free_semaphores(self.sems)
            self.nc.all_engine_barrier()


class Chain:

    def __init__(self, eng, sem):
        self.eng, self.sem, self.n = eng, sem, 0

    def __call__(self, instruction):
        self.n += 1
        instruction.then_inc(self.sem, 1)
        self.eng.wait_ge(self.sem, self.n)


def mm3(nc, out, a, b, start, stop):
    last = None
    for n, (i, j) in enumerate(((0, 0), (0, 1), (1, 0))):
        last = nc.tensor.matmul(out, a[i], b[j], start=start and n == 0, stop=stop and n == 2)
    return last


def add_masks(nc, K, S, n):
    col, blocks = ((384, 1), (256, 2), (128, 1))[n]
    out = S[n][:, col:col + blocks * P]
    if blocks == 1:
        return nc.tensor.matmul(out, K.ident_r[:], K.mask_r[:], start=False, stop=True)
    return nc.tensor.matmul(out.rearrange("p (n k) -> p n k", n=blocks), K.ident_r[:],
                            K.mask_r[:].unsqueeze(1).to_broadcast([P, blocks, P]), start=False, stop=True)


def setup_stage(nc, K, dram, pre):
    with ExitStack() as ctx:
        m = Memory(nc, ctx, pre)
        mask = m.sb("mask", [P, P])
        x_in, made, done = m.sem("x_in"), m.sem("made"), m.sem("done")
        block = ctx.enter_context(nc.Block())

        @block.sync
        def _(sp):
            sp.dma_start(K.xs[:], dram["x"].rearrange("(t p) d -> p t d", p=P)).then_inc(x_in, 16)
            sp.wait_ge(x_in, 16)

        @block.gpsimd
        def _(pool):
            step = Chain(pool, made)
            step(nc.gpsimd.memset(K.ident[:], 0.0))
            step(nc.gpsimd.affine_select(out=K.ident[:], in_=K.ident[:], compare_op=ALU.not_equal, fill=1.0,
                                         base=0, pattern=[[-1, P]], channel_multiplier=1))
            step(nc.gpsimd.memset(mask[:], 0.0))
            step(nc.gpsimd.affine_select(out=mask[:], in_=mask[:], compare_op=ALU.is_ge, fill=MASKED,
                                         base=0, pattern=[[-1, P]], channel_multiplier=1))
            step(nc.gpsimd.memset(K.half[:], -0.5))
            step(nc.gpsimd.memset(K.zero[:], 0.0))
            nc.gpsimd.tensor_copy(K.ident_r[:], K.ident[:]).then_inc(done, 1)
            nc.gpsimd.tensor_copy(K.mask_r[:], mask[:]).then_inc(done, 1)
            pool.wait_ge(done, 2)


def norm_stage(nc, K, pre, normalize=True, full=None, out=None):
    with ExitStack() as ctx:
        m = Memory(nc, ctx, pre)
        stats, mv = m.sb("stats", [P, NT, 6]), m.sb("mv", [P, NT, 2])
        rstd, vare = m.sb("rstd", [P, NT]), m.sb("vare", [P, NT])
        shift = m.sb("shift", [P, NT])
        banks = [m.ps(f"bank{n}") for n in range(4)]
        stats_done, mv_done, eps_done, rstd_done = (m.sem(n) for n in ("stats", "mv", "eps", "rstd"))
        normed, transposed, hi_done, evacuated = (m.sem(n) for n in ("normed", "transposed", "hi", "evacuated"))
        normed_act = m.sem("normed_act")
        stored = K.stored
        block = ctx.enter_context(nc.Block())

        if out is not None:
            @block.sync
            def _(sp):
                for t in range(NT):
                    b, h, n = t // TB, t % TB // (TB // 2), t % (TB // 2)
                    sp.wait_ge((normed, normed_act)[h], b * TB // 2 + n + 1)
                    sp.dma_start(out[t * P:(t + 1) * P, :], K.xs[:, t, :]).then_inc(stored, 16)
                sp.wait_ge(stored, 16 * NT)

        if normalize:
            @block.gpsimd
            def _(pool):
                for b in range(NB):
                    s = slice(b * TB, (b + 1) * TB)
                    pool.wait_ge(mv_done, (b + 1) * TB)
                    nc.gpsimd.tensor_scalar(vare[:, s], mv[:, s, 1], LN_EPS, None, ALU.add).then_inc(eps_done, 1)
                    pool.wait_ge(eps_done, 3 * b + 1)
                    nc.gpsimd.tensor_tensor(rstd[:, s], vare[:, s], K.half[:, s], ALU.pow).then_inc(eps_done, 1)
                    pool.wait_ge(eps_done, 3 * b + 2)
                    nc.gpsimd.tensor_tensor(shift[:, s], mv[:, s, 0], rstd[:, s], ALU.mult).then_inc(eps_done, 1)
                    pool.wait_ge(eps_done, 3 * b + 3)
                    nc.gpsimd.tensor_scalar(shift[:, s], shift[:, s], -1.0, None, ALU.mult).then_inc(rstd_done, 1)

        @block.vector
        def _(dve):
            if normalize:
                for b in range(NB):
                    tiles = range(b * TB, (b + 1) * TB)
                    for t in tiles:
                        nc.vector.bn_stats(stats[:, t, :], K.xs[:, t, :]).then_inc(stats_done, 1)
                    for t in tiles:
                        dve.wait_ge(stats_done, t + 1)
                        nc.vector.bn_aggr(mv[:, t, :], stats[:, t, :]).then_inc(mv_done, 1)
                for b in range(NB):
                    dve.wait_ge(rstd_done, b + 1)
                    for t in range(b * TB, b * TB + TB // 2):
                        nc.vector.tensor_scalar(K.xs[:, t, :], K.xs[:, t, :], mv[:, t, 0:1], rstd[:, t:t + 1],
                                                ALU.subtract, ALU.mult).then_inc(normed, 1)
            if out is None and full is None:
                for n in range(NB * NC_):
                    b, c = divmod(n, NC_)
                    dve.wait_ge(hi_done, n + 1)
                    s = slice(b * SEQ, (b + 1) * SEQ)
                    nc.vector.tensor_tensor(K.xl[:, c, s], banks[n % 4][:], K.xh[:, c, s].bitcast(F32),
                                            ALU.subtract).then_inc(evacuated, 1)

        @block.tensor
        def _(pe):
            for n in range(0 if out is not None else NB * NC_):
                b, c = divmod(n, NC_)
                if normalize and c == 0:
                    pe.wait_ge(normed, (b + 1) * TB // 2)
                    pe.wait_ge(normed_act, (b + 1) * TB // 2)
                if n >= 4:
                    pe.wait_ge(evacuated, n - 3)
                for i in range(TB):
                    last = nc.tensor.transpose(banks[n % 4][:, i * P:(i + 1) * P],
                                               K.xs[:, b * TB + i, c * P:(c + 1) * P], K.ident[:])
                last.then_inc(transposed, 1)

        @block.scalar
        def _(act):
            def normed_batch(b):
                act.wait_ge(rstd_done, b + 1)
                for t in range(b * TB + TB // 2, (b + 1) * TB):
                    nc.scalar.activation(K.xs[:, t, :], K.xs[:, t, :], ACT.Identity, scale=rstd[:, t:t + 1],
                                         bias=shift[:, t:t + 1]).then_inc(normed_act, 1)

            if normalize:
                for b in range(NB):
                    normed_batch(b)
            for b in range(NB):
                for n in range(b * NC_, (b + 1) * NC_) if out is None else ():
                    c = n % NC_
                    s = slice(b * SEQ, (b + 1) * SEQ)
                    act.wait_ge(transposed, n + 1)
                    if full is None:
                        nc.scalar.activation(K.xh[:, c, s], banks[n % 4][:], ACT.Copy).then_inc(hi_done, 1)
                    else:
                        nc.scalar.activation(full[:, c, s], banks[n % 4][:], ACT.Copy).then_inc(evacuated, 1)


HD0 = 16
G0 = (GROUP + 2) * HD0


def rotary_attention_stage(nc, K, dram, pre):
    NEG = -float(HD0) ** -0.5
    with ExitStack() as ctx:
        m = Memory(nc, ctx, pre)
        sb, sem = m.sb, m.sem
        S = [m.ps(f"scores{n}") for n in range(3)]
        T = [m.ps(f"turned{n}") for n in range(3)]
        O = m.ps("mixed")
        W = m.ps("work")
        area = [sb(f"area{n}", [P, KV * SEQ], F32R) for n in "hl"]
        w = [a[:, 0:NC_ * KV * G0] for a in area]
        cT = [[a[:].rearrange("p c t -> p (c t)") for a in (K.xh, K.xl)], [a[:] for a in area]]
        wo = [sb(f"wo{n}", [P, KV, D], F32R) for n in "hl"]
        cos, sin = sb("cos", [P, TB, HD0]), sb("sin", [P, TB, HD0])
        qkv = sb("qkv", [P, NT, KV * G0])
        rot, rot2 = sb("rot", [P, TB, GROUP + 1, HD0]), sb("rot2", [P, TB, GROUP + 1, HD0])
        v_in_hand = sb("v_in_hand", [P, TB, HD0])
        qs = sb("qs", [P, TB, GROUP, 2, HD0])
        ks = [sb(f"ks{n}", [P, TB, 2 * GROUP, HD0]) for n in "hl"]
        qT = sb("qT", [P, NB, SEQ], F32R)
        kT = [sb(f"kT{n}", [P, NB, SEQ], F32R) for n in "hl"]
        v = [sb(f"v{n}", [P, NB, TB, 224], F32R) for n in "hl"]
        probs = sb("probs", [P, 2 * PACKED])
        n_w, n_wo = NC_ * KV * G0, KV * D // 2
        flat = qkv[:].rearrange("p t n -> p (t n)")
        w_raw = flat[:, 0:n_w]
        wo_raw = [a.rearrange("p (i n) -> p i n", n=D) for a in (flat[:, n_w:n_w + n_wo], probs[:, 0:n_wo])]
        negmax = sb("negmax", [P, 2, 4])
        rowsum, recip = sb("rowsum", [P, NB, TB, GROUP]), sb("recip", [P, TB, GROUP])
        wide = sb("wide", [P, TB, GROUP, 32])
        product = sb("product", [P, SEQ])
        pT = [sb(f"pT{n}", [P, 2, PACKED], F32R) for n in "hl"]
        x = [K.xh, K.xl]
        w_in, table_in, wo_in = [sem(f"w_in{c}") for c in range(NC_)], sem("table_in"), [sem(f"wo_in{n}") for n in range(2)]
        pool_step = sem("pool_step")
        w_hi, w_split, wo_split = sem("w_hi"), sem("w_split"), sem("wo_split")
        work_full, work_free = sem("work_full"), sem("work_free")
        proj_full, proj_taken = sem("proj_full"), sem("proj_taken")
        rotated_step, rotated, parts_step, parts_done = (
            sem(n) for n in ("rotated_step", "rotated", "parts_step", "parts"))
        scored, min_done, exp_done, recip_done, widened = (
            sem(n) for n in ("scored", "min", "exp", "recip", "widened"))
        values_step, values_done = sem("values_step"), sem("values")
        turned, pT_hi_done, pT_done = sem("turned"), sem("pT_hi"), sem("pT")
        divided, mixed, mixed_hi, mixed_taken, out_full, out_free = (
            sem(n) for n in ("divided", "mixed", "mixed_hi", "mixed_taken", "out", "out_free"))
        block = ctx.enter_context(nc.Block())

        def unit(i, b, j):
            return 8 * i + 4 * b + j

        def ends(i, b):
            at = isinstance(i, int)
            return at and i == 0 and b == 0, at and i == KV - 1 and b == 1

        def use(i, b, n):
            p = 2 * i + b
            if isinstance(p, int) and n < 3 and (p == 0 or (p, n) == (1, 0)):
                return 3 * p + n
            if isinstance(p, int) and n == 7 and p >= 2 * KV - 2:
                return 4 * (2 * KV - 1) + 2 + p - (2 * KV - 2)
            return 4 * p + {0: -2, 1: 0, 2: 1, 7: 7}[n]

        def before(i, b, j, n=1):
            return (i, b, j - n) if j >= n else (i, 0, j + 4 - n) if b else (i - 1, 1, j + 4 - n)

        def after(i, b, j):
            return (i, b, j + 1) if j < 3 else (i, 1, 0) if b == 0 else (i + 1, 0, 0)

        def loop(eng, body):
            body(0)
            with eng.Fori(1, KV - 1) as i:
                body(i)
            body(KV - 1)

        @block.sync
        def _(sp):
            for c in range(NC_):
                sp.dma_start(w_raw[:, c * KV * G0:(c + 1) * KV * G0], dram["w0"][:, c * KV * G0:(c + 1) * KV * G0]
                             ).then_inc(w_in[c], 16)
            sp.dma_start(cos[:], dram["cos"]).then_inc(table_in, 16)
            sp.dma_start(sin[:], dram["sin"]).then_inc(table_in, 16)
            for n in range(2):
                sp.dma_start(wo_raw[n], dram["wo0"][:, n * KV // 2:(n + 1) * KV // 2, :]).then_inc(wo_in[n], 16)

        @block.gpsimd
        def _(pool):
            step = Chain(pool, pool_step)
            for a in v:
                step(nc.gpsimd.memset(a[:].bitcast(F32), 0.0))
            for n in range(2):
                hi, lo = (a[:, n * KV // 2:(n + 1) * KV // 2, :] for a in wo)
                pool.wait_ge(wo_in[n], 16)
                step(nc.gpsimd.tensor_copy(hi, wo_raw[n]))
                nc.gpsimd.tensor_tensor(lo, wo_raw[n], hi.bitcast(F32), ALU.subtract).then_inc(wo_split, 1)

            def parts(i, b):
                p = 2 * i + b
                pool.wait_ge(rotated, p + 1)
                if not (isinstance(p, int) and p == 0):
                    pool.wait_ge(values_done, p)
                if not (isinstance(p, int) and p == 0):
                    new = (i, 0) if b else (i - 1, 1)
                    pool.wait_ge(work_full, use(*new, 2) + 1)
                zero = K.zero[:, 0:1].unsqueeze(2)
                q_in = rot[:, :, 0:GROUP, :]
                k_in = rot[:, :, GROUP:GROUP + 1, :].to_broadcast([P, TB, 2 * GROUP, HD0])
                q_hi = qs[:, :, :, 0, :]
                nc.gpsimd.tensor_tensor(q_hi.bitcast(F32R), q_in,
                                        zero.unsqueeze(3).to_broadcast([P, TB, GROUP, HD0]), ALU.add
                                        ).then_inc(parts_step, 1)
                nc.gpsimd.tensor_tensor(ks[0][:].bitcast(F32R), k_in,
                                        zero.unsqueeze(3).to_broadcast([P, TB, 2 * GROUP, HD0]), ALU.add
                                        ).then_inc(parts_step, 1)
                v_in = qkv[:, b * TB:(b + 1) * TB, bass.ds(i * G0 + (GROUP + 1) * HD0, HD0)]
                nc.gpsimd.tensor_tensor(v_in_hand[:], v_in, zero.to_broadcast([P, TB, HD0]), ALU.add
                                        ).then_inc(parts_step, 1)
                pool.wait_ge(parts_step, 3 * p + 3)
                nc.gpsimd.tensor_tensor(qs[:, :, :, 1, :].bitcast(F32R), q_in, q_hi, ALU.subtract
                                        ).then_inc(parts_done, 1)
                nc.gpsimd.tensor_tensor(ks[1][:].bitcast(F32R), k_in, ks[0][:], ALU.subtract
                                        ).then_inc(parts_done, 1)

            def value_parts(i, b):
                p = 2 * i + b
                v_in = v_in_hand[:]
                if not (isinstance(p, int) and p < 2):
                    pool.wait_ge(mixed, 4 * (p - 1))
                zero = K.zero[:, 0:1].unsqueeze(2).to_broadcast([P, TB, HD0])
                for a in v:
                    nc.gpsimd.tensor_tensor(a[:, b, :, 96:96 + HD0], v_in, zero, ALU.add).then_inc(values_step, 1)
                pool.wait_ge(values_step, 2 * p + 2)
                nc.gpsimd.tensor_tensor(v[0][:, b, :, 96 + HD0:128], v_in, v[0][:, b, :, 96:96 + HD0].bitcast(F32),
                                        ALU.subtract).then_inc(values_done, 1)

            def widen(i, b):
                p = 2 * i + b
                pool.wait_ge(recip_done, p + 1)
                if not (isinstance(p, int) and p == 0):
                    new = (i, 0) if b else (i - 1, 1)
                    pool.wait_ge(work_full, use(*new, 7) + 1)
                nc.gpsimd.tensor_tensor(wide[:], recip[:].unsqueeze(3).to_broadcast([P, TB, GROUP, 32]),
                                        K.zero[:, 0:1].unsqueeze(2).unsqueeze(3)
                                        .to_broadcast([P, TB, GROUP, 32]), ALU.add).then_inc(widened, 1)

            parts(0, 0)
            value_parts(0, 0)
            parts(0, 1)

            def body(i):
                for b in range(NB):
                    if not ends(i, b)[0]:
                        widen(*before(i, b, 0)[:2])
                    if not ends(i, b)[1]:
                        value_parts(*((i, 1) if b == 0 else (i + 1, 0)))
                    if not (isinstance(i, int) and i == KV - 1):
                        parts(i + 1, b)
            loop(pool, body)
            widen(KV - 1, 1)

        @block.tensor
        def _(pe):
            wv = [a.rearrange("p (c n) -> p c n", c=NC_) for a in w]

            half = KV * G0 // 2
            for n in range(2 * NT):
                t, h = divmod(n, 2)
                if n >= 2:
                    pe.wait_ge(proj_taken, n - 1)
                for c in range(NC_):
                    if n == 0:
                        pe.wait_ge(w_split, c + 1)
                    last = mm3(nc, (W, O)[h][:, 0:half], [a[:, c, t * P:(t + 1) * P] for a in x],
                               [a[:, c, h * half:(h + 1) * half] for a in wv], c == 0, c == NC_ - 1)
                last.then_inc(proj_full, 1)

            def turn(i, b, n):
                if not (ends(i, b)[0] and n == 0):
                    pe.wait_ge(work_free, use(i, b, n))
                if n == 0:
                    pe.wait_ge(parts_done, 2 * (2 * i + b) + 2)
                for t in range(TB):
                    src = (qs[:, t].rearrange("p h a d -> p (h a d)") if n == 0 else
                           ks[n - 1][:, t].rearrange("p h d -> p (h d)"))
                    last = nc.tensor.transpose(W[:, t * P:(t + 1) * P], src, K.ident[:])
                last.then_inc(work_full, 1)

            def scores(i, b, j):
                u = unit(i, b, j)
                if j == 0:
                    pe.wait_ge(work_free, use(i, b, 2) + 1)
                strip = slice(32 * j, 32 * j + 32)
                for n, group in enumerate(((3,), (2, 0), (1,))):
                    if not (ends(i, b)[0] and j == 0):
                        pe.wait_ge(exp_done, 4 * (u - 1) + (1, 3, 4)[n])
                    for qi in group:
                        keys = (qi + 1) * P
                        off = COL[qi] - 512 * n
                        out = S[n][:, off:off + keys]
                        for a in (0, 1):
                            nc.tensor.matmul(out, qT[strip, b, qi * P:(qi + 1) * P], kT[a][strip, b, 0:keys],
                                             start=a == 0 and qi == group[0], stop=False)
                    add_masks(nc, K, S, n).then_inc(scored, 1)

            def turn_probs(i, b, j):
                u = unit(i, b, j)
                pe.wait_ge(exp_done, 4 * (u + 1))
                for n, group in enumerate(((3,), (2, 0), (1,))):
                    if not (ends(i, b)[0] and j == 0):
                        pe.wait_ge(pT_done, 3 * (u - 1) + n + 1)
                    for back in group:
                        kj = 3 - back
                        off = COL[back] - 512 * n
                        for qi in range(kj, TB):
                            last = nc.tensor.transpose(
                                T[n][:, off + (qi - kj) * P:off + (qi - kj + 1) * P],
                                probs[:, j % 2 * PACKED + COL[qi] + kj * P:][:, 0:P], K.ident[:])
                    last.then_inc(turned, 1)

            def mix(i, b, j):
                if j == 0:
                    pe.wait_ge(values_done, 2 * i + b + 1)
                    if not ends(i, b)[0]:
                        pe.wait_ge(divided, 2 * i + b)
                pe.wait_ge(pT_done, 3 * unit(i, b, j) + 3)
                for kj in range(TB):
                    for a in (0, 1):
                        last = nc.tensor.matmul(O[:, kj * P:], v[a][:, b, kj, 96 - 32 * j:224 - 32 * j],
                                                pT[a][:, j % 2, COL[3 - kj]:COL[3 - kj] + (TB - kj) * P],
                                                start=j == 0 and kj == 0 and a == 0,
                                                stop=j == 3 and kj == 3 and a == 1)
                last.then_inc(mixed, 1)

            def turn_recips(i, b):
                pe.wait_ge(work_free, use(i, b, 7))
                pe.wait_ge(widened, 2 * i + b + 1)
                for t in range(TB):
                    last = nc.tensor.transpose(W[:, t * P:(t + 1) * P], wide[:, t].rearrange("p h n -> p (h n)"),
                                               K.ident[:])
                last.then_inc(work_full, 1)

            pe.wait_ge(proj_taken, 2 * NT)
            for n in range(3):
                turn(0, 0, n)
            scores(0, 0, 0)

            def body(i):
                for b in range(NB):
                    last = ends(i, b)[1]
                    for j in range(GROUP):
                        new = (i, 1) if b == 0 else (i + 1, 0)
                        if not (last and j == 3):
                            scores(*after(i, b, j))
                        if not last and j < 3:
                            turn(*new, j)
                        turn_probs(i, b, j)
                        if not (ends(i, b)[0] and j == 0):
                            mix(*before(i, b, j))
                            if j == 0:
                                turn_recips(*before(i, b, 0)[:2])
            loop(pe, body)
            mix(KV - 1, 1, 3)
            turn_recips(KV - 1, 1)

            pe.wait_ge(wo_split, 2)
            for t in range(NT):
                b, q = divmod(t, TB)
                if t == 0:
                    pe.wait_ge(exp_done, 4 * 64)
                if t == TB:
                    pe.wait_ge(mixed_taken, 2 * KV)
                if t == NT - 1:
                    pe.wait_ge(out_free, 1)
                for i in range(KV):
                    at = i * SEQ + q * P
                    last = mm3(nc, (S + T + [W, S[0]])[t][:], [a[:, at:at + P] for a in cT[b]],
                               [a[:, i, :] for a in wo], i == 0, i == KV - 1)
                last.then_inc(out_full, 1)

        @block.scalar
        def _(act):
            for c in range(NC_):
                act.wait_ge(w_in[c], 16)
                nc.scalar.activation(w[0][:, c * KV * G0:(c + 1) * KV * G0],
                                     w_raw[:, c * KV * G0:(c + 1) * KV * G0], ACT.Copy).then_inc(w_hi, 1)
            for n in range(2 * NT):
                t, h = divmod(n, 2)
                half = KV * G0 // 2
                act.wait_ge(proj_full, n + 1)
                if n == 0:
                    act.wait_ge(w_split, NC_)
                if t == NT // 2:
                    act.wait_ge(wo_split, 1)
                nc.scalar.activation(qkv[:, t, h * half:(h + 1) * half], (W, O)[h][:, 0:half], ACT.Copy
                                     ).then_inc(proj_taken, 1)

            def keep(i, b, n):
                act.wait_ge(work_full, use(i, b, n) + 1)
                if n == 7 and not (isinstance(i, int) and (i, b) == (0, 0)):
                    act.wait_ge(mixed_taken, 2 * i + b)
                dst = product[:] if n == 7 else (qT if n == 0 else kT[n - 1])[:, b, :]
                nc.scalar.activation(dst, W[:], ACT.Copy, scale=NEG if n == 0 else 1.0
                                     ).then_inc(work_free, 1)

            def exps(i, b, j):
                u = unit(i, b, j)
                for qi, minima in zip(ORDER, (1, 3, 3, 4)):
                    act.wait_ge(min_done, 4 * u + minima)
                    nc.scalar.activation(probs[:, j % 2 * PACKED + COL[qi]:j % 2 * PACKED + COL[qi] + (qi + 1) * P],
                                         S[SLOT[qi][0]][:, SLOT[qi][1]:SLOT[qi][1] + (qi + 1) * P],
                                         ACT.Exp, bias=negmax[:, j % 2, qi:qi + 1], scale=-1.0,
                                         accum_out=rowsum[:, b, qi, j:j + 1]).then_inc(exp_done, 1)

            for n in range(3):
                keep(0, 0, n)
            act.wait_ge(wo_split, 2)
            exps(0, 0, 0)

            def body(i):
                for b in range(NB):
                    last = ends(i, b)[1]
                    ni, nb = (i, 1) if b == 0 else (i + 1, 0)
                    for j in range(GROUP):
                        u = unit(i, b, j)
                        if not last and j < 3:
                            keep(ni, nb, j)
                        if not (last and j == 3):
                            exps(*after(i, b, j))
                        for n in range(3):
                            act.wait_ge(turned, 3 * u + n + 1)
                            s = slice(512 * n, min(512 * (n + 1), PACKED))
                            nc.scalar.activation(pT[0][:, j % 2, s], T[n][:, 0:s.stop - s.start], ACT.Copy
                                                 ).then_inc(pT_hi_done, 1)
                        if j == 0 and not ends(i, b)[0]:
                            keep(*before(i, b, 0)[:2], 7)
            loop(act, body)
            keep(KV - 1, 1, 7)

        @block.vector
        def _(dve):
            def rotate(i, b, n):
                p = 2 * i + b
                qk = (qkv[:, b * TB:(b + 1) * TB, bass.ds(i * G0, (GROUP + 1) * HD0)]
                      .rearrange("p t (h d) -> p t h d", d=HD0))
                half = HD0 // 2

                def table(t, lo, hi):
                    return t[:, :, lo:hi].unsqueeze(2).to_broadcast([P, TB, GROUP + 1, hi - lo])
                if n == 0:
                    if not (isinstance(p, int) and p == 0):
                        dve.wait_ge(parts_done, 2 * p)
                    if isinstance(p, int) and p < 2:
                        dve.wait_ge(proj_taken, (b + 1) * NT)
                    nc.vector.tensor_tensor(rot[:], qk, table(cos, 0, HD0), ALU.mult).then_inc(rotated_step, 1)
                elif n == 1:
                    nc.vector.tensor_tensor(rot2[:, :, :, 0:half], qk[:, :, :, half:], table(sin, 0, half),
                                            ALU.mult).then_inc(rotated_step, 1)
                    nc.vector.tensor_tensor(rot2[:, :, :, half:], qk[:, :, :, 0:half], table(sin, half, HD0),
                                            ALU.mult).then_inc(rotated_step, 1)
                else:
                    dve.wait_ge(rotated_step, 3 * p + 3)
                    nc.vector.tensor_tensor(rot[:], rot[:], rot2[:], ALU.add).then_inc(rotated, 1)

            def minima(i, b, j):
                u = unit(i, b, j)
                for qi, need in zip(ORDER, (1, 2, 2, 3)):
                    dve.wait_ge(scored, 3 * u + need)
                    nc.vector.tensor_reduce(negmax[:, j % 2, qi:qi + 1],
                                            S[SLOT[qi][0]][:, SLOT[qi][1]:SLOT[qi][1] + (qi + 1) * P],
                                            AX_X, ALU.min).then_inc(min_done, 1)

            def reciprocals(i, b):
                p = 2 * i + b
                dve.wait_ge(exp_done, 4 * 4 * (p + 1))
                if not (isinstance(p, int) and p == 0):
                    dve.wait_ge(widened, p)
                nc.vector.reciprocal(recip[:], rowsum[:, b]).then_inc(recip_done, 1)

            for c in range(NC_):
                s = slice(c * KV * G0, (c + 1) * KV * G0)
                dve.wait_ge(w_hi, c + 1)
                nc.vector.tensor_tensor(w[1][:, s], w_raw[:, s], w[0][:, s].bitcast(F32), ALU.subtract
                                        ).then_inc(w_split, 1)
            dve.wait_ge(table_in, 32)
            for b in range(NB):
                for n in range(3):
                    rotate(0, b, n)
            minima(0, 0, 0)

            def divide(i, b):
                p = 2 * i + b
                dve.wait_ge(mixed, 4 * p + 4)
                dve.wait_ge(work_free, use(i, b, 7) + 1)
                nc.vector.tensor_tensor(product[:], O[:], product[:], ALU.mult).then_inc(divided, 1)

            def take_hi(i, b):
                p = 2 * i + b
                hi = cT[b][0][:, bass.ds(i * SEQ, SEQ)]
                dve.wait_ge(divided, p + 1)
                nc.vector.tensor_tensor(hi, product[:], K.zero[:, 0:1].to_broadcast([P, SEQ]), ALU.add
                                        ).then_inc(mixed_hi, 1)

            def take_lo(i, b):
                p = 2 * i + b
                hi, lo = (a[:, bass.ds(i * SEQ, SEQ)] for a in cT[b])
                dve.wait_ge(mixed_hi, p + 1)
                nc.vector.tensor_tensor(lo, product[:], hi.bitcast(F32), ALU.subtract).then_inc(mixed_taken, 1)

            def body(i):
                for b in range(NB):
                    last = ends(i, b)[1]
                    for j in range(GROUP):
                        u = unit(i, b, j)
                        if j < 2 and not ends(i, b)[0]:
                            (reciprocals, divide)[j](*before(i, b, 0)[:2])
                        if not (last and j == 3):
                            minima(*after(i, b, j))
                        if j < 3 and not (isinstance(i, int) and i == KV - 1):
                            rotate(i + 1, b, j)
                        if j > 1 and not ends(i, b)[0]:
                            (take_hi, take_lo)[j - 2](*before(i, b, 0)[:2])
                        for n in range(3):
                            dve.wait_ge(pT_hi_done, 3 * u + n + 1)
                            s = slice(512 * n, min(512 * (n + 1), PACKED))
                            nc.vector.tensor_tensor(pT[1][:, j % 2, s], T[n][:, 0:s.stop - s.start],
                                                    pT[0][:, j % 2, s].bitcast(F32), ALU.subtract
                                                    ).then_inc(pT_done, 1)
            loop(dve, body)
            reciprocals(KV - 1, 1)
            for take in (divide, take_hi, take_lo):
                take(KV - 1, 1)
            for t in range(NT):
                dve.wait_ge(out_full, t + 1)
                xt = K.xs[:, t, :]
                done = nc.vector.tensor_tensor(xt, xt, (S + T + [W, S[0]])[t][:], ALU.add)
                if t == 0:
                    done.then_inc(out_free, 1)


FF = 1376
NF = -(-FF // P)


def gated_ffn_stage(nc, K, dram, pre):
    with ExitStack() as ctx:
        m = Memory(nc, ctx, pre)
        sb, sem = m.sb, m.sem
        bank = [[[m.ps(f"bank{s}{w}{b}") for b in range(NB)] for w in range(2)] for s in range(2)]
        raw = sb("raw", [P, 2, 2 * NC_ * P], I32)
        wgu = sb("wgu", [P, 2, 2, NC_, P], F32R)
        down = sb("down", [P, NF, D], F32R)
        down_raw = sb("down_raw", [P, 2, D], I32)
        scales = sb("scales", [P, NF, 2])
        gate_scale = sb("gate_scale", [P, 2])
        down_scale, scaled = sb("down_scale", [P, D]), sb("scaled", [P, 2, D])
        silu = sb("silu", [P, 2, TOK])
        h = sb("h", [P, TOK])
        hT = [sb(f"hT{n}", [P, NF, TOK], F32R) for n in "hl"]
        raw_in, scale_in, down_in = [sem("raw_in0"), sem("raw_in1")], sem("scale_in"), [sem("down_in0"), sem("down_in1")]
        w_ready, down_ready = sem("w_ready"), sem("down_ready")
        full, gate_taken, gate_scaled, h_step, h_done = (
            sem(n) for n in ("full", "gate_taken", "gate_scaled", "h_step", "h_done"))
        out_full, out_step, out_done = sem("out_full"), sem("out_step"), sem("out_done")
        down_scale_in = sem("down_scale_in")
        block = ctx.enter_context(nc.Block())
        x = [K.xh, K.xl]

        def loop(eng, body):
            body(0, 0)
            body(1, 1)
            with eng.Fori(2, NF - 1, 2) as f:
                body(f, 0)
                body(f + 1, 1)
            body(NF - 1, (NF - 1) % 2)

        @block.sync
        def _(sp):
            sp.dma_start(scales[:], dram["gu_scale"]).then_inc(scale_in, 16)

            def body(f, s):
                if not (isinstance(f, int) and f < 2):
                    sp.wait_ge(w_ready, f - 1)
                row = bass.ds(f, 1)
                sp.dma_start(raw[:, s, :], dram["gu"][row, :, :].rearrange("a p n -> p (a n)")
                             ).then_inc(raw_in[s], 16)
                if isinstance(f, int) and f == 1:
                    sp.dma_start(down_scale[:], dram["down_scale"]).then_inc(down_scale_in, 16)
                if not (isinstance(f, int) and f < 2):
                    sp.wait_ge(down_ready, f - 1)
                sp.dma_start(down_raw[:, s, :], dram["down"][row, :, :].rearrange("a p n -> p (a n)")
                             ).then_inc(down_in[s], 16)
            loop(sp, body)

        @block.gpsimd
        def _(pool):
            for f in range(NF):
                pool.wait_ge(down_in[f % 2], 16 * (f // 2 + 1))
                nc.gpsimd.tensor_copy(down[:, f, :], down_raw[:, f % 2, :]).then_inc(down_ready, 1)

        @block.tensor
        def _(pe):
            def body(f, s):
                pe.wait_ge(w_ready, f + 1)
                for w in range(2):
                    if not (isinstance(f, int) and f < 2):
                        if w == 0:
                            pe.wait_ge(gate_taken, f - 1)
                        else:
                            pe.wait_ge(h_step, 2 * (f - 2) + 2)
                    for c in range(NC_):
                        for a in range(2):
                            for b in range(NB):
                                last = nc.tensor.matmul(bank[s][w][b][:], wgu[:, s, w, c, :],
                                                        x[a][:, c, b * SEQ:(b + 1) * SEQ],
                                                        start=c == 0 and a == 0, stop=c == NC_ - 1 and a == 1)
                    last.then_inc(full, 1)
            loop(pe, body)
            pe.wait_ge(down_ready, NF)
            flat = [bank[s][w][b] for s in range(2) for w in range(2) for b in range(NB)]
            pe.wait_ge(h_done, NF)
            for t in range(NT):
                for f in range(NF):
                    for a in range(2):
                        last = nc.tensor.matmul(flat[t][:], hT[a][:, f, t * P:(t + 1) * P], down[:, f, :],
                                                start=f == 0 and a == 0, stop=f == NF - 1 and a == 1)
                last.then_inc(out_full, 1)

        @block.scalar
        def _(act):
            def body(f, s):
                if not (isinstance(f, int) and f < 2):
                    act.wait_ge(h_step, 2 * (f - 2) + 2)
                act.wait_ge(gate_scaled, f + 1)
                act.wait_ge(full, 2 * f + 1)
                nc.scalar.activation(silu[:, s, 0:SEQ], bank[s][0][0][:], ACT.Silu, scale=gate_scale[:, s:s + 1])
                nc.scalar.activation(silu[:, s, SEQ:], bank[s][0][1][:], ACT.Silu, scale=gate_scale[:, s:s + 1]
                                     ).then_inc(gate_taken, 1)
            loop(act, body)

        @block.vector
        def _(dve):
            dve.wait_ge(scale_in, 16)

            def prepare(f, s):
                if not (isinstance(f, int) and f < 2):
                    dve.wait_ge(gate_taken, f - 1)
                nc.vector.tensor_scalar(gate_scale[:, s:s + 1], scales[:, bass.ds(f, 1), 0:1]
                                        .rearrange("p a b -> p (a b)"), 1.0, None, ALU.mult
                                        ).then_inc(gate_scaled, 1)
                dve.wait_ge(raw_in[s], 16 * count(f, s))
                if not (isinstance(f, int) and f < 2):
                    dve.wait_ge(full, 2 * (f - 2) + 2)
                nc.vector.tensor_copy(wgu[:, s].rearrange("p w c n -> p (w c n)"), raw[:, s, :]
                                      ).then_inc(w_ready, 1)

            marks = {}

            def count(f, s):
                return f // 2 + 1 if isinstance(f, int) else marks["k"] + 1

            def hidden(f):
                s = marks["s"]
                dve.wait_ge(gate_taken, f + 1)
                dve.wait_ge(full, 2 * f + 2)
                if not (isinstance(f, int) and f == 0):
                    dve.wait_ge(h_done, f)
                for b in range(NB):
                    cols = slice(b * SEQ, (b + 1) * SEQ)
                    nc.vector.scalar_tensor_tensor(
                        out=h[:, cols], in0=bank[s][1][b][:],
                        scalar=scales[:, bass.ds(f, 1), 1:2].rearrange("p a b -> p (a b)"),
                        in1=silu[:, s, cols], op0=ALU.mult, op1=ALU.mult).then_inc(h_step, 1)
                dve.wait_ge(h_step, 2 * f + 2)
                hi = hT[0][:, bass.ds(f, 1), :].rearrange("p a n -> p (a n)")
                nc.vector.tensor_scalar(hi, h[:], 1.0, None, ALU.mult).then_inc(hi_done, 1)
                dve.wait_ge(hi_done, f + 1)
                nc.vector.tensor_tensor(hT[1][:, bass.ds(f, 1), :].rearrange("p a n -> p (a n)"), h[:],
                                        hi.bitcast(F32), ALU.subtract).then_inc(h_done, 1)
            hi_done = sem("hi_done")
            prepare(0, 0)
            prepare(1, 1)
            marks["s"] = 0
            hidden(0)
            prepare(2, 0)
            marks["s"] = 1
            hidden(1)
            prepare(3, 1)
            with dve.Fori(1, (NF - 1) // 2 - 1) as k:
                for s in range(2):
                    marks["s"] = s
                    marks["k"] = k + 1
                    hidden(2 * k + s)
                    prepare(2 * k + s + 2, s)
            for f in range(NF - 3, NF):
                marks["s"] = f % 2
                hidden(f)
                if f == NF - 3:
                    prepare(NF - 1, (NF - 1) % 2)
            flat = [bank[s][w][b] for s in range(2) for w in range(2) for b in range(NB)]
            dve.wait_ge(down_scale_in, 16)
            for t in range(NT):
                dve.wait_ge(out_full, t + 1)
                nc.vector.tensor_tensor(scaled[:, t % 2, :], flat[t][:], down_scale[:], ALU.mult
                                        ).then_inc(out_step, 1)
                dve.wait_ge(out_step, t + 1)
                nc.vector.tensor_tensor(K.xs[:, t, :], K.xs[:, t, :], scaled[:, t % 2, :], ALU.add
                                        ).then_inc(out_done, 1)


RAW_SLOTS = 2
PIECES = 10
RMS_EPS = 1e-6


def attention_stage(nc, K, dram, kind, pre):
    NEG = -float(P) ** -0.5
    with ExitStack() as ctx:
        m = Memory(nc, ctx, pre)
        sb, sem = m.sb, m.sem
        S = [m.ps(f"scores{n}") for n in range(3)]
        T = [m.ps(f"turned{n}") for n in range(2)]
        O = m.ps("mixed")
        WB = [m.ps(f"work{n}") for n in range(2)]
        T.append(S[2][:, 256:])
        probs = sb("probs", [P, 2, PACKED])
        negmax, rowsum, recip = (sb(n, [P, 2, 4]) for n in ("negmax", "rowsum", "recip"))
        pT = [sb(f"pT{n}", [P, PACKED], F32R) for n in "hl"]
        raw_in = [sem(f"raw_in{n}") for n in range(RAW_SLOTS)]
        raw_split = sem("raw_split")
        pool_step = sem("pool_step")
        work_full, work_hi, work_free = sem("work_full"), sem("work_hi"), sem("work_free")
        scored, min_done, exp_done, recip_done, scaled = (
            sem(n) for n in ("scored", "min", "exp", "recip", "scaled"))
        turned, pT_hi_done, pT_done = sem("turned"), sem("pT_hi"), sem("pT")
        mixed, mixed_hi, mixed_done = sem("mixed"), sem("mixed_hi"), sem("mixed_done")

        raw = sb("raw", [P, RAW_SLOTS, 512])
        wq = [sb(f"wq{n}", [P, GROUP, NC_, P], F32R) for n in "hl"]
        wkv = [sb(f"wkv{n}", [P, NC_, 2, P], F32R) for n in "hl"]
        wk, wv = ([a[:, :, n, :] for a in wkv] for n in range(2))
        wd = [sb(f"wd{n}", [P, GROUP, D], F32R) for n in "hl"]
        q = [sb(f"q{n}", [P, 2, GROUP, SEQ], F32R) for n in "hl"]
        k = [sb(f"k{n}", [P, NB, SEQ], F32R) for n in "hl"]
        v = [sb(f"v{n}", [P, NB, TB, P], F32R) for n in "hl"]
        ctxT = [sb(f"c{n}", [P, NB, GROUP, SEQ], F32R) for n in "hl"]
        x = [K.xh, K.xl]
        if kind == 1:
            v_raw = sb("v_raw", [P, 512])
            to_turn = {"VT": v_raw}
        else:
            square = sb("square", [P, 512])
            square_k = sb("square_k", [P, TB * P])
            sumsq, rms, qkw = sb("sumsq", [P, 4]), sb("rms", [P, 4]), sb("qkw", [P, 2])
            tab, pick = sb("tab", [3 * GROUP, SEQ], BF16), sb("pick", [3 * GROUP, GROUP, P], BF16)
            square_done, sumsq_done, mean_done, rms_done = (
                sem(n) for n in ("square", "sumsq", "mean", "rms"))
            qkw_in, pick_in, tab_in = sem("qkw_in"), sem("pick_in"), sem("tab_in")
            qkw_done = sem("qkw_done")
            to_turn = {"QT": square, "KT": square_k}
            raw_q = sb("raw_q", [P, GROUP, 512])
            raw_q_in, wq_hi, wq_split = sem("raw_q_in"), sem("wq_hi"), sem("wq_split")
        block = ctx.enter_context(nc.Block())

        def ends(i, b):
            at = isinstance(i, int)
            return at and i == 0 and b == 0, at and i == KV - 1 and b == 1

        OUT_TILES = ((), (0,), (1,), (2, 3))

        def uses(i, b, j):
            first, last = ends(i, b)
            out = [] if first else [f"D{t}" for t in OUT_TILES[j]]
            if last:
                return out
            if j == 0:
                return ["Q", "K"] if kind == 1 else ["Q", "QT", "KV0", "KV1"]
            if kind == 2:
                return ["Q"] + ["KT"] * (j == 1) + out + ["QT"]
            return ["Q"] + ["VT"] * (j == 3) + out + ["V"] * (j == 2)

        PROLOGUE = ["Q"] * 4 + ["K", "V", "VT"] if kind == 1 else ["Q", "QT"] * 4 + ["KV0", "KV1", "KT"]
        PRO = len(PROLOGUE)

        def start(i, b):
            return PRO if ends(i, b)[0] else (PRO + 4) * (2 * i + b) + PRO - 4

        def use(i, b, j, name):
            if isinstance(i, int) and i == -1:
                return [n for n, o in enumerate(PROLOGUE) if o == name][j if name in ("Q", "QT") else 0]
            return start(i, b) + sum(len(uses(i, b, jj)) for jj in range(j)) + uses(i, b, j).index(name)

        def work(i, b, j, name):
            return WB[use(i if isinstance(i, int) else 1, b, j, name) % 2]

        def before(i, b, j):
            return (i, b, j - 1) if j else (i, 0, 3) if b else (i - 1, 1, 3)

        def unit(i, b, j):
            return 8 * i + 4 * b + j

        STREAM = [0, 4, 1, 2, 5, 3] if kind == 1 else [4, 5]
        FIRST, PER = len(STREAM), len(STREAM) + GROUP
        SPLIT_AT = ({(0, 0): (0, 4), (0, 1): (1,), (0, 2): (2, 5), (0, 3): (3, 6), (1, 0): (7, 8, 9)} if kind == 1
                    else {(0, 1): (4,), (0, 2): (5,), (0, 3): (6, 7), (1, 0): (8, 9)})

        def piece(g, n):
            if n < 6:
                return (sorted(STREAM).index(n) if isinstance(g, int) and g == 0
                        else FIRST + PER * (g - 1) + STREAM.index(n))
            return FIRST + PER * g + (n - 6 if isinstance(g, int) and g == KV - 1 else FIRST + n - 6)

        def stream(i):
            last = isinstance(i, int) and i == KV - 1
            out = [] if last else [(i + 1, n, FIRST + at) for at, n in enumerate(STREAM)]
            return out + [(i, n, FIRST + n - 6 + (0 if last else FIRST)) for n in range(6, PIECES)]

        def arrivals(i, place):
            return (PER // RAW_SLOTS) * i + place // RAW_SLOTS + 1

        def loop(eng, body):
            body(0)
            with eng.Fori(1, KV - 1) as i:
                body(i)
            body(KV - 1)

        @block.sync
        def _(sp):
            w = dram["w"]
            if kind == 2:
                sp.dma_start(qkw[:], dram["qkw"]).then_inc(qkw_in, 16)

            def load(i, g, n, place):
                if not (isinstance(i, int) and i == 0 and place < RAW_SLOTS):
                    sp.wait_ge(raw_split, PER * i + place - RAW_SLOTS + 1)
                sp.dma_start(raw[:, place % RAW_SLOTS, :],
                             w[bass.ds(PIECES * g + n, 1), :, :].rearrange("a p n -> p (a n)")
                             ).then_inc(raw_in[place % RAW_SLOTS], 16)

            def load_q(g):
                if not (isinstance(g, int) and g == 0):
                    sp.wait_ge(wq_split, g)
                sp.dma_start(raw_q[:], w[bass.ds(PIECES * g, GROUP), :, :].rearrange("a p n -> p a n")
                             ).then_inc(raw_q_in, 16)

            if kind == 2:
                load_q(0)
            for place, n in enumerate(sorted(STREAM)):
                load(0, 0, n, place)

            def body(i):
                if kind == 2 and not (isinstance(i, int) and i == KV - 1):
                    load_q(i + 1)
                for g, n, place in stream(i):
                    load(i, g, n, place)
            loop(sp, body)

        @block.gpsimd
        def _(pool):
            parts = [(wq, j) for j in range(4)] + [(wk, None), (wv, None)] + [(wd, j) for j in range(4)]

            def split(i, n, place):
                pool.wait_ge(raw_in[place % RAW_SLOTS], 16 * arrivals(i, place))
                pair, j = parts[n]
                hi, lo = (t[:, j] if j is not None else t for t in pair)
                if n >= 6:
                    hi, lo = (t.rearrange("p (c d) -> p c d", c=NC_) for t in (hi, lo))
                src = raw[:, place % RAW_SLOTS, :].rearrange("p (c d) -> p c d", c=NC_)
                zero = K.zero[:, 0:1].unsqueeze(2).to_broadcast([P, NC_, P])
                nc.gpsimd.tensor_tensor(hi, src, zero, ALU.add
                                        ).then_inc(pool_step, 1)
                pool.wait_ge(pool_step, PER * i + place + 1)
                nc.gpsimd.tensor_tensor(lo, src, hi.bitcast(F32), ALU.subtract).then_inc(raw_split, 1)

            def ran(i, b, j, name):
                pool.wait_ge(work_full, use(i, b, j, name) + 1)

            def scale(i, b, j):
                pool.wait_ge(recip_done, unit(i, b, j) + 1)
                for qi in ORDER:
                    pr = probs[:, j % 2, COL[qi]:COL[qi] + (qi + 1) * P]
                    nc.gpsimd.tensor_tensor(pr, pr, recip[:, j % 2, qi:qi + 1].to_broadcast([P, (qi + 1) * P]),
                                            ALU.mult).then_inc(scaled, 1)

            def root(n, s=slice(0, 4)):
                pool.wait_ge(mean_done, n + 1)
                nc.gpsimd.tensor_tensor(rms[:, s], sumsq[:, s], K.half[:, s], ALU.pow).then_inc(rms_done, 1)

            def load_tab(g):
                pool.dma_start(tab[:], dram["tab"][bass.ds(g, 1), :, :].rearrange("a r n -> r (a n)")
                               ).then_inc(tab_in, 16)

            def body(i):
                for b in range(NB):
                    last = ends(i, b)[1]
                    for j in range(GROUP):
                        scale(i, b, j)
                        if kind == 2 and not last:
                            root(6 + 12 * i + 6 * b + (j and j + 2))
                        if kind == 2 and not last and j == 0:
                            for n in range(2):
                                root(6 + 12 * i + 6 * b + 1 + n, slice(2 * n, 2 * n + 2))
                        if kind == 2 and b == 1 and j == 2 and not last:
                            pool.wait_ge(scored, 3 * unit(i, 1, 4))
                            load_tab(i + 1)
                        for g, n, place in stream(i):
                            if n in SPLIT_AT.get((b, j), ()):
                                at = {4: (0, "K" if kind == 1 else "KV1"), 5: (2, "V") if kind == 1 else None,
                                      6: None if isinstance(i, int) and i == 0 else (3, "D3")}.get(n)
                                if n < 4:
                                    at = (n, "Q")
                                if at:
                                    ran(i, 0, *at)
                                split(i, n, place)

            if kind == 2:
                pool.dma_start(pick[:], dram["pick"]).then_inc(pick_in, 16)
                load_tab(0)
            for place, n in enumerate(sorted(STREAM)):
                split(0, n, place)
            if kind == 2:
                for n in range(4):
                    root(n)
                for n in range(2):
                    root(4 + n, slice(2 * n, 2 * n + 2))
            loop(pool, body)

        @block.tensor
        def _(pe):
            def bank(n):
                if not (isinstance(n, int) and n < 2):
                    pe.wait_ge(work_free, n - 1)

            def weights(g, n):
                pe.wait_ge(raw_split, piece(g, n) + 1)

            def project_q(i, b, j, g, nb):
                W = work(i, b, j, "Q")
                bank(use(i, b, j, "Q"))
                if kind == 1:
                    weights(g, j)
                    for c in range(NC_):
                        last = mm3(nc, W[:], [w[:, j, c, :] for w in wq],
                                   [a[:, c, nb * SEQ:(nb + 1) * SEQ] for a in x], c == 0, c == NC_ - 1)
                else:
                    pe.wait_ge(wq_split, g + 1)
                    t = nb * TB + j
                    for c in range(NC_):
                        last = mm3(nc, W[:].rearrange("p (h d) -> p h d", h=GROUP),
                                   [a[:, c, t * P:(t + 1) * P] for a in x],
                                   [w[:, :, c, :] for w in wq], c == 0, c == NC_ - 1)
                last.then_inc(work_full, 1)

            def project_feature(w, i, b, j, name, g, nb, pc):
                W = work(i, b, j, name)
                bank(use(i, b, j, name))
                weights(g, pc)
                for c in range(NC_):
                    last = mm3(nc, W[:], [y[:, c, :] for y in w],
                               [a[:, c, nb * SEQ:(nb + 1) * SEQ] for a in x], c == 0, c == NC_ - 1)
                last.then_inc(work_full, 1)

            def project_kv(i, b, j, g, nb, n):
                W = work(i, b, j, f"KV{n}")
                bank(use(i, b, j, f"KV{n}"))
                weights(g, 5)
                for t in range(2):
                    s = slice((nb * TB + 2 * n + t) * P, (nb * TB + 2 * n + t + 1) * P)
                    for c in range(NC_):
                        last = mm3(nc, W[:, 2 * t * P:2 * (t + 1) * P], [a[:, c, s] for a in x],
                                   [a[:, c].rearrange("p k d -> p (k d)") for a in wkv], c == 0, c == NC_ - 1)
                last.then_inc(work_full, 1)

            def turn(i, b, j, name):
                W = work(i, b, j, name)
                bank(use(i, b, j, name))
                at = {"QT": (j, "Q"), "KT": (0, "KV1"), "VT": (2, "V")}[name]
                pe.wait_ge(work_free, use(i, b, *at) + 1)
                for h in range(4):
                    src = to_turn[name][:, h * P:(h + 1) * P]
                    last = nc.tensor.transpose(W[:, h * P:(h + 1) * P], src, K.ident[:])
                last.then_inc(work_full, 1)

            def scores(i, b, j):
                u = unit(i, b, j)
                if j == 0:
                    pe.wait_ge(work_free, start(i, b))
                    if kind == 2:
                        pe.wait_ge(tab_in, 16 * (i + 1))
                        if ends(i, b)[0]:
                            pe.wait_ge(pick_in, 16)
                for n, group in enumerate(((3,), (2, 0), (1,))):
                    if not (ends(i, b)[0] and j == 0):
                        pe.wait_ge(exp_done, 4 * (u - 1) + (1, 3, 4)[n])
                    if n == 2 and not (ends(i, b)[0] and j < 2):
                        pe.wait_ge(pT_done, 3 * (u - 1 if j else u))
                    for qi in group:
                        keys = (qi + 1) * P
                        off = COL[qi] - 512 * n
                        out = S[n][:, off:off + keys]
                        mm3(nc, out, [a[:, b, j, qi * P:(qi + 1) * P] for a in q],
                            [a[:, b, 0:keys] for a in k], qi == group[0], False)
                        if kind == 2:
                            nc.tensor.matmul(out, pick[:, j, :], tab[:, SEQ - keys:SEQ],
                                             start=False, stop=False)
                    add_masks(nc, K, S, n).then_inc(scored, 1)

            def turn_probs(i, b, j):
                u = unit(i, b, j)
                pe.wait_ge(scaled, 4 * (u + 1))
                for n, group in enumerate(((3,), (2, 0), (1,))):
                    if not (ends(i, b)[0] and j == 0):
                        pe.wait_ge(pT_done, 3 * (u - 1) + n + 1)
                    if n == 2 and j < 3:
                        pe.wait_ge(exp_done, 4 * (u + 2))
                    for back in group:
                        kj = 3 - back
                        off = COL[back] - 512 * n
                        for qi in range(kj, TB):
                            last = nc.tensor.transpose(
                                T[n][:, off + (qi - kj) * P:off + (qi - kj + 1) * P],
                                probs[:, j % 2, COL[qi] + kj * P:COL[qi] + (kj + 1) * P], K.ident[:])
                    last.then_inc(turned, 1)

            def mix(i, b, j):
                u = unit(i, b, j)
                if not (ends(i, b)[0] and j == 0):
                    pe.wait_ge(mixed_done, u)
                for kj, bank_n in ((0, 0), (1, 1), (3, 1), (2, 2)):
                    pe.wait_ge(pT_done, 3 * u + bank_n + 1)
                    cols = slice(COL[3 - kj], COL[3 - kj] + (TB - kj) * P)
                    last = mm3(nc, O[:, kj * P:], [a[:, b, kj, :] for a in v], [a[:, cols] for a in pT],
                               kj == 0, kj == 2)
                last.then_inc(mixed, 1)

            def project_out(i, b, j, t):
                pi, pb = (i, 0) if b == 1 else (i - 1, 1)
                W = work(i, b, j, f"D{t}")
                bank(use(i, b, j, f"D{t}"))
                if t == 0:
                    weights(pi, PIECES - 1)
                    pe.wait_ge(mixed_done, unit(pi, pb, 4))
                for h in range(GROUP):
                    last = mm3(nc, W[:], [a[:, pb, h, t * P:(t + 1) * P] for a in ctxT],
                               [w[:, h, :] for w in wd], h == 0, h == GROUP - 1)
                last.then_inc(work_full, 1)

            def body(i):
                for b in range(NB):
                    first, last = ends(i, b)
                    g, nb = (i, 1) if b == 0 else (i + 1, 0)
                    scores(i, b, 0)
                    for j in range(GROUP):
                        if not last:
                            project_q(i, b, j, g, nb)
                        if j < 3:
                            scores(i, b, j + 1)
                        if not (first and j == 0):
                            mix(*before(i, b, j))
                        turn_probs(i, b, j)
                        if kind == 2 and j == 1 and not last:
                            turn(i, b, j, "KT")
                        if kind == 1 and j == 3 and not last:
                            turn(i, b, j, "VT")
                        if not first:
                            for t in OUT_TILES[j]:
                                project_out(i, b, j, t)
                        if kind == 2 and not last:
                            turn(i, b, j, "QT")
                            for n in range(2 if j == 0 else 0):
                                project_kv(i, b, j, g, nb, n)
                        if kind == 1 and j == 0 and not last:
                            project_feature(wk, i, b, j, "K", g, nb, 4)
                        if kind == 1 and j == 2 and not last:
                            project_feature(wv, i, b, j, "V", g, nb, 5)

            for j in range(GROUP):
                project_q(-1, 0, j, 0, 0)
                if kind == 2:
                    turn(-1, 0, j, "QT")
            if kind == 2:
                for n in range(2):
                    project_kv(-1, 0, 0, 0, 0, n)
                turn(-1, 0, 0, "KT")
            else:
                project_feature(wk, -1, 0, 0, "K", 0, 0, 4)
                project_feature(wv, -1, 0, 0, "V", 0, 0, 5)
                turn(-1, 0, 0, "VT")
            loop(pe, body)
            mix(KV - 1, 1, 3)
            weights(KV - 1, PIECES - 1)
            pe.wait_ge(mixed_done, unit(KV - 1, 1, 4))
            for j in range(TB):
                dst = (S + T)[j]
                for h in range(GROUP):
                    last = mm3(nc, dst[:], [a[:, 1, h, j * P:(j + 1) * P] for a in ctxT],
                               [w[:, h, :] for w in wd], h == 0, h == GROUP - 1)
                last.then_inc(work_full, 1)

        FINAL = (PRO + 4) * (2 * KV - 1) + PRO - 4 + 4

        @block.scalar
        def _(act):
            def high(i, b, j, name, dst, scale):
                act.wait_ge(work_full, use(i, b, j, name) + 1)
                src = work(i, b, j, name)[:]
                if len(dst.shape) == 3:
                    src = src.rearrange("p (a b) -> p a b", a=4)
                nc.scalar.activation(dst, src, ACT.Copy, scale=scale).then_inc(work_hi, 1)

            def squares(i, b, j, name):
                act.wait_ge(work_full, use(i, b, j, name) + 1)
                nc.scalar.activation(square[:], work(i, b, j, name)[:], ACT.Square).then_inc(square_done, 1)

            def split_q(g):
                act.wait_ge(raw_q_in, 16 * (g + 1))
                nc.scalar.activation(wq[0][:].rearrange("p j c n -> p (j c n)"),
                                     raw_q[:].rearrange("p j n -> p (j n)"), ACT.Copy).then_inc(wq_hi, 1)

            def exps(i, b, j):
                u = unit(i, b, j)
                for qi, minima in zip(ORDER, (1, 3, 3, 4)):
                    act.wait_ge(min_done, 4 * u + minima)
                    nc.scalar.activation(probs[:, j % 2, COL[qi]:COL[qi] + (qi + 1) * P],
                                         S[SLOT[qi][0]][:, SLOT[qi][1]:SLOT[qi][1] + (qi + 1) * P],
                                         ACT.Exp, bias=negmax[:, j % 2, qi:qi + 1], scale=-1.0,
                                         accum_out=rowsum[:, j % 2, qi:qi + 1]).then_inc(exp_done, 1)

            def queries(i, b, j, nb):
                if kind == 1:
                    high(i, b, j, "Q", q[0][:, nb, j, :], NEG)
                else:
                    squares(i, b, j, "Q")

            def keys_values(i, b, j, nb, n):
                src = work(i, b, j, f"KV{n}")[:].rearrange("p (t k d) -> p t k d", t=2, k=2)
                act.wait_ge(work_full, use(i, b, j, f"KV{n}") + 1)
                nc.scalar.activation(square_k[:].rearrange("p (t d) -> p t d", t=TB)[:, 2 * n:2 * n + 2, :],
                                     src[:, :, 0, :], ACT.Square
                                     ).then_inc(square_done, 1)
                nc.scalar.activation(v[0][:, nb, 2 * n:2 * n + 2, :], src[:, :, 1, :], ACT.Copy
                                     ).then_inc(work_hi, 1)

            def keys(i, b, j, nb):
                high(i, b, j, "K", k[0][:, nb, :], 1.0)

            def values(i, b, j, nb):
                high(i, b, j, "VT", v[0][:, nb, :, :], 1.0)

            def turned_q(i, b, j, nb):
                high(i, b, j, "QT", q[0][:, nb, :, j * P:(j + 1) * P], qkw[:, 0:1])

            def turned_k(i, b, j, nb):
                high(i, b, j, "KT", k[0][:, nb, :], qkw[:, 1:2])

            def take_mixed(i, b, j):
                act.wait_ge(mixed, unit(i, b, j) + 1)
                nc.scalar.activation(ctxT[0][:, b, j, :], O[:], ACT.Copy).then_inc(mixed_hi, 1)

            def body(i):
                for b in range(NB):
                    last = ends(i, b)[1]
                    nb = 1 - b
                    exps(i, b, 0)
                    for j in range(GROUP):
                        u = unit(i, b, j)
                        if not last:
                            queries(i, b, j, nb)
                        if j < 3:
                            exps(i, b, j + 1)
                        if not (ends(i, b)[0] and j == 0):
                            take_mixed(*before(i, b, j))
                        for n in range(3):
                            act.wait_ge(turned, 3 * u + n + 1)
                            s = slice(512 * n, min(512 * (n + 1), PACKED))
                            nc.scalar.activation(pT[0][:, s], T[n][:, 0:s.stop - s.start], ACT.Copy
                                                 ).then_inc(pT_hi_done, 1)
                        if kind == 2 and b == 0 and j == 3 and not (isinstance(i, int) and i == KV - 1):
                            split_q(i + 1)
                        if kind == 2 and not last:
                            if j == 1:
                                turned_k(i, b, j, nb)
                            turned_q(i, b, j, nb)
                            for n in range(2 if j == 0 else 0):
                                keys_values(i, b, j, nb, n)
                        if kind == 1 and j == 0 and not last:
                            keys(i, b, j, nb)
                        if kind == 1 and j == 3 and not last:
                            values(i, b, j, nb)

            if kind == 2:
                split_q(0)
                act.wait_ge(qkw_done, 1)
            for j in range(GROUP):
                queries(-1, 0, j, 0)
                if kind == 2:
                    turned_q(-1, 0, j, 0)
            if kind == 2:
                for n in range(2):
                    keys_values(-1, 0, 0, 0, n)
                turned_k(-1, 0, 0, 0)
            else:
                keys(-1, 0, 0, 0)
                values(-1, 0, 0, 0)
            loop(act, body)
            take_mixed(KV - 1, 1, 3)

        @block.vector
        def _(dve):
            def hi_count(i, b, j, name):
                count = 0
                mine = [nm for nm in PROLOGUE if takes_hi(nm)]
                if isinstance(i, int) and i == -1:
                    at = use(i, b, j, name)
                    return sum(takes_hi(nm) for nm in PROLOGUE[:at + 1])
                per = len(mine)
                at = sum(takes_hi(nm) for jj in range(j) for nm in uses(i, b, jj))
                names = uses(i, b, j)
                at += sum(takes_hi(nm) for nm in names[:names.index(name) + 1])
                return per + per * (2 * i + b) + at

            def takes_hi(name):
                return name in (("Q", "K", "VT") if kind == 1 else ("QT", "KT", "KV0", "KV1"))

            def low(i, b, j, name, hi, lo, scale):
                dve.wait_ge(work_hi, hi_count(i, b, j, name))
                src = work(i, b, j, name)[:]
                if len(hi.shape) == 3:
                    src = src.rearrange("p (a b) -> p a b", a=4)
                if scale is None:
                    ins = nc.vector.tensor_tensor(lo, src, hi.bitcast(F32), ALU.subtract)
                else:
                    ins = nc.vector.scalar_tensor_tensor(out=lo, in0=src, scalar=scale, in1=hi.bitcast(F32),
                                                         op0=ALU.mult, op1=ALU.subtract)
                ins.then_inc(work_free, 1)

            def split_q(g):
                four = "p j c n -> p (j c n)"
                dve.wait_ge(wq_hi, g + 1)
                nc.vector.tensor_tensor(wq[1][:].rearrange(four), raw_q[:].rearrange("p j n -> p (j n)"),
                                        wq[0][:].rearrange(four).bitcast(F32), ALU.subtract).then_inc(wq_split, 1)

            def mean(n):
                four = "p (h d) -> p h d"
                dve.wait_ge(square_done, n + 1)
                nc.vector.reduce_sum(sumsq[:], square[:].rearrange(four, h=4), AX_X
                                     ).then_inc(sumsq_done, 1)
                dve.wait_ge(sumsq_done, n + 1)
                nc.vector.tensor_scalar(sumsq[:], sumsq[:], 1.0 / P, RMS_EPS, ALU.mult, ALU.add
                                        ).then_inc(mean_done, 1)

            def norm(i, b, j, name, n):
                four = "p (h d) -> p h d"
                dve.wait_ge(rms_done, n + 1)
                nc.vector.tensor_tensor(square[:].rearrange(four, h=4), work(i, b, j, name)[:].rearrange(four, h=4),
                                        rms[:].unsqueeze(2).to_broadcast([P, 4, P]),
                                        ALU.mult).then_inc(work_free, 1)

            def queries(i, b, j, nb, n):
                if kind == 1:
                    low(i, b, j, "Q", q[0][:, nb, j, :], q[1][:, nb, j, :], NEG)
                else:
                    mean(n)

            def keys(i, b, j, nb):
                low(i, b, j, "K", k[0][:, nb, :], k[1][:, nb, :], None)

            def keys_values(i, b, j, nb, n, root):
                src = work(i, b, j, f"KV{n}")[:].rearrange("p (t k d) -> p t k d", t=2, k=2)
                s = slice(2 * n, 2 * n + 2)
                sq = square_k[:].rearrange("p (t d) -> p t d", t=TB)[:, s, :]
                dve.wait_ge(square_done, root + 1)
                nc.vector.reduce_sum(sumsq[:, s], sq, AX_X).then_inc(sumsq_done, 1)
                dve.wait_ge(sumsq_done, root + 1)
                nc.vector.tensor_scalar(sumsq[:, s], sumsq[:, s], 1.0 / P, RMS_EPS, ALU.mult, ALU.add
                                        ).then_inc(mean_done, 1)
                dve.wait_ge(work_hi, hi_count(i, b, j, f"KV{n}"))
                nc.vector.tensor_tensor(v[1][:, nb, s, :], src[:, :, 1, :], v[0][:, nb, s, :].bitcast(F32),
                                        ALU.subtract)
                dve.wait_ge(rms_done, root + 1)
                nc.vector.tensor_tensor(sq, src[:, :, 0, :],
                                        rms[:, s].unsqueeze(2).to_broadcast([P, 2, P]), ALU.mult
                                        ).then_inc(work_free, 1)

            def values_out(i, b, j):
                dve.wait_ge(work_full, use(i, b, j, "V") + 1)
                nc.vector.tensor_copy(v_raw[:], work(i, b, j, "V")[:]).then_inc(work_free, 1)

            def values(i, b, j, nb):
                low(i, b, j, "VT", v[0][:, nb, :, :], v[1][:, nb, :, :], None)

            def turned_q(i, b, j, nb):
                s = slice(j * P, (j + 1) * P)
                low(i, b, j, "QT", q[0][:, nb, :, s], q[1][:, nb, :, s], qkw[:, 0:1])

            def turned_k(i, b, j, nb):
                low(i, b, j, "KT", k[0][:, nb, :], k[1][:, nb, :], qkw[:, 1:2])

            def minima(i, b, j):
                u = unit(i, b, j)
                for qi, need in zip(ORDER, (1, 2, 2, 3)):
                    dve.wait_ge(scored, 3 * u + need)
                    nc.vector.tensor_reduce(negmax[:, j % 2, qi:qi + 1],
                                            S[SLOT[qi][0]][:, SLOT[qi][1]:SLOT[qi][1] + (qi + 1) * P],
                                            AX_X, ALU.min).then_inc(min_done, 1)

            def reciprocals(i, b, j):
                dve.wait_ge(exp_done, 4 * unit(i, b, j) + 4)
                nc.vector.reciprocal(recip[:, j % 2, :], rowsum[:, j % 2, :]).then_inc(recip_done, 1)

            def body(i):
                for b in range(NB):
                    first, last = ends(i, b)
                    nb = 1 - b
                    pb = 1 - b
                    turns = 6 + 12 * i + 6 * b
                    minima(i, b, 0)
                    reciprocals(i, b, 0)
                    for j in range(GROUP):
                        u = unit(i, b, j)
                        if not last:
                            queries(i, b, j, nb, turns + (j and j + 2))
                        if j < 3:
                            minima(i, b, j + 1)
                        if kind == 2 and not last:
                            norm(i, b, j, "Q", turns + (j and j + 2))

                        if not (first and j == 0):
                            take_mixed(*before(i, b, j))
                        if j < 3:
                            reciprocals(i, b, j + 1)
                        for n in range(3):
                            dve.wait_ge(pT_hi_done, 3 * u + n + 1)
                            s = slice(512 * n, min(512 * (n + 1), PACKED))
                            nc.vector.tensor_tensor(pT[1][:, s], T[n][:, 0:s.stop - s.start],
                                                    pT[0][:, s].bitcast(F32), ALU.subtract
                                                    ).then_inc(pT_done, 1)
                        if kind == 2 and j == 1 and not last:
                            turned_k(i, b, j, nb)
                        if kind == 1 and j == 3 and not last:
                            values(i, b, j, nb)
                        for t in () if first else OUT_TILES[j]:
                            dve.wait_ge(work_full, use(i, b, j, f"D{t}") + 1)
                            xt = K.xs[:, pb * TB + t, :]
                            nc.vector.tensor_tensor(xt, xt, work(i, b, j, f"D{t}")[:], ALU.add
                                                    ).then_inc(work_free, 1)
                        if kind == 2 and b == 0 and j == 3 and not (isinstance(i, int) and i == KV - 1):
                            split_q(i + 1)
                        if kind == 2 and not last:
                            turned_q(i, b, j, nb)
                            for n in range(2 if j == 0 else 0):
                                keys_values(i, b, j, nb, n, turns + 1 + n)
                        if kind == 1 and j == 0 and not last:
                            keys(i, b, j, nb)
                        if kind == 1 and j == 2 and not last:
                            values_out(i, b, j)

            def take_mixed(i, b, j):
                dve.wait_ge(mixed_hi, unit(i, b, j) + 1)
                nc.vector.tensor_tensor(ctxT[1][:, b, j, :], O[:], ctxT[0][:, b, j, :].bitcast(F32),
                                        ALU.subtract).then_inc(mixed_done, 1)

            if kind == 2:
                dve.wait_ge(qkw_in, 16)
                nc.vector.tensor_scalar(qkw[:, 0:1], qkw[:, 0:1], NEG, None, ALU.mult).then_inc(qkw_done, 1)
                dve.wait_ge(qkw_done, 1)
                split_q(0)
            for j in range(GROUP):
                queries(-1, 0, j, 0, j)
                if kind == 2:
                    norm(-1, 0, j, "Q", j)
                    turned_q(-1, 0, j, 0)
            if kind == 2:
                for n in range(2):
                    keys_values(-1, 0, 0, 0, n, 4 + n)
                turned_k(-1, 0, 0, 0)
            else:
                keys(-1, 0, 0, 0)
                values_out(-1, 0, 0)
                values(-1, 0, 0, 0)
            loop(dve, body)
            take_mixed(KV - 1, 1, 3)
            for j in range(TB):
                dve.wait_ge(work_full, FINAL + j + 1)
                t = TB + j
                nc.vector.tensor_tensor(K.xs[:, t, :], K.xs[:, t, :], (S + T)[j][:], ALU.add
                                        ).then_inc(work_free, 1)


SINK_ITERS = 50
UNROLL = 5
TAU = 0.1
STREAMS = 4
RMS1_EPS = 1.1920929e-07


def streams_stage(nc, K, dram, pre):
    N, C = STREAMS, P
    NL = N * N + 2 * N
    HALF = NT // 2
    with ExitStack() as ctx:
        m = Memory(nc, ctx, pre)
        sb, sem = m.sb, m.sem
        w_raw, w = sb("w_raw", [P, NC_, NL]), [sb(f"w{n}", [P, NC_, P], F32R) for n in "hl"]
        lgT = sb("logitsT", [NL, TOK])
        wb_raw, wb = sb("wb_raw", [P, C]), [sb(f"wb{n}", [P, C], F32R) for n in "hl"]
        base = sb("base", [P, NL])
        gate = sb("gate", [P, 4])
        square = sb("square", [P, 2, D])
        ms, rms = sb("ms", [P, NT]), sb("rms", [P, NT])
        logit = sb("logit", [P, NT, NL])
        Z = sb("Z", [P, NT, N, N])
        diff, expd = sb("diff", [P, NT, N, N]), sb("expd", [P, NT, N, N])
        top, total, logs = (sb(n, [P, NT, N]) for n in ("top", "total", "logs"))
        u, v = sb("u", [P, NT, N]), sb("v", [P, NT, N])
        H = sb("H", [P, NT, N, N])
        soft = sb("soft", [P, NT, 2, N])
        sm, ss = sb("sm", [P, NT, 2]), sb("ss", [P, NT, 2])
        eye = sb("eye", [P, N, N])
        xin, part_in = sb("xin", [P, NT, C]), sb("part_in", [P, C])
        xT = [sb(f"xT{n}", [P, NT, P], F32R) for n in "hl"]
        acc, term = sb("acc", [P, 2, D]), sb("term", [P, C])
        term_done = sem("term_done")
        lg = m.ps("logits")
        tb = [m.ps(f"turned{n}") for n in range(2)]
        yb = [m.ps(f"branch{n}") for n in range(2)]
        in_w, in_wb, in_base, in_gate = sem("in_w"), sem("in_wb"), sem("in_base"), sem("in_gate")
        pool_step, w_split, eye_made = sem("pool_step"), sem("w_split"), sem("eye_made")
        ms_done, rms_done, logits, ready = sem("ms_done"), sem("rms_done"), sem("logits"), sem("ready")
        d0, d1 = sem("dve_set0"), sem("dve_set1")
        exp_done, log_done = [sem("exp0"), sem("exp1")], [sem("log0"), sem("log1")]
        logits_T, logits_out = sem("logits_T"), sem("logits_out")
        soft_ready, xin_step = sem("soft_ready"), sem("xin_step")
        small, small_exp = sem("small"), sem("small_exp")
        xin_done, xturned, x_hi, x_lo = sem("xin"), sem("xturned"), sem("x_hi"), sem("x_lo")
        branch, out_step = sem("branch"), [sem(f"out_step{n}") for n in range(2)]
        branch_out, H_ready, taken = sem("branch_out"), sem("H_ready"), sem("taken")
        chain = sem("chain")
        block = ctx.enter_context(nc.Block())
        x = [K.xh, K.xl]

        @block.sync
        def _(sp):
            sp.dma_start(w_raw[:], dram["s_w"]).then_inc(in_w, 16)
            sp.dma_start(wb_raw[:], dram["s_wb"]).then_inc(in_wb, 16)
            sp.dma_start(base[:], dram["s_base"]).then_inc(in_base, 16)
            sp.dma_start(gate[:, 0:1], dram["s_gate"]).then_inc(in_gate, 16)

        @block.gpsimd
        def _(pool):
            step = Chain(pool, pool_step)
            step(nc.gpsimd.memset(eye[:], 0.0))
            for n in range(N):
                last = nc.gpsimd.memset(eye[:, n, n:n + 1], 1.0)
            last.then_inc(eye_made, 1)
            for a in w:
                step(nc.gpsimd.memset(a[:].bitcast(F32), 0.0))
            pool.wait_ge(in_w, 16)
            hi, lo = (a[:, :, 0:NL] for a in w)
            step(nc.gpsimd.tensor_copy(hi, w_raw[:]))
            nc.gpsimd.tensor_tensor(lo, w_raw[:], hi.bitcast(F32), ALU.subtract).then_inc(w_split, 1)
            pool.wait_ge(in_wb, 16)
            step(nc.gpsimd.tensor_copy(wb[0][:], wb_raw[:]))
            nc.gpsimd.tensor_tensor(wb[1][:], wb_raw[:], wb[0][:].bitcast(F32), ALU.subtract).then_inc(w_split, 1)
            pool.wait_ge(ms_done, NT + 1)
            nc.gpsimd.tensor_tensor(rms[:], ms[:], K.half[:], ALU.pow).then_inc(rms_done, 1)
            pool.wait_ge(soft_ready, 1)
            count = 0
            for t in range(NT):
                for n in range(N):
                    dst = part_in[:] if n else xin[:, t, :]
                    nc.gpsimd.tensor_tensor(dst, K.xs[:, t, n * C:(n + 1) * C],
                                            soft[:, t, 0, n:n + 1].to_broadcast([P, C]), ALU.mult
                                            ).then_inc(xin_step, 1)
                    count += 1
                    if n:
                        pool.wait_ge(xin_step, count)
                        nc.gpsimd.tensor_tensor(xin[:, t, :], xin[:, t, :], part_in[:], ALU.add
                                                ).then_inc(xin_done if n == N - 1 else xin_step, 1)
                        count += n < N - 1
                        if n < N - 1:
                            pool.wait_ge(xin_step, count)
                        else:
                            pool.wait_ge(xin_done, t + 1)
            pool.wait_ge(H_ready, 1)
            for t in range(NT):
                pool.wait_ge(branch_out, t + 1)
                for n in range(N):
                    x_n = K.xs[:, t, n * C:(n + 1) * C]
                    if t or n:
                        pool.wait_ge(out_step[1], N * t + n)
                    nc.gpsimd.tensor_tensor(term[:], x_n, H[:, t, N - 1, n:n + 1].to_broadcast([P, C]), ALU.mult
                                            ).then_inc(term_done, 1)
                    pool.wait_ge(term_done, N * t + n + 1)
                    o = acc[:, t % 2, (N - 1) * C:]
                    nc.gpsimd.tensor_tensor(o, o, term[:], ALU.add).then_inc(out_step[1], 1)

        @block.tensor
        def _(pe):
            pe.wait_ge(w_split, 1)
            for b in range(NB):
                for c in range(NC_):
                    last = mm3(nc, yb[b][:], [a[:, c, :] for a in w],
                               [a[:, c, b * SEQ:(b + 1) * SEQ] for a in x], c == 0, c == NC_ - 1)
                last.then_inc(logits_T, 1)
            for t in range(NT):
                pe.wait_ge(logits_out, t // TB + 1)
                last = nc.tensor.transpose(lg[:, t * NL:(t + 1) * NL], lgT[:, t * P:(t + 1) * P],
                                           K.ident[0:NL, 0:NL])
            last.then_inc(logits, 1)
            pe.wait_ge(w_split, 2)
            for t in range(NT):
                pe.wait_ge(xin_done, t + 1)
                at = t % HALF * P
                nc.tensor.transpose(tb[t // HALF][:, at:at + P], xin[:, t, :], K.ident[:]).then_inc(xturned, 1)
            for t in range(NT):
                pe.wait_ge(x_lo, t // HALF + 1)
                if t >= 2:
                    pe.wait_ge(branch_out, t - 1)
                mm3(nc, yb[t % 2][:, 0:C], [a[:, t, :] for a in xT], [a[:] for a in wb], True, True
                    ).then_inc(branch, 1)

        @block.scalar
        def _(act):
            act.wait_ge(in_gate, 16)
            nc.scalar.activation(gate[:, 1:2], gate[:, 0:1], ACT.Exp, scale=-1.0).then_inc(small_exp, 1)
            for b in range(NB):
                act.wait_ge(logits_T, b + 1)
                nc.scalar.activation(lgT[:, b * SEQ:(b + 1) * SEQ], yb[b][0:NL, :], ACT.Copy).then_inc(logits_out, 1)
            act.wait_ge(small, 1)
            nc.scalar.activation(soft[:], soft[:], ACT.Exp).then_inc(small_exp, 1)

            def step(n, k):
                s = slice(n * HALF, (n + 1) * HALF)
                act.wait_ge(d[n], 5 * k + 3)
                nc.scalar.activation(expd[:, s], diff[:, s], ACT.Exp).then_inc(exp_done[n], 1)
                return s

            def log(n, k):
                s = slice(n * HALF, (n + 1) * HALF)
                act.wait_ge(d[n], 5 * k + 4)
                nc.scalar.activation(logs[:, s], total[:, s], ACT.Ln).then_inc(log_done[n], 1)
            d = [d0, d1]
            nc.scalar.preload_act_table_set("natural_log_exp_and_others")
            with act.Fori(0, SINK_ITERS // UNROLL) as i:
                for at in range(2 * UNROLL):
                    for part in (step, log):
                        for n in range(2):
                            part(n, 2 * UNROLL * i + at)
            for n in range(2):
                s = slice(n * HALF, (n + 1) * HALF)
                act.wait_ge(d[n], 10 * SINK_ITERS + 2)
                nc.scalar.activation(H[:, s], diff[:, s], ACT.Exp).then_inc(exp_done[n], 1)
            for n in range(2):
                act.wait_ge(xturned, HALF * (n + 1))
                nc.scalar.activation(xT[0][:, n * HALF:(n + 1) * HALF, :].rearrange("p t c -> p (t c)"), tb[n][:],
                                     ACT.Copy).then_inc(x_hi, 1)
            for t in range(NT + 1):
                if t < NT:
                    act.wait_ge(branch, t + 1)
                    if t >= 2:
                        act.wait_ge(taken, t - 1)
                    for i in range(N):
                        last = nc.scalar.activation(acc[:, t % 2, i * C:(i + 1) * C], yb[t % 2][:, 0:C], ACT.Copy,
                                                    scale=soft[:, t, 1, i:i + 1])
                    last.then_inc(branch_out, 1)
                if t:
                    act.wait_ge(out_step[0], (N - 1) * N * t)
                    act.wait_ge(out_step[1], N * t)
                    nc.scalar.activation(K.xs[:, t - 1, :], acc[:, (t - 1) % 2, :], ACT.Copy).then_inc(taken, 1)

        @block.vector
        def _(dve):
            step = Chain(dve, chain)
            for t in range(NT):
                if t >= 2:
                    dve.wait_ge(ms_done, t - 1)
                nc.vector.tensor_tensor_reduce(out=square[:, t % 2, :], in0=K.xs[:, t, :], in1=K.xs[:, t, :],
                                               scale=1.0, scalar=0.0, op0=ALU.mult, op1=ALU.add,
                                               accum_out=ms[:, t:t + 1]).then_inc(ms_done, 1)
            dve.wait_ge(ms_done, NT)
            nc.vector.tensor_scalar(ms[:], ms[:], 1.0 / D, RMS1_EPS, ALU.mult, ALU.add).then_inc(ms_done, 1)
            dve.wait_ge(logits, 1)
            dve.wait_ge(rms_done, 1)
            dve.wait_ge(in_base, 16)
            lv = lg[:, 0:NT * NL].rearrange("p (t n) -> p t n", t=NT)
            step(nc.vector.tensor_tensor(logit[:], lv, rms[:].unsqueeze(2).to_broadcast([P, NT, NL]), ALU.mult))
            step(nc.vector.tensor_tensor(logit[:], logit[:], base[:].unsqueeze(1).to_broadcast([P, NT, NL]),
                                         ALU.add))
            Zl = logit[:, :, 0:N * N].rearrange("p t (i j) -> p t i j", i=N)
            nc.vector.tensor_scalar(Z[:], Zl, 1.0 / TAU, None, ALU.mult)
            nc.vector.memset(v[:], 0.0)
            two = logit[:, :, N * N:].rearrange("p t (a n) -> p t a n", a=2)
            step(nc.vector.tensor_reduce(sm[:], two, AX_X, ALU.max))
            nc.vector.tensor_tensor(soft[:], two, sm[:].unsqueeze(3).to_broadcast([P, NT, 2, N]), ALU.subtract
                                    ).then_inc(small, 1)
            dve.wait_ge(small_exp, 2)
            step(nc.vector.reduce_sum(ss[:], soft[:], AX_X))
            step(nc.vector.reciprocal(ss[:], ss[:]))
            nc.vector.tensor_tensor(soft[:], soft[:], ss[:].unsqueeze(3).to_broadcast([P, NT, 2, N]), ALU.mult
                                    ).then_inc(soft_ready, 1)

            d = [d0, d1]

            def views(n, way):
                s = slice(n * HALF, (n + 1) * HALF)
                order = "p t i j -> p t i j" if way == 0 else "p t i j -> p t j i"
                return s, [a[:, s].rearrange(order) for a in (Z, diff, expd)]

            def begin(n, way, k):
                s, (z, df, _) = views(n, way)
                other = (v if way == 0 else u)[:, s].unsqueeze(2).to_broadcast([P, HALF, N, N])
                if not (isinstance(k, int) and k == 0):
                    dve.wait_ge(d[n], 5 * k)
                nc.vector.tensor_tensor(df, z, other, ALU.add).then_inc(d[n], 1)

            def maxima(n, way, k):
                s, (_, df, _) = views(n, way)
                dve.wait_ge(d[n], 5 * k + 1)
                nc.vector.tensor_reduce(top[:, s], df, AX_X, ALU.max).then_inc(d[n], 1)

            def shift(n, way, k):
                s, (_, df, _) = views(n, way)
                dve.wait_ge(d[n], 5 * k + 2)
                nc.vector.tensor_tensor(df, df, top[:, s].unsqueeze(3).to_broadcast([P, HALF, N, N]),
                                        ALU.subtract).then_inc(d[n], 1)

            def sums(n, way, k):
                s, (_, _, e) = views(n, way)
                dve.wait_ge(exp_done[n], k + 1)
                nc.vector.tensor_reduce(total[:, s], e, AX_X, ALU.add).then_inc(d[n], 1)

            def end(n, way, k):
                s = slice(n * HALF, (n + 1) * HALF)
                dve.wait_ge(log_done[n], k + 1)
                nc.vector.scalar_tensor_tensor(out=(u if way == 0 else v)[:, s], in0=top[:, s], scalar=-1.0,
                                               in1=logs[:, s], op0=ALU.mult, op1=ALU.subtract
                                               ).then_inc(d[n], 1)

            step(nc.vector.memset(u[:], 0.0))
            with dve.Fori(0, SINK_ITERS // UNROLL) as i:
                for at in range(2 * UNROLL):
                    for part in (begin, maxima, shift, sums, end):
                        for n in range(2):
                            part(n, at % 2, 2 * UNROLL * i + at)
            for n in range(2):
                s = slice(n * HALF, (n + 1) * HALF)
                base_n = 10 * SINK_ITERS
                dve.wait_ge(d[n], base_n)
                nc.vector.tensor_tensor(diff[:, s], Z[:, s], u[:, s].unsqueeze(3).to_broadcast([P, HALF, N, N]),
                                        ALU.add).then_inc(d[n], 1)
                dve.wait_ge(d[n], base_n + 1)
                nc.vector.tensor_tensor(diff[:, s], diff[:, s],
                                        v[:, s].unsqueeze(2).to_broadcast([P, HALF, N, N]), ALU.add
                                        ).then_inc(d[n], 1)
            step(nc.vector.tensor_scalar(gate[:, 1:2], gate[:, 1:2], 1.0, None, ALU.add))
            step(nc.vector.reciprocal(gate[:, 2:3], gate[:, 1:2]))
            step(nc.vector.tensor_scalar(gate[:, 3:4], gate[:, 2:3], -1.0, 2.0, ALU.mult, ALU.add))
            dve.wait_ge(eye_made, 1)
            step(nc.vector.tensor_scalar(eye[:], eye[:], gate[:, 3:4], None, ALU.mult))
            for n in range(2):
                dve.wait_ge(x_hi, n + 1)
                hi, lo = (a[:, n * HALF:(n + 1) * HALF, :].rearrange("p t c -> p (t c)") for a in xT)
                nc.vector.tensor_tensor(lo, tb[n][:], hi.bitcast(F32), ALU.subtract).then_inc(x_lo, 1)
            for n in range(2):
                dve.wait_ge(exp_done[n], 2 * SINK_ITERS + 1)
            step(nc.vector.tensor_scalar(H[:], H[:], gate[:, 2:3], None, ALU.mult))
            nc.vector.tensor_tensor(H[:], H[:], eye[:].unsqueeze(1).to_broadcast([P, NT, N, N]), ALU.add
                                    ).then_inc(H_ready, 1)
            dve.wait_ge(H_ready, 1)
            for t in range(NT):
                dve.wait_ge(branch_out, t + 1)
                for n in range(N):
                    for i in range(N - 1):
                        o = acc[:, t % 2, i * C:(i + 1) * C]
                        nc.vector.scalar_tensor_tensor(out=o, in0=K.xs[:, t, n * C:(n + 1) * C],
                                                       scalar=H[:, t, i, n:n + 1], in1=o,
                                                       op0=ALU.mult, op1=ALU.add).then_inc(out_step[0], 1)
                    if n < N - 1:
                        dve.wait_ge(out_step[0], (N - 1) * (N * t + n + 1))


BOT, RDIM, NSLOT, TOPK, VB = 64, 48, 128, 8, 32
TAU_LOW, TAU_HIGH, EARLY_EXIT = 0.5, 2.0, 0.05
HIDDEN = 3.0e38


def slots_stage(nc, K, dram, pre):
    with ExitStack() as ctx:
        m = Memory(nc, ctx, pre)
        sb, sem = m.sb, m.sem
        names = {"wq": [P, NC_, BOT], "wr": [RDIM, BOT], "wrT": [BOT, RDIM], "keysT": [BOT, NSLOT],
                 "valuesT": [P, NC_, NSLOT], "wvdT": [P, NC_, VB], "wvuT": [VB, D], "wu1": [P, NC_, P],
                 "wu2": [P, 1], "bu1": [P, 1], "scalars": [P, 3], "log_rel": [P, NSLOT]}
        W = {n: sb(n, s) for n, s in names.items()}
        loaded = {n: sem(f"in_{n}") for n in names}
        wq = [sb(f"wq{n}", [P, NC_, P], F32R) for n in "hl"]
        wu = [sb(f"wu{n}", [P, NC_, P], F32R) for n in "hl"]
        rkT, avT = sb("rkT", [RDIM, NSLOT]), sb("avT", [VB, NSLOT])
        router = sb("router", [BOT, 2 * NSLOT])
        slot_out = sb("slot_out", [NSLOT, D])
        query = sb("query", [BOT, TOK])
        act_u = sb("act_u", [P, TOK])
        stats, mv = sb("stats", [P, NT, 6]), sb("mv", [P, NT, 2])
        logv, logsum, mean = sb("logv", [P, NT]), sb("logsum", [P, 1]), sb("mean", [P, 1])
        ones = sb("ones", [P, P])
        learned, gate, live = sb("learned", [P, NT]), sb("gate", [P, NT]), sb("live", [P, NT])
        R, R2, A = (sb(n, [P, 2, NSLOT]) for n in ("R", "R2", "A"))
        best = sb("best", [P, 2, 8])
        chosen, off = sb("chosen", [P, 2, NSLOT]), sb("off", [P, 2, NSLOT])
        least, total, factor = sb("least", [P, NT]), sb("total", [P, NT]), sb("factor", [P, NT])
        E, ET = sb("E", [P, 2, NSLOT]), sb("ET", [P, 2, P])
        pre_bank, u_bank, l_bank = m.ps("prepare_bank"), m.ps("uncertain_bank"), m.ps("learned_bank")
        s_bank = [m.ps(f"scores{n}") for n in range(2)]
        t_bank = m.ps("turned")
        o_bank = [m.ps(f"out{n}") for n in range(2)]
        split, split_step, ones_made = sem("split"), sem("split_step"), sem("ones_made")
        prep, prep_out = sem("prep"), sem("prep_out")
        u_full, u_out = sem("u_full"), sem("u_out")
        l_full, var_done, logv_done, sum_done, mean_full = (
            sem(n) for n in ("l_full", "var", "logv", "sum", "mean_full"))
        z_ready, z_exp = sem("z_ready"), sem("z_exp")
        s_full, s_out, least_done, E_done, E_turned, ET_done, out_full, out_done = (
            sem(n) for n in ("s_full", "s_out", "least", "E", "E_turned", "ET", "out_full", "out"))
        stats_done, doubled, chain = sem("stats_done"), sem("doubled"), sem("chain")
        block = ctx.enter_context(nc.Block())
        x = [K.xh, K.xl]

        @block.sync
        def _(sp):
            for n in names:
                sp.dma_start(W[n][:], dram[f"u_{n}"]).then_inc(loaded[n], 16)

        @block.gpsimd
        def _(pool):
            step = Chain(pool, split_step)
            nc.gpsimd.memset(ones[:], 1.0).then_inc(ones_made, 1)
            nc.gpsimd.memset(wq[0][:].bitcast(F32), 0.0)
            step(nc.gpsimd.memset(wq[1][:].bitcast(F32), 0.0))
            pool.wait_ge(loaded["wq"], 16)
            step(nc.gpsimd.tensor_copy(wq[0][:, :, 0:BOT], W["wq"][:]))
            nc.gpsimd.tensor_tensor(wq[1][:, :, 0:BOT], W["wq"][:], wq[0][:, :, 0:BOT].bitcast(F32), ALU.subtract
                                    ).then_inc(split, 1)
            pool.wait_ge(loaded["wu1"], 16)
            step(nc.gpsimd.tensor_copy(wu[0][:], W["wu1"][:]))
            nc.gpsimd.tensor_tensor(wu[1][:], W["wu1"][:], wu[0][:].bitcast(F32), ALU.subtract
                                    ).then_inc(split, 1)
            for t in range(NT):
                pool.wait_ge(stats_done, t + 1)
                nc.gpsimd.tensor_tensor(K.xs[:, t, :], K.xs[:, t, :], K.xs[:, t, :], ALU.add
                                        ).then_inc(doubled, 1)

        @block.tensor
        def _(pe):
            pe.wait_ge(loaded["wrT"], 16)
            pe.wait_ge(loaded["keysT"], 16)
            nc.tensor.matmul(pre_bank[0:RDIM, 0:NSLOT], W["wrT"][:], W["keysT"][:], start=True, stop=True)
            pe.wait_ge(loaded["valuesT"], 16)
            pe.wait_ge(loaded["wvdT"], 16)
            for c in range(NC_):
                last = nc.tensor.matmul(pre_bank[0:VB, NSLOT:2 * NSLOT], W["wvdT"][:, c, :], W["valuesT"][:, c, :],
                                        start=c == 0, stop=c == NC_ - 1)
            last.then_inc(prep, 1)
            pe.wait_ge(split, 1)
            for n in range(2 * NB):
                b, which = divmod(n, 2)
                if n == 1:
                    pe.wait_ge(split, 2)
                if n > 0:
                    pe.wait_ge(u_out, n)
                for c in range(NC_):
                    last = mm3(nc, u_bank[:], [a[:, c, :] for a in (wq, wu)[which]],
                               [a[:, c, b * SEQ:(b + 1) * SEQ] for a in x], c == 0, c == NC_ - 1)
                last.then_inc(u_full, 1)
            pe.wait_ge(prep_out, 2)
            pe.wait_ge(loaded["wr"], 16)
            nc.tensor.matmul(pre_bank[0:BOT, 0:NSLOT], W["wr"][:], rkT[:], start=True, stop=True).then_inc(prep, 1)
            pe.wait_ge(prep_out, 3)
            pe.wait_ge(loaded["wvuT"], 16)
            nc.tensor.matmul(pre_bank[:], avT[:], W["wvuT"][:], start=True, stop=True).then_inc(prep, 1)
            pe.wait_ge(u_out, 2 * NB)
            pe.wait_ge(loaded["wu2"], 16)
            for t in range(NT):
                nc.tensor.matmul(l_bank[:, t:t + 1], act_u[:, t * P:(t + 1) * P], W["wu2"][:],
                                 start=True, stop=True)
            pe.wait_ge(sum_done, 1)
            pe.wait_ge(ones_made, 1)
            nc.tensor.matmul(l_bank[:, NT:NT + 1], ones[:], logsum[:], start=True, stop=True).then_inc(l_full, 1)
            pe.wait_ge(prep_out, 5)

            def scores(t):
                if t >= 2:
                    pe.wait_ge(s_out, 2 * (t - 1))
                nc.tensor.matmul(s_bank[t % 2][:, 0:2 * NSLOT], query[:, t * P:(t + 1) * P], router[:],
                                 start=True, stop=True).then_inc(s_full, 1)
            scores(0)
            for t in range(NT):
                if t + 1 < NT:
                    scores(t + 1)
                pe.wait_ge(E_done, t + 1)
                if t:
                    pe.wait_ge(ET_done, t)
                nc.tensor.transpose(t_bank[:, 0:P], E[:, t % 2, :], K.ident[:]).then_inc(E_turned, 1)
                pe.wait_ge(ET_done, t + 1)
                if t >= 2:
                    pe.wait_ge(out_done, t - 1)
                nc.tensor.matmul(o_bank[t % 2][:], ET[:, t % 2, :], slot_out[:], start=True, stop=True
                                 ).then_inc(out_full, 1)

        @block.scalar
        def _(act):
            act.wait_ge(prep, 1)
            nc.scalar.activation(rkT[:], pre_bank[0:RDIM, 0:NSLOT], ACT.Copy).then_inc(prep_out, 1)
            nc.scalar.activation(avT[:], pre_bank[0:VB, NSLOT:2 * NSLOT], ACT.Copy).then_inc(prep_out, 1)
            act.wait_ge(loaded["bu1"], 16)
            for n in range(2 * NB):
                b, which = divmod(n, 2)
                s = slice(b * SEQ, (b + 1) * SEQ)
                act.wait_ge(u_full, n + 1)
                if which == 0:
                    nc.scalar.activation(query[:, s], u_bank[0:BOT, :], ACT.Copy).then_inc(u_out, 1)
                else:
                    nc.scalar.activation(act_u[:, s], u_bank[:], ACT.Gelu_apprx_tanh, bias=W["bu1"][:, 0:1]
                                         ).then_inc(u_out, 1)
            act.wait_ge(prep, 2)
            nc.scalar.activation(router[:, 0:NSLOT], pre_bank[0:BOT, 0:NSLOT], ACT.Copy).then_inc(prep_out, 1)
            nc.scalar.activation(router[:, NSLOT:], W["keysT"][:], ACT.Copy).then_inc(prep_out, 1)
            act.wait_ge(prep, 3)
            nc.scalar.activation(slot_out[:], pre_bank[:], ACT.Copy).then_inc(prep_out, 1)
            act.wait_ge(var_done, NT)
            nc.scalar.activation(logv[:], mv[:, :, 1], ACT.Ln, bias=1.0).then_inc(logv_done, 1)
            act.wait_ge(z_ready, 1)
            nc.scalar.activation(learned[:], learned[:], ACT.Exp, scale=-1.0
                                 ).then_inc(z_exp, 1)
            act.wait_ge(z_ready, 2)
            nc.scalar.activation(gate[:], gate[:], ACT.Exp, scale=-1.0
                                 ).then_inc(z_exp, 1)
            for t in range(NT):
                act.wait_ge(least_done, t + 1)
                if t >= 2:
                    act.wait_ge(E_turned, t - 1)
                nc.scalar.activation(E[:, t % 2, :], A[:, t % 2, :], ACT.Exp, scale=-1.0, bias=least[:, t:t + 1],
                                     accum_out=total[:, t:t + 1]).then_inc(E_done, 1)
                act.wait_ge(E_turned, t + 1)
                if t >= 2:
                    act.wait_ge(out_full, t - 1)
                nc.scalar.activation(ET[:, t % 2, :], t_bank[:, 0:P], ACT.Copy).then_inc(ET_done, 1)

        @block.vector
        def _(dve):
            step = Chain(dve, chain)
            for t in range(NT):
                nc.vector.bn_stats(stats[:, t, :], K.xs[:, t, :]).then_inc(stats_done, 1)
            for t in range(NT):
                dve.wait_ge(stats_done, t + 1)
                nc.vector.bn_aggr(mv[:, t, :], stats[:, t, :]).then_inc(var_done, 1)
            dve.wait_ge(logv_done, 1)
            nc.vector.reduce_sum(logsum[:], logv[:], AX_X).then_inc(sum_done, 1)
            dve.wait_ge(loaded["scalars"], 16)
            dve.wait_ge(l_full, 1)
            nc.vector.tensor_scalar(learned[:], l_bank[:, 0:NT], W["scalars"][:, 0:1], -80.0, ALU.add, ALU.max
                                    ).then_inc(z_ready, 1)
            step(nc.vector.tensor_scalar(mean[:], l_bank[:, NT:NT + 1], 1.0 / TOK, 1e-6, ALU.mult, ALU.add))
            step(nc.vector.reciprocal(mean[:], mean[:]))
            step(nc.vector.tensor_scalar(logv[:], logv[:], mean[:, 0:1], 0.5, ALU.mult, ALU.mult))
            dve.wait_ge(z_exp, 1)
            step(nc.vector.tensor_scalar(learned[:], learned[:], 1.0, None, ALU.add))
            step(nc.vector.reciprocal(learned[:], learned[:]))
            step(nc.vector.scalar_tensor_tensor(out=gate[:], in0=learned[:], scalar=2.5, in1=logv[:],
                                                op0=ALU.mult, op1=ALU.add))
            step(nc.vector.tensor_scalar(gate[:], gate[:], 0.0, 5.0, ALU.max, ALU.min))
            step(nc.vector.tensor_scalar(gate[:], gate[:], TAU_LOW, 1.0 / (TAU_HIGH - TAU_LOW),
                                         ALU.subtract, ALU.mult))
            step(nc.vector.tensor_scalar(gate[:], gate[:], 0.0, 1.0, ALU.max, ALU.min))
            step(nc.vector.tensor_scalar(gate[:], gate[:], W["scalars"][:, 1:2], W["scalars"][:, 2:3],
                                         ALU.mult, ALU.add))
            nc.vector.tensor_scalar(gate[:], gate[:], -80.0, None, ALU.max).then_inc(z_ready, 1)
            dve.wait_ge(z_exp, 2)
            step(nc.vector.tensor_scalar(gate[:], gate[:], 1.0, None, ALU.add))
            step(nc.vector.reciprocal(gate[:], gate[:]))
            step(nc.vector.tensor_scalar(live[:], gate[:], EARLY_EXIT, None, ALU.is_ge))
            step(nc.vector.tensor_tensor(gate[:], gate[:], live[:], ALU.mult))
            dve.wait_ge(loaded["log_rel"], 16)

            def pick(t):
                n = t % 2
                dve.wait_ge(s_full, t + 1)
                if t >= 2:
                    dve.wait_ge(E_done, t - 1)
                nc.vector.scalar_tensor_tensor(out=R[:, n, :], in0=s_bank[n][:, 0:NSLOT],
                                               scalar=float(RDIM) ** -0.5, in1=W["log_rel"][:],
                                               op0=ALU.mult, op1=ALU.add).then_inc(s_out, 1)
                nc.vector.scalar_tensor_tensor(out=A[:, n, :], in0=s_bank[n][:, NSLOT:2 * NSLOT],
                                               scalar=-float(BOT) ** -0.5, in1=W["log_rel"][:],
                                               op0=ALU.mult, op1=ALU.subtract).then_inc(s_out, 1)
                dve.wait_ge(s_out, 2 * t + 2)
                step(nc.vector.max(best[:, n, :], R[:, n, :]))
                step(nc.vector.match_replace(out=R2[:, n, :], in_to_replace=best[:, n, :], in_values=R[:, n, :],
                                             imm_value=-HIDDEN))
                step(nc.vector.tensor_tensor(chosen[:, n, :], R[:, n, :], R2[:, n, :], ALU.not_equal))
                nc.vector.tensor_scalar(off[:, n, :], chosen[:, n, :], 1.0, -HIDDEN, ALU.subtract, ALU.mult)
                step(nc.vector.tensor_tensor(A[:, n, :], A[:, n, :], chosen[:, n, :], ALU.mult))
                step(nc.vector.tensor_tensor(A[:, n, :], A[:, n, :], off[:, n, :], ALU.add))
                nc.vector.tensor_reduce(least[:, t:t + 1], A[:, n, :], AX_X, ALU.min).then_inc(least_done, 1)
            pick(0)
            for t in range(NT):
                if t + 1 < NT:
                    pick(t + 1)
                dve.wait_ge(E_done, t + 1)
                step(nc.vector.reciprocal(factor[:, t:t + 1], total[:, t:t + 1]))
                step(nc.vector.tensor_tensor(factor[:, t:t + 1], factor[:, t:t + 1], gate[:, t:t + 1], ALU.mult))
                dve.wait_ge(out_full, t + 1)
                dve.wait_ge(doubled, t + 1)
                nc.vector.scalar_tensor_tensor(out=K.xs[:, t, :], in0=o_bank[t % 2][:], scalar=factor[:, t:t + 1],
                                               in1=K.xs[:, t, :], op0=ALU.mult, op1=ALU.add).then_inc(out_done, 1)


def pair_stage(nc, K, xf, pre):
    SCALE = float(SEQ) ** -0.5
    with ExitStack() as ctx:
        m = Memory(nc, ctx, pre)
        sb, sem = m.sb, m.sem
        prod = sb("prod", [P, 2, SEQ])
        G = sb("G", [P, NC_, NB, NB])
        top, total = sb("top", [P, NC_, NB]), sb("total", [P, NC_, NB])
        mixed, other = sb("mixed", [P, NC_, TOK]), sb("other", [P, 2, SEQ])
        bank = [m.ps(f"bank{n}") for n in range(4)]
        dots, chain, diff, expd, prob = sem("dots"), sem("chain"), sem("diff"), sem("expd"), sem("prob")
        other_done, mixed_done, turned, taken = (sem(n) for n in ("other", "mixed", "turned", "taken"))
        block = ctx.enter_context(nc.Block())

        @block.vector
        def _(dve):
            step = Chain(dve, chain)
            n = 0
            for c in range(NC_):
                for i, j in ((0, 0), (0, 1), (1, 1)):
                    if n >= 2:
                        dve.wait_ge(dots, n - 1)
                    nc.vector.tensor_tensor_reduce(
                        out=prod[:, n % 2, :], in0=xf[:, c, i * SEQ:(i + 1) * SEQ],
                        in1=xf[:, c, j * SEQ:(j + 1) * SEQ], scale=SCALE, scalar=0.0, op0=ALU.mult,
                        op1=ALU.add, accum_out=G[:, c, i, j:j + 1]).then_inc(dots, 1)
                    n += 1
            dve.wait_ge(dots, n)
            step(nc.vector.tensor_copy(G[:, :, 1, 0], G[:, :, 0, 1]))
            step(nc.vector.tensor_reduce(top[:], G[:], AX_X, ALU.max))
            nc.vector.tensor_tensor(G[:], G[:], top[:].unsqueeze(3).to_broadcast([P, NC_, NB, NB]), ALU.subtract
                                    ).then_inc(diff, 1)
            dve.wait_ge(expd, 1)
            step(nc.vector.reduce_sum(total[:], G[:], AX_X))
            step(nc.vector.reciprocal(total[:], total[:]))
            step(nc.vector.tensor_tensor(G[:], G[:], total[:].unsqueeze(3).to_broadcast([P, NC_, NB, NB]),
                                         ALU.mult))
            for b in range(NB):
                ins = nc.vector.tensor_scalar(G[:, :, b, b], G[:, :, b, b], 1.0, None, ALU.add)
            ins.then_inc(prob, 1)
            dve.wait_ge(prob, 1)
            for n in range(NB * NC_):
                b, c = divmod(n, NC_)
                s = slice(b * SEQ, (b + 1) * SEQ)
                dve.wait_ge(other_done, n + 1)
                nc.vector.scalar_tensor_tensor(out=mixed[:, c, s], in0=xf[:, c, s], scalar=G[:, c, b, b:b + 1],
                                               in1=other[:, n % 2, :], op0=ALU.mult, op1=ALU.add
                                               ).then_inc(mixed_done, 1)

        @block.scalar
        def _(act):
            act.wait_ge(diff, 1)
            nc.scalar.activation(G[:], G[:], ACT.Exp).then_inc(expd, 1)
            act.wait_ge(prob, 1)

            def other_part(n):
                b, c = divmod(n, NC_)
                if n >= 2:
                    act.wait_ge(mixed_done, n - 1)
                nc.scalar.activation(other[:, n % 2, :], xf[:, c, (1 - b) * SEQ:(2 - b) * SEQ], ACT.Copy,
                                     scale=G[:, c, b, 1 - b:2 - b]).then_inc(other_done, 1)
            for b in range(NB):
                for c in range(NC_):
                    other_part(b * NC_ + c)
            for t in range(NT):
                act.wait_ge(turned, t + 1)
                nc.scalar.activation(K.xs[:, t, :], bank[t % 4][:], ACT.Copy).then_inc(taken, 1)

        @block.tensor
        def _(pe):
            for t in range(NT):
                pe.wait_ge(mixed_done, NC_ * (t // TB + 1))
                if t >= 4:
                    pe.wait_ge(taken, t - 3)
                for c in range(NC_):
                    last = nc.tensor.transpose(bank[t % 4][:, c * P:(c + 1) * P], mixed[:, c, t * P:(t + 1) * P],
                                               K.ident[:])
                last.then_inc(turned, 1)


EXPERTS, RANK = 8, 16
SCALING = 32.0 / 16.0


def experts_stage(nc, K, dram, pre):
    ER = EXPERTS * RANK
    NA = ER + EXPERTS
    with ExitStack() as ctx:
        m = Memory(nc, ctx, pre)
        sb, sem = m.sb, m.sem
        shapes = {"wa": [P, NC_, NA], "wb": [P, NC_, D], "lb": [ER, D]}
        raw = {n: sb(f"{n}_raw", s) for n, s in shapes.items()}
        W = {n: [sb(f"{n}{h}", s, F32R) for h in "hl"] for n, s in shapes.items()}
        bias = sb("bias", [P, D])
        ranks = sb("ranks", [P, NT, EXPERTS, RANK])
        rT = [sb(f"rT{n}", [P, TOK], F32R) for n in "hl"]
        L, first, cand, best = (sb(n, [P, NT, EXPERTS]) for n in ("L", "first", "cand", "best"))
        weight, order = sb("weight", [P, NT, EXPERTS]), sb("order", [P, EXPERTS])
        top, m1, m2 = sb("top", [P, NT]), sb("m1", [P, NT]), sb("m2", [P, NT])
        a_bank = [m.ps(f"ranks{n}") for n in range(2)]
        t_bank = [m.ps(f"turned{n}") for n in range(2)]
        o_bank = [m.ps(f"out{n}") for n in range(4)]
        loaded = {n: sem(f"in_{n}") for n in (*shapes, "bias", "order")}
        split_step, split = sem("split_step"), sem("split")
        a_full, a_out, chain, ready, expd, weighted = (
            sem(n) for n in ("a_full", "a_out", "chain", "ready", "expd", "weighted"))
        turned, t_hi, t_lo, o_full, o_out, biased = (
            sem(n) for n in ("turned", "t_hi", "t_lo", "o_full", "o_out", "biased"))
        block = ctx.enter_context(nc.Block())
        x = [K.xh, K.xl]

        @block.sync
        def _(sp):
            for n in shapes:
                sp.dma_start(raw[n][:], dram[f"e_{n}"]).then_inc(loaded[n], 16)
            sp.dma_start(bias[:], dram["e_bias"]).then_inc(loaded["bias"], 16)
            sp.dma_start(order[:], dram["e_order"]).then_inc(loaded["order"], 16)

        @block.gpsimd
        def _(pool):
            step = Chain(pool, split_step)
            for n in shapes:
                pool.wait_ge(loaded[n], 16)
                hi, lo = W[n]
                step(nc.gpsimd.tensor_copy(hi[:], raw[n][:]))
                nc.gpsimd.tensor_tensor(lo[:], raw[n][:], hi[:].bitcast(F32), ALU.subtract).then_inc(split, 1)

        @block.tensor
        def _(pe):
            pe.wait_ge(split, 1)
            for t in range(NT):
                if t >= 2:
                    pe.wait_ge(a_out, t - 1)
                for c in range(NC_):
                    last = mm3(nc, a_bank[t % 2][:, 0:NA], [a[:, c, t * P:(t + 1) * P] for a in x],
                               [a[:, c, :] for a in W["wa"]], c == 0, c == NC_ - 1)
                last.then_inc(a_full, 1)

            def base(t):
                if t >= 4:
                    pe.wait_ge(o_out, t - 3)
                for c in range(NC_):
                    mm3(nc, o_bank[t % 4][:], [a[:, c, t * P:(t + 1) * P] for a in x],
                        [a[:, c, :] for a in W["wb"]], c == 0, False)
            pe.wait_ge(split, 2)
            for t in range(4):
                base(t)
            pe.wait_ge(weighted, 1)
            for b in range(NB):
                for i in range(TB):
                    t = b * TB + i
                    last = nc.tensor.transpose(t_bank[b][:, i * P:(i + 1) * P],
                                               ranks[:, t].rearrange("p e r -> p (e r)"), K.ident[:])
                last.then_inc(turned, 1)
            pe.wait_ge(split, 3)
            for t in range(NT):
                if t >= 4:
                    base(t)
                if t % TB == 0:
                    pe.wait_ge(t_lo, t // TB + 1)
                mm3(nc, o_bank[t % 4][:], [a[:, t * P:(t + 1) * P] for a in rT], [a[:] for a in W["lb"]],
                    False, True).then_inc(o_full, 1)

        @block.scalar
        def _(act):
            for t in range(NT):
                act.wait_ge(a_full, t + 1)
                nc.scalar.activation(ranks[:, t].rearrange("p e r -> p (e r)"), a_bank[t % 2][:, 0:ER], ACT.Copy)
                nc.scalar.activation(L[:, t, :], a_bank[t % 2][:, ER:NA], ACT.Copy).then_inc(a_out, 1)
            act.wait_ge(ready, 1)
            nc.scalar.activation(L[:], L[:], ACT.Exp).then_inc(expd, 1)
            for b in range(NB):
                act.wait_ge(turned, b + 1)
                nc.scalar.activation(rT[0][:, b * SEQ:(b + 1) * SEQ], t_bank[b][:], ACT.Copy).then_inc(t_hi, 1)

        @block.vector
        def _(dve):
            step = Chain(dve, chain)
            wide = [P, NT, EXPERTS]

            def over(t):
                return t[:].unsqueeze(2).to_broadcast(wide)
            dve.wait_ge(loaded["order"], 16)
            dve.wait_ge(a_out, NT)
            step(nc.vector.tensor_reduce(top[:], L[:], AX_X, ALU.max))
            nc.vector.tensor_tensor(L[:], L[:], over(top), ALU.subtract).then_inc(ready, 1)
            dve.wait_ge(expd, 1)
            step(nc.vector.reduce_sum(top[:], L[:], AX_X))
            step(nc.vector.reciprocal(top[:], top[:]))
            step(nc.vector.tensor_tensor(L[:], L[:], over(top), ALU.mult))

            def first_best(value, mark):
                step(nc.vector.tensor_reduce(value[:], L[:], AX_X, ALU.max))
                step(nc.vector.tensor_tensor(cand[:], L[:], over(value), ALU.is_equal))
                step(nc.vector.tensor_tensor(cand[:], cand[:], order[:].unsqueeze(1).to_broadcast(wide), ALU.mult))
                step(nc.vector.tensor_reduce(top[:], cand[:], AX_X, ALU.max))
                step(nc.vector.tensor_tensor(mark[:], cand[:], over(top), ALU.is_equal))
            first_best(m1, first)
            step(nc.vector.scalar_tensor_tensor(out=L[:].rearrange("p t e -> p (t e)"),
                                                in0=first[:].rearrange("p t e -> p (t e)"), scalar=-2.0,
                                                in1=L[:].rearrange("p t e -> p (t e)"),
                                                op0=ALU.mult, op1=ALU.add))
            first_best(m2, best)
            step(nc.vector.tensor_tensor(first[:], first[:], over(m1), ALU.mult))
            step(nc.vector.tensor_tensor(best[:], best[:], over(m2), ALU.mult))
            step(nc.vector.tensor_tensor(weight[:], first[:], best[:], ALU.add))
            step(nc.vector.tensor_tensor(m1[:], m1[:], m2[:], ALU.add))
            step(nc.vector.reciprocal(m1[:], m1[:]))
            step(nc.vector.tensor_scalar(m1[:], m1[:], SCALING, None, ALU.mult))
            step(nc.vector.tensor_tensor(weight[:], weight[:], over(m1), ALU.mult))
            flat = ranks[:].rearrange("p t e r -> p (t e) r")
            nc.vector.tensor_tensor(flat, flat, weight[:].rearrange("p t e -> p (t e)").unsqueeze(2)
                                    .to_broadcast([P, NT * EXPERTS, RANK]), ALU.mult).then_inc(weighted, 1)
            dve.wait_ge(loaded["bias"], 16)
            for t in range(NT):
                nc.vector.tensor_tensor(K.xs[:, t, :], K.xs[:, t, :], bias[:], ALU.add).then_inc(biased, 1)
            for b in range(NB):
                dve.wait_ge(t_hi, b + 1)
                s = slice(b * SEQ, (b + 1) * SEQ)
                nc.vector.tensor_tensor(rT[1][:, s], t_bank[b][:], rT[0][:, s].bitcast(F32), ALU.subtract
                                        ).then_inc(t_lo, 1)
            for t in range(NT):
                dve.wait_ge(o_full, t + 1)
                dve.wait_ge(biased, t + 1)
                nc.vector.tensor_tensor(K.xs[:, t, :], K.xs[:, t, :], o_bank[t % 4][:], ALU.add).then_inc(o_out, 1)


class Kept:

    def __init__(self, nc, ctx):
        m = Memory(nc, ctx, "kept")
        self.stored = m.sem("stored")
        self.xs = m.sb("x", [P, NT, D])
        self.xh = m.sb("x_hi", [P, NC_, TOK], F32R)
        self.xl = m.sb("x_lo", [P, NC_, TOK], F32R)
        self.ident = m.sb("ident", [P, P])
        self.ident_r, self.mask_r = m.sb("ident_r", [P, P], F32R), m.sb("mask_r", [P, P], F32R)
        self.half, self.zero = m.sb("minus_half", [P, NT]), m.sb("zero", [P, 1])


def program(nc, dram, out, stages=STAGES):
    with ExitStack() as ctx:
        K = Kept(nc, ctx)
        x0 = dram["x"].rearrange("b t d -> (b t) d")
        setup_stage(nc, K, {"x": x0}, "setup")
        norm_stage(nc, K, "turn0", normalize=False)
        for n, stage in enumerate(stages):
            if stage == "attn3":
                with ExitStack() as own:
                    xf = Memory(nc, own, "pair").sb("x_turned", [P, NC_, TOK])
                    norm_stage(nc, K, f"turn{n + 1}", normalize=False, full=xf)
                    pair_stage(nc, K, xf, "a3")
            else:
                STAGE[stage](nc, K, dram)
            end = n == len(stages) - 1
            norm_stage(nc, K, f"norm{n}", out=out.rearrange("b t d -> (b t) d") if end else None)


STAGE = {
    "ffn2": lambda nc, K, d: slots_stage(nc, K, d, "f2"),
    "ffn3": lambda nc, K, d: experts_stage(nc, K, d, "f3"),
    "ffn1": lambda nc, K, d: streams_stage(nc, K, d, "f1"),
    "attn0": lambda nc, K, d: rotary_attention_stage(nc, K, d, "a0"),
    "ffn0": lambda nc, K, d: gated_ffn_stage(nc, K, d, "f0"),
    "attn1": lambda nc, K, d: attention_stage(nc, K, {"w": d["w1"]}, 1, "a1"),
    "attn2": lambda nc, K, d: attention_stage(nc, K, {"w": d["w2"], "qkw": d["qkw"], "pick": d["pick"],
                                                      "tab": d["tab"]}, 2, "a2"),
}


def layout(inputs):
    import numpy as np
    a = {n: np.asarray(v) for n, v in inputs.items()}
    f = np.float32

    def group_weights(wq, wk, wv, wo):
        q = wq.reshape(NC_, P, KV, GROUP, P).transpose(2, 3, 1, 0, 4).reshape(KV, GROUP, P, 512)
        k = wk.reshape(NC_, P, KV, P).transpose(2, 1, 0, 3).reshape(KV, 1, P, 512)
        v = wv.reshape(NC_, P, KV, P).transpose(2, 1, 0, 3).reshape(KV, 1, P, 512)
        o = wo.reshape(KV, GROUP, P, D)
        return np.concatenate([q, k, v, o], axis=1).reshape(KV * PIECES, P, 512)

    out = {"x": a["L0_attn_x"]}
    wq = a["L0_attn_Wq"].reshape(NC_, P, KV, GROUP * HD0)
    wk, wv = (a[n].reshape(NC_, P, KV, HD0) for n in ("L0_attn_Wk", "L0_attn_Wv"))
    out["w0"] = np.concatenate([wq, wk, wv], axis=3).transpose(1, 0, 2, 3).reshape(P, -1)
    wo = a["L0_attn_Wo"].reshape(KV, GROUP, 1, HD0, D)
    out["wo0"] = np.concatenate([wo, wo], axis=2).reshape(KV, P, D).transpose(1, 0, 2)
    inv_freq = f(1.0) / f(500000.0) ** (np.arange(0, HD0, 2, dtype=f) / f(HD0))
    angle = np.arange(SEQ, dtype=f)[:, None] * inv_freq.astype(f)[None, :]
    cos, sin = np.cos(angle).astype(f), np.sin(angle).astype(f)
    out["cos"] = np.concatenate([cos, cos], axis=1).reshape(TB, P, HD0).transpose(1, 0, 2)
    out["sin"] = np.concatenate([-sin, sin], axis=1).reshape(TB, P, HD0).transpose(1, 0, 2)
    pad = NF * P - FF

    def hidden_rows(w):
        return np.pad(w, ((0, pad), (0, 0)))
    gu = [hidden_rows(a[n]).reshape(NF, P, NC_, P).transpose(0, 3, 2, 1)
          for n in ("L0_ffn_gate_w", "L0_ffn_up_w")]
    out["gu"] = np.stack(gu, axis=2).reshape(NF, P, 2 * NC_ * P)
    out["gu_scale"] = np.stack([hidden_rows(a[n]).reshape(NF, P).T for n in ("L0_ffn_gate_s", "L0_ffn_up_s")],
                               axis=2)
    out["down"] = hidden_rows(a["L0_ffn_down_w"].T).reshape(NF, P, D)
    out["down_scale"] = np.broadcast_to(a["L0_ffn_down_s"].reshape(1, D), (P, D))
    w = a["L1_attn_w_qkv"].T
    n, kv = HEADS * P, KV * P
    out["w1"] = group_weights(w[:, :n], w[:, n:n + kv], w[:, n + kv:], a["L1_attn_w_dense"].T)
    ws = np.concatenate([a["L1_ffn_W_res"], a["L1_ffn_W_pre"], a["L1_ffn_W_post"]], axis=0)
    out["s_w"] = ws.T.reshape(NC_, P, -1).transpose(1, 0, 2)
    out["s_wb"] = a["L1_ffn_W_branch"]
    b = np.concatenate([a["L1_ffn_H_res_base"].reshape(-1), a["L1_ffn_H_pre_base"], a["L1_ffn_H_post_base"]])
    out["s_base"] = np.broadcast_to(b, (P, b.size))
    out["s_gate"] = np.broadcast_to(a["L1_ffn_gate"], (P, 1))
    out["w2"] = group_weights(a["L2_attn_Wq"].T, a["L2_attn_Wk"].T, a["L2_attn_Wv"].T, a["L2_attn_Wo"].T)
    out["qkw"] = np.stack([a["L2_attn_q_norm_w"], a["L2_attn_k_norm_w"]], axis=1)
    def chunks(w):
        return w.reshape(NC_, P, -1).transpose(1, 0, 2)
    s = {n: a[f"L2_ffn_{n}"] for n in ("Wq", "Wr", "aux_keys", "aux_values", "Wvd", "Wvu", "Wu1", "bu1", "Wu2",
                                       "bu2", "gate_w1", "gate_bias", "log_rel")}
    out.update(u_wq=chunks(s["Wq"].T), u_wr=s["Wr"], u_wrT=s["Wr"].T, u_keysT=s["aux_keys"].T,
               u_valuesT=chunks(s["aux_values"].T), u_wvdT=chunks(s["Wvd"].T), u_wvuT=s["Wvu"].T,
               u_wu1=chunks(s["Wu1"].T), u_wu2=s["Wu2"].T, u_bu1=s["bu1"].reshape(P, 1),
               u_scalars=np.broadcast_to(np.stack([s["bu2"].reshape(()), s["gate_w1"], s["gate_bias"]]), (P, 3)),
               u_log_rel=np.broadcast_to(s["log_rel"], (P, NSLOT)))
    out["e_wa"] = chunks(np.concatenate([a["L3_ffn_lora_A"].reshape(-1, D), a["L3_ffn_W_router"]]).T)
    out["e_wb"] = chunks(a["L3_ffn_W_base"].T)
    out["e_lb"] = a["L3_ffn_lora_B"].transpose(0, 2, 1).reshape(-1, D)
    out["e_bias"] = np.broadcast_to(a["L3_ffn_b_base"], (P, D))
    out["e_order"] = np.broadcast_to(np.arange(EXPERTS, 0, -1).astype(f), (P, EXPERTS))
    import math
    start = 2 ** (-2 ** (-(math.log2(HEADS) - 3)))
    slopes = np.array([start * start ** i for i in range(HEADS)], dtype=f)
    t = -(slopes[:, None] * (np.arange(SEQ, dtype=f) - f(SEQ - P // 2)))

    def top(t):
        return (t.view(np.uint32) & np.uint32(0xFFFF0000)).view(f)
    hi = top(t)
    mid = top(t - hi)
    out["tab"] = np.stack([hi, mid, t - hi - mid], axis=1).reshape(KV, 3 * GROUP, SEQ)
    pick = np.zeros((3 * GROUP, GROUP, P), f)
    for j in range(GROUP):
        pick[3 * j:3 * j + 3, j, :] = 1.0
    out["pick"] = pick
    used = NEEDS["x"].union(*(NEEDS[s] for s in STAGES))
    return {n: np.ascontiguousarray(v) for n, v in out.items() if n in used}


NEEDS = {"x": {"x"}, "attn3": set(), "ffn3": {"e_wa", "e_wb", "e_lb", "e_bias", "e_order"},
         "ffn2": {"u_wq", "u_wr", "u_wrT", "u_keysT", "u_valuesT", "u_wvdT", "u_wvuT", "u_wu1", "u_wu2", "u_bu1",
                  "u_scalars", "u_log_rel"},
         "ffn1": {"s_w", "s_wb", "s_base", "s_gate"}, "attn0": {"w0", "wo0", "cos", "sin"}, "ffn0": {"gu", "gu_scale", "down", "down_scale"}, "attn1": {"w1"}, "attn2": {"w2", "qkw", "pick", "tab"}}


def kernel(**inputs):
    import concourse.bacc as _bacc
    from concourse import mybir as _mybir
    from concourse.bass_utils import run_bass_kernel_spmd as _run

    nc = _bacc.Bacc("TRN2", target_bir_lowering=False, num_devices=1)
    arrays, dram = {}, {}
    for name, a in layout(inputs).items():
        arrays[f"in_{name}"] = a
        dram[name] = nc.dram_tensor(f"in_{name}", a.shape, _mybir.dt.from_np(a.dtype), kind="ExternalInput").ap()
    out = nc.dram_tensor("out", (NB, SEQ, D), F32, kind="ExternalOutput").ap()
    program(nc, dram, out)
    r = _run(nc, [arrays], core_ids=[0])
    return r.results[0]["out"]
```
